# Optimizing a Trainium2 kernel written in Bass

```python
import numpy as np
import jax
import jax.numpy as jnp

def _softmax(x, axis=-1):
    return jax.nn.softmax(x, axis=axis)

def _gelu(x):
    return jax.nn.gelu(x, approximate=True)

def _silu(x):
    return jax.nn.silu(x)

def _sigmoid(x):
    return jax.nn.sigmoid(x)

def _layernorm(x, axis=-1, eps=1e-05):
    m = jnp.mean(x, axis=axis, keepdims=True)
    v = jnp.var(x, axis=axis, keepdims=True)
    return (x - m) / jnp.sqrt(v + eps)

def _scatter_add(tgt, idx, src, axis=0):
    return tgt.at[idx].add(src)

def _segment_sum(src, seg, n):
    return jax.ops.segment_sum(src, seg, n)
kernel_name = 'mk_xattn_ffn_d2_seqx_r4_6e1f30'

def setup_inputs(seed: int=0):
    np.random.seed(seed)
    _w = jnp.asarray

    def _rec_inputs():
        import jax
        import jax.numpy as jnp
        _rk = jax.random.key(seed)
        x = -0.0002928 + 1 * jax.random.normal(jax.random.fold_in(_rk, 1), (16, 128, 256), jnp.float32)
        _lenS = 128 - jax.random.randint(jax.random.fold_in(_rk, 7), (16,), 0, max(1, 128 // 4) + 1, jnp.int32)
        _lenS2 = 128 - jax.random.randint(jax.random.fold_in(_rk, 8), (16,), 0, max(1, 128 // 4) + 1, jnp.int32)
        _ctx_1024P = jax.random.normal(jax.random.fold_in(_rk, 11), (16, 16, 256), jnp.float32)
        _ctx_1024c = jax.random.dirichlet(jax.random.fold_in(_rk, 511), 0.3 * jnp.ones((16,), jnp.float32), (16, 128))
        _ctx_1024t = jnp.einsum('bsk,bkd->bsd', _ctx_1024c, _ctx_1024P)
        _ctx_1024t = _ctx_1024t * jax.lax.rsqrt(jnp.mean(jnp.square(_ctx_1024t)) + 1e-12) * 0.953939
        ctx_1024 = -1.39393e-06 + 0.999914 * (_ctx_1024t + 0.3 * jax.random.normal(jax.random.fold_in(_rk, 611), (16, 128, 256), jnp.float32))
        return (x, ctx_1024)
    x, ctx_1024 = _rec_inputs()

    def _L0_xattn_setup():
        import jax, jax.numpy as jnp
        import numpy as np
        EMB = 256
        NH = 8
        HD = EMB // NH
        EPS = 1e-06

        def _mlstm_head(q, k, v, ig, fg):
            S, DH = q.shape
            log_fg = jax.nn.log_sigmoid(fg)
            cs = jnp.concatenate([jnp.zeros((1, 1), q.dtype), jnp.cumsum(log_fg, axis=0)], axis=0)
            fg_mat_full = cs - cs.T
            ltr = jnp.tril(jnp.ones((S, S), bool))
            log_fg_matrix = jnp.where(ltr, fg_mat_full[1:, 1:], -jnp.inf)
            log_D = log_fg_matrix + ig.T
            max_log_D = jnp.max(log_D, axis=-1, keepdims=True)
            D = jnp.exp(log_D - max_log_D)
            qk = q @ (k.T / jnp.sqrt(jnp.asarray(DH, q.dtype)))
            C = qk * D
            normalizer = jnp.maximum(jnp.abs(C.sum(-1, keepdims=True)), jnp.exp(-max_log_D))
            return C / (normalizer + EPS) @ v
        key = jax.random.key(seed)
        ks = jax.random.split(key, 6)
        B, S = (2, 512)
        q = jax.random.normal(ks[0], (B, S, EMB), jnp.float32)
        k = jax.random.normal(ks[1], (B, S, EMB), jnp.float32)
        v = jax.random.normal(ks[2], (B, S, EMB), jnp.float32)
        igate_kernel = jax.random.normal(ks[3], (3 * EMB, NH), jnp.float32) * 0.02
        igate_bias = jax.random.normal(ks[4], (NH,), jnp.float32) * 0.1
        fgate_kernel = jax.random.normal(ks[5], (3 * EMB, NH), jnp.float32) * 0.02
        fgate_bias = jnp.linspace(3.0, 6.0, NH).astype(jnp.float32)
        return dict(q=q, k=k, v=v, igate_kernel=igate_kernel, igate_bias=igate_bias, fgate_kernel=fgate_kernel, fgate_bias=fgate_bias)
    _L0_xattn_all = _L0_xattn_setup()
    _L0_xattn_in = {k: v for k, v in _L0_xattn_all.items() if k in ('igate_kernel', 'igate_bias', 'fgate_kernel', 'fgate_bias')}
    del _L0_xattn_all

    def _L0_ffn_setup():
        import jax, jax.numpy as jnp
        import numpy as np
        D_MODEL = 256
        FF = 1024
        E = 8
        TOP_K = 2
        CAP_FACTOR = 1.25
        B, T = (4, 512)

        def _moe_forward(x, gate_w, gate_b, w1, b1, w2, b2):
            Bb, Tt, d = x.shape
            S = Bb * Tt
            C = int(CAP_FACTOR * S / E)
            xf = x.reshape(S, d)
            logits = xf @ gate_w + gate_b
            probs = jax.nn.softmax(logits, axis=1)
            topk_p, topk_i = jax.lax.top_k(probs, TOP_K)
            topk_pn = topk_p / jnp.sum(topk_p, axis=1, keepdims=True)
            rows = jnp.arange(S)
            w_te = jnp.zeros((S, E), xf.dtype).at[rows[:, None], topk_i].set(topk_pn)
            mask = jnp.zeros((S, E), bool).at[rows[:, None], topk_i].set(True)
            rank = jnp.cumsum(mask.astype(jnp.int32), axis=0)
            slot = jnp.where(mask & (rank <= C), rank - 1, C)
            e_grid = jnp.broadcast_to(jnp.arange(E), (S, E))
            t_grid = jnp.broadcast_to(rows[:, None], (S, E))
            buf = jnp.full((E, C + 1), S, jnp.int32).at[e_grid, slot].set(t_grid)
            idx = buf[:, :C]
            valid = idx < S
            x_pad = jnp.concatenate([xf, jnp.zeros((1, d), xf.dtype)], axis=0)
            xin = x_pad[idx]
            h = jax.nn.relu(jnp.einsum('ecd,edh->ech', xin, w1) + b1[:, None, :])
            out = jnp.einsum('ech,ehd->ecd', h, w2) + b2[:, None, :]
            w_pad = jnp.concatenate([w_te, jnp.zeros((1, E), xf.dtype)], axis=0)
            tok_w = w_pad[idx, jnp.arange(E)[:, None]]
            out = out * jnp.where(valid, tok_w, 0.0)[:, :, None]
            final = jnp.zeros((S + 1, d), xf.dtype).at[idx.reshape(-1)].add(out.reshape(-1, d))[:S]
            return final.reshape(Bb, Tt, d)
        key = jax.random.key(seed)
        ks = jax.random.split(key, 7)
        s = 0.02
        return {'x': jax.random.normal(ks[0], (B, T, D_MODEL), jnp.float32), 'gate_w': jax.random.normal(ks[1], (D_MODEL, E), jnp.float32) * s, 'gate_b': jnp.zeros((E,), jnp.float32), 'w1': jax.random.normal(ks[2], (E, D_MODEL, FF), jnp.float32) * s, 'b1': jnp.zeros((E, FF), jnp.float32), 'w2': jax.random.normal(ks[3], (E, FF, D_MODEL), jnp.float32) * s, 'b2': jnp.zeros((E, D_MODEL), jnp.float32)}
    _L0_ffn_all = _L0_ffn_setup()
    _L0_ffn_in = {k: v for k, v in _L0_ffn_all.items() if k in ('gate_w', 'gate_b', 'w1', 'b1', 'w2', 'b2')}
    del _L0_ffn_all

    def _L1_xattn_setup():
        import jax, jax.numpy as jnp
        import numpy as np
        HIDDEN = 256
        ATTN = 256
        B, S = (4, 512)
        key = jax.random.key(seed)
        ks = jax.random.split(key, 6)
        bound = 1.0 / np.sqrt(HIDDEN)
        return {'query': jax.random.normal(ks[0], (B, S, HIDDEN), jnp.float32), 'value': jax.random.normal(ks[1], (B, S, HIDDEN), jnp.float32), 'Wq': jax.random.uniform(ks[2], (HIDDEN, ATTN), jnp.float32, -bound, bound), 'bq': jax.random.uniform(ks[3], (ATTN,), jnp.float32, -bound, bound), 'Wv': jax.random.uniform(ks[4], (HIDDEN, ATTN), jnp.float32, -bound, bound), 'bv': jax.random.uniform(ks[5], (ATTN,), jnp.float32, -bound, bound)}
    _L1_xattn_all = _L1_xattn_setup()
    _L1_xattn_in = {k: v for k, v in _L1_xattn_all.items() if k in ('Wq', 'bq', 'Wv', 'bv')}
    del _L1_xattn_all

    def _L1_ffn_setup():
        import jax, jax.numpy as jnp
        import numpy as np
        GROUP = 16
        EPS = 1e-05

        def _dequant(q, scale):
            w = q.astype(jnp.float32) / 7.5 - 1.0
            return w * jnp.repeat(scale, GROUP, axis=1)

        def _qlora_linear(x, q, scale, bias, la, lb):
            w = _dequant(q, scale)
            base = jnp.einsum('btd,od->bto', x, w) + bias
            lora = jnp.einsum('btr,or->bto', jnp.einsum('btd,rd->btr', x, la), lb)
            return base + lora

        def _layernorm(x, g, b):
            mu = jnp.mean(x, axis=-1, keepdims=True)
            var = jnp.mean(jnp.square(x - mu), axis=-1, keepdims=True)
            return (x - mu) * jax.lax.rsqrt(var + EPS) * g + b
        key = jax.random.key(seed)
        ks = jax.random.split(key, 6)
        D, R, B, T = (256, 32, 8, 1024)
        x = jax.random.normal(ks[0], (B, T, D), dtype=jnp.float32)
        qweights = jax.random.randint(ks[1], (6, D, D), 0, 16, dtype=jnp.int32)
        scales = jax.random.uniform(ks[2], (6, D, D // GROUP), dtype=jnp.float32)
        biases = jax.random.normal(ks[3], (6, D), dtype=jnp.float32) * 0.02
        lora_a = jax.random.normal(ks[4], (6, R, D), dtype=jnp.float32) * 0.02
        lora_b = jax.random.normal(ks[5], (6, D, R), dtype=jnp.float32) * 0.02
        ln_gamma = jnp.ones((3, D), dtype=jnp.float32)
        ln_beta = jnp.zeros((3, D), dtype=jnp.float32)
        return {'x': x, 'qweights': qweights, 'scales': scales, 'biases': biases, 'lora_a': lora_a, 'lora_b': lora_b, 'ln_gamma': ln_gamma, 'ln_beta': ln_beta}
    _L1_ffn_all = _L1_ffn_setup()
    _L1_ffn_in = {k: v for k, v in _L1_ffn_all.items() if k in ('qweights', 'scales', 'biases', 'lora_a', 'lora_b', 'ln_gamma', 'ln_beta')}
    del _L1_ffn_all
    return {'x': x, 'ctx_1024': ctx_1024, 'L0_xattn_igate_kernel': _L0_xattn_in['igate_kernel'], 'L0_xattn_igate_bias': _L0_xattn_in['igate_bias'], 'L0_xattn_fgate_kernel': _L0_xattn_in['fgate_kernel'], 'L0_xattn_fgate_bias': _L0_xattn_in['fgate_bias'], 'L0_ffn_gate_w': _L0_ffn_in['gate_w'], 'L0_ffn_gate_b': _L0_ffn_in['gate_b'], 'L0_ffn_w1': _L0_ffn_in['w1'], 'L0_ffn_b1': _L0_ffn_in['b1'], 'L0_ffn_w2': _L0_ffn_in['w2'], 'L0_ffn_b2': _L0_ffn_in['b2'], 'L1_xattn_Wq': _L1_xattn_in['Wq'], 'L1_xattn_bq': _L1_xattn_in['bq'], 'L1_xattn_Wv': _L1_xattn_in['Wv'], 'L1_xattn_bv': _L1_xattn_in['bv'], 'L1_ffn_qweights': _L1_ffn_in['qweights'], 'L1_ffn_scales': _L1_ffn_in['scales'], 'L1_ffn_biases': _L1_ffn_in['biases'], 'L1_ffn_lora_a': _L1_ffn_in['lora_a'], 'L1_ffn_lora_b': _L1_ffn_in['lora_b'], 'L1_ffn_ln_gamma': _L1_ffn_in['ln_gamma'], 'L1_ffn_ln_beta': _L1_ffn_in['ln_beta']}

def reference(x, ctx_1024, L0_xattn_igate_kernel, L0_xattn_igate_bias, L0_xattn_fgate_kernel, L0_xattn_fgate_bias, L0_ffn_gate_w, L0_ffn_gate_b, L0_ffn_w1, L0_ffn_b1, L0_ffn_w2, L0_ffn_b2, L1_xattn_Wq, L1_xattn_bq, L1_xattn_Wv, L1_xattn_bv, L1_ffn_qweights, L1_ffn_scales, L1_ffn_biases, L1_ffn_lora_a, L1_ffn_lora_b, L1_ffn_ln_gamma, L1_ffn_ln_beta):
    import jax
    import jax.numpy as jnp

    def _L0_xattn_ref(q, k, v, igate_kernel, igate_bias, fgate_kernel, fgate_bias):
        import jax, jax.numpy as jnp
        import numpy as np
        EMB = 256
        NH = 8
        HD = EMB // NH
        EPS = 1e-06

        def _mlstm_head(q, k, v, ig, fg):
            S, DH = q.shape
            log_fg = jax.nn.log_sigmoid(fg)
            cs = jnp.concatenate([jnp.zeros((1, 1), q.dtype), jnp.cumsum(log_fg, axis=0)], axis=0)
            fg_mat_full = cs - cs.T
            ltr = jnp.tril(jnp.ones((S, S), bool))
            log_fg_matrix = jnp.where(ltr, fg_mat_full[1:, 1:], -jnp.inf)
            log_D = log_fg_matrix + ig.T
            max_log_D = jnp.max(log_D, axis=-1, keepdims=True)
            D = jnp.exp(log_D - max_log_D)
            qk = q @ (k.T / jnp.sqrt(jnp.asarray(DH, q.dtype)))
            C = qk * D
            normalizer = jnp.maximum(jnp.abs(C.sum(-1, keepdims=True)), jnp.exp(-max_log_D))
            return C / (normalizer + EPS) @ v
        B, S, H = q.shape
        x = jnp.concatenate([q, k, v], axis=-1)
        ig = x @ igate_kernel + igate_bias
        fg = x @ fgate_kernel + fgate_bias
        qh = q.reshape(B, S, NH, HD).swapaxes(1, 2)
        kh = k.reshape(B, S, NH, HD).swapaxes(1, 2)
        vh = v.reshape(B, S, NH, HD).swapaxes(1, 2)
        igp = ig.swapaxes(1, 2)[..., None]
        fgp = fg.swapaxes(1, 2)[..., None]
        h = jax.vmap(jax.vmap(_mlstm_head))(qh, kh, vh, igp, fgp)
        hf = h.astype(jnp.float32)
        h = (hf * jax.lax.rsqrt(jnp.mean(jnp.square(hf), axis=-1, keepdims=True) + 1e-06)).astype(h.dtype)
        return h.swapaxes(1, 2).reshape(B, S, H)

    def _L0_ffn_ref(x, gate_w, gate_b, w1, b1, w2, b2):
        import jax, jax.numpy as jnp
        import numpy as np
        D_MODEL = 256
        FF = 1024
        E = 8
        TOP_K = 2
        CAP_FACTOR = 1.25
        B, T = (4, 512)

        def _moe_forward(x, gate_w, gate_b, w1, b1, w2, b2):
            Bb, Tt, d = x.shape
            S = Bb * Tt
            C = int(CAP_FACTOR * S / E)
            xf = x.reshape(S, d)
            logits = xf @ gate_w + gate_b
            probs = jax.nn.softmax(logits, axis=1)
            topk_p, topk_i = jax.lax.top_k(probs, TOP_K)
            topk_pn = topk_p / jnp.sum(topk_p, axis=1, keepdims=True)
            rows = jnp.arange(S)
            w_te = jnp.zeros((S, E), xf.dtype).at[rows[:, None], topk_i].set(topk_pn)
            mask = jnp.zeros((S, E), bool).at[rows[:, None], topk_i].set(True)
            rank = jnp.cumsum(mask.astype(jnp.int32), axis=0)
            slot = jnp.where(mask & (rank <= C), rank - 1, C)
            e_grid = jnp.broadcast_to(jnp.arange(E), (S, E))
            t_grid = jnp.broadcast_to(rows[:, None], (S, E))
            buf = jnp.full((E, C + 1), S, jnp.int32).at[e_grid, slot].set(t_grid)
            idx = buf[:, :C]
            valid = idx < S
            x_pad = jnp.concatenate([xf, jnp.zeros((1, d), xf.dtype)], axis=0)
            xin = x_pad[idx]
            h = jax.nn.relu(jnp.einsum('ecd,edh->ech', xin, w1) + b1[:, None, :])
            out = jnp.einsum('ech,ehd->ecd', h, w2) + b2[:, None, :]
            w_pad = jnp.concatenate([w_te, jnp.zeros((1, E), xf.dtype)], axis=0)
            tok_w = w_pad[idx, jnp.arange(E)[:, None]]
            out = out * jnp.where(valid, tok_w, 0.0)[:, :, None]
            final = jnp.zeros((S + 1, d), xf.dtype).at[idx.reshape(-1)].add(out.reshape(-1, d))[:S]
            return final.reshape(Bb, Tt, d)
        return _moe_forward(x, gate_w, gate_b, w1, b1, w2, b2)

    def _L1_xattn_ref(query, value, Wq, bq, Wv, bv):
        import jax, jax.numpy as jnp
        import numpy as np
        HIDDEN = 256
        ATTN = 256
        B, S = (4, 512)
        q = jnp.einsum('bsh,hd->bsd', query, Wq) + bq
        v = jnp.einsum('bsh,hd->bsd', value, Wv) + bv
        scores = jnp.einsum('bqd,bkd->bqk', q, v)
        attn = jax.nn.softmax(scores, axis=-1)
        context = jnp.einsum('bqk,bkd->bqd', attn, v)
        return context

    def _L1_ffn_ref(x, qweights, scales, biases, lora_a, lora_b, ln_gamma, ln_beta):
        import jax, jax.numpy as jnp
        import numpy as np
        GROUP = 16
        EPS = 1e-05

        def _dequant(q, scale):
            w = q.astype(jnp.float32) / 7.5 - 1.0
            return w * jnp.repeat(scale, GROUP, axis=1)

        def _qlora_linear(x, q, scale, bias, la, lb):
            w = _dequant(q, scale)
            base = jnp.einsum('btd,od->bto', x, w) + bias
            lora = jnp.einsum('btr,or->bto', jnp.einsum('btd,rd->btr', x, la), lb)
            return base + lora

        def _layernorm(x, g, b):
            mu = jnp.mean(x, axis=-1, keepdims=True)
            var = jnp.mean(jnp.square(x - mu), axis=-1, keepdims=True)
            return (x - mu) * jax.lax.rsqrt(var + EPS) * g + b
        h = x
        for blk in range(3):
            i0, i1 = (2 * blk, 2 * blk + 1)
            y = _qlora_linear(h, qweights[i0], scales[i0], biases[i0], lora_a[i0], lora_b[i0])
            y = _layernorm(y, ln_gamma[blk], ln_beta[blk])
            y = jax.nn.gelu(y, approximate=False)
            y = _qlora_linear(y, qweights[i1], scales[i1], biases[i1], lora_a[i1], lora_b[i1])
            h = y + h
        return h
    x = x + _L0_xattn_ref(_layernorm(x, axis=-1), ctx_1024, ctx_1024, L0_xattn_igate_kernel, L0_xattn_igate_bias, L0_xattn_fgate_kernel, L0_xattn_fgate_bias)
    x = x + _L0_ffn_ref(_layernorm(x, axis=-1), L0_ffn_gate_w, L0_ffn_gate_b, L0_ffn_w1, L0_ffn_b1, L0_ffn_w2, L0_ffn_b2)
    x = x + _L1_xattn_ref(_layernorm(x, axis=-1), ctx_1024, L1_xattn_Wq, L1_xattn_bq, L1_xattn_Wv, L1_xattn_bv)
    x = x + _L1_ffn_ref(_layernorm(x, axis=-1), L1_ffn_qweights, L1_ffn_scales, L1_ffn_biases, L1_ffn_lora_a, L1_ffn_lora_b, L1_ffn_ln_gamma, L1_ffn_ln_beta)
    return x

_drawn_inputs = setup_inputs


def setup_inputs(seed=0):
    import zlib

    import numpy as np

    out = dict(_drawn_inputs(seed))
    spreads = {'L0_ffn_gate_b': (0.0, 0.1),
     'L0_ffn_b1': (0.0, 0.48),
     'L0_ffn_b2': (0.0, 0.1),
     'L1_ffn_ln_gamma': (1.0, 0.2),
     'L1_ffn_ln_beta': (0.0, 0.1)}
    factors = {'L0_xattn_igate_bias': 64.0,
     'L1_ffn_biases': 8.0,
     'L1_ffn_lora_a': 4.957,
     'L1_ffn_lora_b': 4.95,
     'L1_xattn_bv': 2.675}
    for name, (base, spread) in spreads.items():
        noise = np.random.default_rng([zlib.crc32(name.encode()), seed]).standard_normal(out[name].shape)
        drawn = base * np.exp(spread * noise) if base else spread * noise
        out[name] = jnp.asarray(drawn.astype(out[name].dtype))
    for name, factor in factors.items():
        out[name] = (out[name] * factor).astype(out[name].dtype)
    return out
```

```python
from contextlib import ExitStack

import concourse.bass as bass
from concourse import mybir

P = 128
ALU = mybir.AluOpType
ACT = mybir.ActivationFunctionType
AX = mybir.AxisListType
F32 = mybir.dt.float32
BF16 = mybir.dt.bfloat16
I32 = mybir.dt.int32
U32 = mybir.dt.uint32

CAP_FACTOR, TOP_K, LEVELS, GROUP = 1.25, 2, 7.5, 16
LN_EPS, HEAD_EPS = 1e-5, 1e-6
LOWEST = -3.0e38
DROPPED = 1.0e6


def mega_kernel(nc, x, ctx, igate_kernel, igate_bias, fgate_kernel, fgate_bias, gate_w, gate_b,
                w1, b1, w2, b2, Wq, bq, Wv, bv, qweights, scales, biases, lora_a, lora_b,
                ln_gamma, ln_beta, out):
    NB, S, D = x.shape
    NH = igate_kernel.shape[1]
    HD = D // NH
    E, _, FF = w1.shape
    NL, _, _ = qweights.shape
    NBLK = NL // 2
    R = lora_a.shape[1]
    T = NB * S
    DC, FC = D // P, FF // P
    CAP = int(CAP_FACTOR * T / E)
    SLOTS = E * CAP
    G = 4
    NG = NB // G
    GT = G * P
    HU = NH // 2
    HA = HD + 1
    MT = -(-CAP // P)
    MTAIL = CAP - (MT - 1) * P
    NS = D // GROUP
    assert S == P and NH * NB == P and DC == 2 and HU * HD == P and SLOTS % P == 0

    with ExitStack() as stack:
        def sb(name, shape, dt=F32):
            return stack.enter_context(nc.sbuf_tensor(name, shape, dt))

        def sem(name):
            return stack.enter_context(nc.semaphore(name))

        gates_dram = nc.dram_tensor("gates_dram", (2 * NH, T), F32).ap()
        slots_dram = nc.dram_tensor("slots_dram", (SLOTS, D), F32).ap()
        experts_dram = nc.dram_tensor("experts_dram", (SLOTS, D), F32).ap()

        xres = sb("xres", [P, NB, D])
        ctx_tok = sb("ctx_tok", [P, NB, D])
        v_tok = ctx_tok
        ctxT = sb("ctxT", [P, DC, T])
        xnT = sb("xnT", [P, DC, T])
        hT = xnT
        vT = sb("vT", [P, DC, T])

        wT = sb("wT", [P, NL, DC, D])
        w1_sb = sb("w1_sb", [P, 2, DC, FF])
        w2_sb = sb("w2_sb", [P, 2, FC, D])
        b2_row = sb("b2_row", [P, E, D])
        gk_raw = sb("gk_raw", [P, 3 * DC, 2 * NH])
        gk_ctx = sb("gk_ctx", [P, DC, 2 * NH])
        gate_bias = sb("gate_bias", [2 * NH, 1])
        router_w = sb("router_w", [P, DC, E])
        router_b = sb("router_b", [P, E])
        wq_sb = sb("wq_sb", [P, DC, D])
        wv_sb = sb("wv_sb", [P, DC, D])
        bias_row = sb("bias_row", [P, NBLK, D])
        scale_sb = sb("scale_sb", [P, NL, DC, NS])
        la_sb = sb("la_sb", [R, NL, D])
        lb_sb = sb("lb_sb", [P, NL, DC, R])
        lbT = sb("lbT", [R, 2, D])
        B1, GA, BE, BI, BQ, BV = 0, E * FC, E * FC + NBLK * DC, E * FC + 2 * NBLK * DC, \
            E * FC + (2 * NBLK + NL) * DC, E * FC + (2 * NBLK + NL) * DC + DC
        NROWS = BV + DC
        rows = sb("rows", [NROWS, P])
        cols = sb("cols", [P, NROWS])

        ident = sb("ident", [P, P])
        ones = sb("ones", [P, P])
        tri_bf = sb("tri_bf", [P, P], BF16)
        ones_bf = sb("ones_bf", [P, P], BF16)
        seq_sel = sb("seq_sel", [P, NB])
        head_sel = sb("head_sel", [P, NH])
        expert_no_i = sb("expert_no_i", [P, E], I32)
        expert_no = sb("expert_no", [P, E])
        mhalf = sb("mhalf", [P, 16])
        zero_row = sb("zero_row", [P, D])

        bst = sb("bst", [P, NB, 6])
        bag = sb("bag", [P, NB, 2])
        veps = sb("veps", [P, NB])
        rstd = sb("rstd", [P, NB])
        bst2 = sb("bst2", [P, 2, 6])
        bag2 = sb("bag2", [P, 2, 2])
        veps2 = sb("veps2", [P, 2])
        rstd2 = sb("rstd2", [P, 2])
        gates_sb = sb("gates_sb", [2 * NH, T])
        gT = sb("gT", [P, P])
        limT = sb("limT", [P, P])
        neg_max = sb("neg_max", [P, NH, P])

        scratch = sb("scratch", [P, 8 * GT])

        def view(buf, at, *shape):
            n = 1
            for s in shape:
                n *= s
            flat = buf[:, at:at + n]
            if len(shape) == 1:
                return flat
            names = "abcd"[:len(shape)]
            return flat.rearrange(f"p ({' '.join(names)}) -> p {' '.join(names)}",
                                  **dict(zip(names, shape)))

        decay = view(scratch, 0, 2, HU, P)
        cmat = view(scratch, 2 * GT, 2, HU, P)
        qblk = view(scratch, 4 * GT, 2, HU, P)
        xn = view(scratch, 6 * GT, 4, D)
        xn2 = xn
        work = sb("work", [P, 8 * D])
        v_aug = sb("v_aug", [P, 2, NH, HA])
        sq = view(work, 0, NH, HD)
        yh = view(work, D, NH, HD)
        xn2T = view(work, 2 * D, 2, DC, P)
        qf = view(work, 6 * D, 2, D)
        gsc = sb("gsc", [P, 8, P])
        wraw = sb("wraw", [P, 2, DC, D], I32)
        wdeq = sb("wdeq", [P, 2, DC, D])
        small = sb("small", [P, 8, NH])
        lg = sb("lg", [P, E])
        top_v = sb("top_v", [P, 2, 8])
        top_i = sb("top_i", [P, 2, 8], U32)
        pick = sb("pick", [P, 4, 2, E])
        mask_bf = sb("mask_bf", [P, 4, E], BF16)
        seen_bf = sb("seen_bf", [P, NB + 1, E], BF16)
        topv = sb("topv", [P, NB, 2])
        topi = sb("topi", [P, NB, 2])
        rank = sb("rank", [P, 2, 2])
        ttr_out = sb("ttr_out", [P, 2, E])
        over = sb("over", [P, 2, 2])
        base = sb("base", [P, 2, 2])
        kept = sb("kept", [P, NB, 2])
        dest = sb("dest", [P, NB, 2], U32)
        wtop = sb("wtop", [P, NB, 2])
        xin = view(scratch, 0, 2, MT, D)
        xinT = view(scratch, 2 * MT * D, 2, DC, CAP)
        y_sb = view(work, 0, 2, MT, D)
        h_moe = [view(xnT.rearrange("p c t -> p (c t)"), 0, FC, CAP),
                 view(ctxT.rearrange("p c t -> p (c t)"), 0, FC, CAP)]
        gath = view(neg_max.rearrange("p h i -> p (h i)"), 0, 2, 2, D)
        ctx_flat = ctxT.rearrange("p c t -> p (c t)")
        xn3T = view(ctx_flat, 0, 2, DC, GT)
        qT = view(ctx_flat, 4 * GT, 2, DC, GT)
        xn3 = view(scratch, 0, 2, D)
        attn = view(scratch, 2 * D, 2, P)
        attnT = view(scratch, 3 * D, 2, P)
        xn4 = view(scratch, 4 * D, 2, D)
        smax = sb("smax", [P, 2, 2])
        b1_cur = sb("b1_cur", [P, 2, FC])
        affine = sb("affine", [P, 2, DC])
        w1_flat = w1_sb.rearrange("p a c f -> p (a c f)")
        yb = view(w1_flat, 0, 2 * G, D)
        zn = view(w1_flat, 2 * G * D, 2 * G, D)
        w2_flat = w2_sb.rearrange("p a c f -> p (a c f)")
        aT = view(w2_flat, 0, 2, DC, GT)
        w2cur = view(w2_flat, 4 * GT, DC, D)
        bst5 = sb("bst5", [P, G, 6])
        bag5 = sb("bag5", [P, 2, G, 2])
        veps5 = sb("veps5", [P, 2, G])
        rstd5 = sb("rstd5", [P, 2, G])
        o_sb = view(work, 0, 4, D)

        bank = [stack.enter_context(nc.psum_tensor(f"bank{i}", [P, 512], F32)) for i in range(8)]

        x_in = [sem(f"x_in{g}") for g in range(NG)]
        ctx_in = [sem(f"ctx_in{g}") for g in range(NG)]
        gk_in, rows_in, router_in, attnw_in, ffnw_in, b2_in, biasrow_in = (
            sem(n) for n in ("gk_in", "rows_in", "router_in", "attnw_in", "ffnw_in", "b2_in", "biasrow_in"))
        q_in = [sem(f"q_in{j}") for j in range(2)]
        w1_in = [sem(f"w1_in{j}") for j in range(2)]
        w2_in = [sem(f"w2_in{j}") for j in range(2)]
        slots_zeroed = sem("slots_zeroed")
        gates_out, gates_back = sem("gates_out"), sem("gates_back")
        xin_in = [sem(f"xin_in{j}") for j in range(2)]
        y_out = [sem(f"y_out{j}") for j in range(2)]
        scattered = [sem(f"scattered{j}") for j in range(4)]
        gathered = [sem(f"gathered{j}") for j in range(2)]
        out_done = sem("out_done")
        consts = sem("consts")
        pool_step, dve_step = sem("pool_step"), sem("dve_step")
        dve_consts, cols_turned, cols_ready = sem("dve_consts"), sem("cols_turned"), sem("cols_ready")
        xvar_ready, xrstd_ready, xn_ready = sem("xvar_ready"), sem("xrstd_ready"), sem("xn_ready")
        x_turned, x_copied = sem("x_turned"), sem("x_copied")
        ctx_turned, ctx_copied = sem("ctx_turned"), sem("ctx_copied")
        gkctx_ready, gates_done, gates_copied = sem("gkctx_ready"), sem("gates_done"), sem("gates_copied")
        fabs_ready, fexp_ready, fln_ready, gsum_ready, lim_ready = (
            sem(n) for n in ("fabs_ready", "fexp_ready", "fln_ready", "gsum_ready", "lim_ready"))
        negmax_ready, glim_turned, glim_copied = sem("negmax_ready"), sem("glim_turned"), sem("glim_copied")
        lb_turned, lb_copied, wdeq_ready, wT_done, wT_copied = (
            sem(n) for n in ("lb_turned", "lb_copied", "wdeq_ready", "wT_done", "wT_copied"))
        vT_done, vT_copied = sem("vT_done"), sem("vT_copied")
        qblk_ready, vaug_ready = sem("qblk_ready"), sem("vaug_ready")
        maxb_done, qk_done, exp_done, tri_done, c_ready, cv_done = (
            sem(n) for n in ("maxb_done", "qk_done", "exp_done", "tri_done", "c_ready", "cv_done"))
        sq_ready, ms_ready, rms_ready, yh_ready, var2_ready, rstd2_ready, xn2_ready = (
            sem(n) for n in ("sq_ready", "ms_ready", "rms_ready", "yh_ready", "var2_ready", "rstd2_ready", "xn2_ready"))
        xn2_turned, xn2T_copied, logits_done, logits_read, mask_ready, rank_done, rank_read, dest_ready = (
            sem(n) for n in ("xn2_turned", "xn2T_copied", "logits_done", "logits_read", "mask_ready",
                             "rank_done", "rank_read", "dest_ready"))
        topdiff_ready, topexp_ready = sem("topdiff_ready"), sem("topexp_ready")
        vtok_turned, vtok_copied = sem("vtok_turned"), sem("vtok_copied")
        xin_turned, xinT_copied, h_done, h_copied, y_done, y_ready = (
            sem(n) for n in ("xin_turned", "xinT_copied", "h_done", "h_copied", "y_done", "y_ready"))
        gath_zeroed, x2_ready = sem("gath_zeroed"), sem("x2_ready")
        var3_ready, rstd3_ready, xn3_ready, xn3_turned, xn3T_copied, q_done, q_copied = (
            sem(n) for n in ("var3_ready", "rstd3_ready", "xn3_ready", "xn3_turned", "xn3T_copied", "q_done", "q_copied"))
        score_done, smax_ready, attn_ready, attn_turned, attnT_copied, ctxv_done = (
            sem(n) for n in ("score_done", "smax_ready", "attn_ready", "attn_turned", "attnT_copied", "ctxv_done"))
        x3_ready, var4_ready, rstd4_ready, xn4_ready, xn4_turned, h_ready = (
            sem(n) for n in ("x3_ready", "var4_ready", "rstd4_ready", "xn4_ready", "xn4_turned", "h_ready"))
        w2cur_ready, yf_done, yb_ready, var5_ready, rstd5_ready, zn_ready, zn_turned, a_ready, y2_done, _unused = (
            sem(n) for n in ("w2cur_ready", "yf_done", "yb_ready", "var5_ready", "rstd5_ready", "zn_ready",
                             "zn_turned", "a_ready", "y2_done", "unused"))
        b1_ready, affine_ready, memset_done = sem("b1_ready"), sem("affine_ready"), sem("memset_done")
        fin_turned, fin_ready = sem("fin_turned"), sem("fin_ready")

        LAST = NB + 5
        VT_AT = {NB: (0, 1), NB + 1: (2, 3), NB + 2: (4, 5), NB + 3: (6,), NB + 4: (7,)}
        assert sum(len(v) for v in VT_AT.values()) == NG * DC
        block = stack.enter_context(nc.Block())

        @block.sync
        def _(sp):
            xv = x.rearrange("t p d -> p t d")
            cv = ctx.rearrange("t p d -> p t d")
            for g in range(NG):
                sp.dma_start(xres[:, g * G:(g + 1) * G, :], xv[:, g * G:(g + 1) * G, :]).then_inc(x_in[g], 16)
                sp.dma_start(ctx_tok[:, g * G:(g + 1) * G, :], cv[:, g * G:(g + 1) * G, :]).then_inc(ctx_in[g], 16)
            sp.dma_start(la_sb[:, :, :], lora_a.rearrange("l r d -> r l d")).then_inc(ffnw_in, 16)
            sp.dma_start(lb_sb[:, :, :, :].rearrange("p l c r -> p (l c) r"),
                         lora_b.rearrange("l (c p) r -> p (l c) r", p=P)).then_inc(ffnw_in, 16)
            sp.dma_start(scale_sb[:, :, :, :].rearrange("p l c s -> p (l c) s"),
                         scales.rearrange("l (c p) s -> p (l c) s", p=P)).then_inc(ffnw_in, 16)
            def load_quantised(l):
                if l >= 2:
                    sp.wait_ge(wdeq_ready, 2 * (l - 2) + 1)
                sp.dma_start(wraw[:, l % 2, :, :],
                             qweights[l].rearrange("(c p) d -> p c d", p=P)).then_inc(q_in[l % 2], 16)

            for l in range(4):
                load_quantised(l)
            sp.wait_ge(gates_copied, NG)
            sp.dma_start(gates_dram, gates_sb[:, :]).then_inc(gates_out, 16)
            sp.wait_ge(gates_out, 16)
            gview = gates_dram.rearrange("(k h) (b s) -> k (h b) s", k=2, s=P)
            sp.dma_start(gsc[:, 0, :], gview[0]).then_inc(gates_back, 16)
            sp.dma_start(gsc[:, 1, :], gview[1]).then_inc(gates_back, 16)
            for l in range(4, NL):
                load_quantised(l)
            for e in range(2):
                sp.dma_start(w1_sb[:, e, :, :], w1[e].rearrange("(c p) f -> p c f", p=P)).then_inc(w1_in[e], 16)
                sp.dma_start(w2_sb[:, e, :, :], w2[e].rearrange("(c p) d -> p c d", p=P)).then_inc(w2_in[e], 16)

            def load_slots(e, j):
                rows_e = slots_dram[bass.ds(e * CAP, CAP), :]
                sp.dma_start(xin[:, j, 0:MT - 1, :],
                             rows_e[0:(MT - 1) * P, :].rearrange("(m p) d -> p m d", p=P)).then_inc(xin_in[j], 16)
                sp.dma_start(xin[0:MTAIL, j, MT - 1, :], rows_e[(MT - 1) * P:CAP, :]).then_inc(xin_in[j], 16)

            def store_rows(e, j):
                rows_e = experts_dram[bass.ds(e * CAP, CAP), :]
                sp.wait_ge(y_ready, MT * e + MT)
                sp.dma_start(rows_e[0:(MT - 1) * P, :].rearrange("(m p) d -> p m d", p=P),
                             y_sb[:, j, 0:MT - 1, :]).then_inc(y_out[j], 16)
                sp.dma_start(rows_e[(MT - 1) * P:CAP, :], y_sb[0:MTAIL, j, MT - 1, :]).then_inc(y_out[j], 16)

            for j in range(4):
                sp.wait_ge(scattered[j], 32 * (NB // 4))
            for e in range(2):
                load_slots(e, e)
            with sp.Fori(0, E // 2 - 1) as k:
                for j in range(2):
                    e = 2 * k + j
                    sp.wait_ge(xin_turned, DC * e + DC)
                    load_slots(e + 2, j)
                    sp.wait_ge(h_done, FC * e + FC)
                    sp.dma_start(w1_sb[:, j, :, :],
                                 w1[bass.ds(e + 2, 1)].rearrange("a (c p) f -> p (a c) f", p=P)).then_inc(w1_in[j], 16)
                    sp.wait_ge(y_done, MT * e + MT)
                    sp.dma_start(w2_sb[:, j, :, :],
                                 w2[bass.ds(e + 2, 1)].rearrange("a (c p) d -> p (a c) d", p=P)).then_inc(w2_in[j], 16)
                    store_rows(e, j)
            for e in range(E - 2, E):
                store_rows(e, e % 2)
            ov = out.rearrange("t p d -> p t d")
            for t in range(NB):
                sp.wait_ge(fin_ready, t + 1)
                sp.dma_start(ov[:, t, :], o_sb[:, t % 4, :]).then_inc(out_done, 16)
                if t % 4 == 3:
                    sp.wait_ge(out_done, 16 * (t + 1))

        @block.gpsimd
        def _(pool):
            steps = [0]

            def link(ins):
                steps[0] += 1
                ins.then_inc(pool_step, 1)
                pool.wait_ge(pool_step, steps[0])

            pool.memset(ident[:, :], 0.0).then_inc(pool_step, 1)
            pool.memset(tri_bf[:, :], 1.0).then_inc(pool_step, 1)
            steps[0] += 2
            pool.wait_ge(pool_step, 2)
            pool.affine_select(out=ident[:, :], in_=ident[:, :], compare_op=ALU.not_equal, fill=1.0,
                               base=0, pattern=[[-1, P]], channel_multiplier=1).then_inc(consts, 1)
            pool.memset(zero_row[:, :], 0.0).then_inc(consts, 1)
            pool.wait_ge(consts, 2)
            pool.dma_start(slots_dram.rearrange("(p r) d -> p r d", p=P),
                           zero_row[:, :].unsqueeze(1).to_broadcast([P, SLOTS // P, D])).then_inc(slots_zeroed, 16)
            pool.memset(mhalf[:, :], -0.5).then_inc(consts, 1)
            pool.affine_select(out=tri_bf[:, :], in_=tri_bf[:, :], compare_op=ALU.is_ge, fill=0.0,
                               base=0, pattern=[[1, P]], channel_multiplier=-1).then_inc(consts, 1)
            pool.memset(ones_bf[:, :], 1.0).then_inc(consts, 1)
            pool.memset(ones[:, :], 1.0).then_inc(consts, 1)
            pool.memset(v_aug[:, :, :, :], 1.0).then_inc(consts, 1)
            pool.iota(expert_no_i[:, :], pattern=[[1, E]], base=0, channel_multiplier=0).then_inc(consts, 1)
            pool.wait_ge(consts, 3)
            for g in range(NG):
                pool.wait_ge(xvar_ready, g + 1)
                pool.tensor_tensor(rstd[:, g * G:(g + 1) * G], veps[:, g * G:(g + 1) * G],
                                   mhalf[:, 0:G], ALU.pow).then_inc(xrstd_ready, 1)

            pool.wait_ge(slots_zeroed, 16)

            def causal(u):
                pool.wait_ge(exp_done, HU * (u + 1))
                d = decay[:, u % 2, :, :]
                pool.affine_select(out=d, in_=d, compare_op=ALU.is_ge, fill=0.0, base=0,
                                   pattern=[[0, HU], [1, P]], channel_multiplier=-1).then_inc(tri_done, 1)

            def head_rms(b):
                pool.wait_ge(ms_ready, b + 1)
                if b >= 2:
                    pool.wait_ge(yh_ready, b - 1)
                pool.tensor_tensor(small[:, 4 + b % 2, :], small[:, 2 + b % 2, :], mhalf[:, 0:NH],
                                   ALU.pow).then_inc(rms_ready, 1)

            def norm2(b):
                pool.wait_ge(var2_ready, b + 1)
                pool.tensor_tensor(rstd2[:, b % 2:b % 2 + 1], veps2[:, b % 2:b % 2 + 1], mhalf[:, 0:1],
                                   ALU.pow).then_inc(rstd2_ready, 1)

            def scatter(b):
                pool.wait_ge(dest_ready, b + 1)
                for k in range(TOP_K):
                    pool.indirect_dma_start(
                        out=slots_dram[:, :],
                        out_offset=bass.IndirectOffsetOnAxis(ap=dest[:, b, k:k + 1], axis=0),
                        in_=xn2[:, b % 4, :], in_offset=None,
                        bounds_check=SLOTS - 1, oob_is_err=False).then_inc(scattered[b % 4], 16)

            for i in range(LAST):
                if i < NB:
                    causal(2 * i)
                if 2 <= i < NB + 2:
                    head_rms(i - 2)
                if i < NB:
                    causal(2 * i + 1)
                if 2 <= i < NB + 2:
                    norm2(i - 2)
                if 5 <= i:
                    scatter(i - 5)

            pool.wait_ge(gath_zeroed, 1)
            for j in range(2):
                pool.wait_ge(y_out[j], 32 * (E // 2))

            def gather(b):
                if b >= 2:
                    pool.wait_ge(x2_ready, b - 1)
                for k in range(TOP_K):
                    pool.indirect_dma_start(
                        out=gath[:, b % 2, k, :], out_offset=None, in_=experts_dram[:, :],
                        in_offset=bass.IndirectOffsetOnAxis(ap=dest[:, b, k:k + 1], axis=0),
                        bounds_check=SLOTS - 1, oob_is_err=False).then_inc(gathered[b % 2], 16)

            gather(0)
            for i in range(NB + 5):
                if i + 1 < NB:
                    gather(i + 1)
                if i < NB:
                    pool.wait_ge(var3_ready, i + 1)
                    pool.tensor_tensor(rstd2[:, i % 2:i % 2 + 1], veps2[:, i % 2:i % 2 + 1],
                                       mhalf[:, 0:1], ALU.pow).then_inc(rstd3_ready, 1)
                if i >= 5:
                    pool.wait_ge(var4_ready, i - 4)
                    pool.tensor_tensor(rstd5[:, 0, (i - 5) % 2:(i - 5) % 2 + 1],
                                       veps5[:, 0, (i - 5) % 2:(i - 5) % 2 + 1],
                                       mhalf[:, 0:1], ALU.pow).then_inc(rstd4_ready, 1)
            with pool.Fori(0, NBLK) as blk:
                for g in range(NG):
                    pool.wait_ge(var5_ready, NG * blk + (g + 1))
                    pool.tensor_tensor(rstd5[:, g % 2, :], veps5[:, g % 2, :], mhalf[:, 0:G],
                                       ALU.pow).then_inc(rstd5_ready, 1)

        @block.scalar
        def _(act):
            act.dma_start(gk_raw[:, :, 0:NH], igate_kernel.rearrange("(c p) h -> p c h", p=P)).then_inc(gk_in, 16)
            act.dma_start(gk_raw[:, :, NH:2 * NH], fgate_kernel.rearrange("(c p) h -> p c h", p=P)).then_inc(gk_in, 16)
            act.dma_start(gate_bias[0:NH, :], igate_bias.unsqueeze(1)).then_inc(gk_in, 16)
            act.dma_start(gate_bias[NH:2 * NH, :], fgate_bias.unsqueeze(1)).then_inc(gk_in, 16)
            for at, src in ((B1, b1), (GA, ln_gamma), (BE, ln_beta), (BI, biases)):
                n = src.shape[0] * src.shape[1] // P
                act.dma_start(rows[at:at + n, :], src.rearrange("n (c p) -> (n c) p", p=P)).then_inc(rows_in, 16)
            act.dma_start(rows[BQ:BQ + DC, :], bq.rearrange("(c p) -> c p", p=P)).then_inc(rows_in, 16)
            act.dma_start(rows[BV:BV + DC, :], bv.rearrange("(c p) -> c p", p=P)).then_inc(rows_in, 16)
            act.dma_start(router_w[:, :, :], gate_w.rearrange("(c p) e -> p c e", p=P)).then_inc(router_in, 16)
            act.dma_start(router_b[:, :], gate_b.partition_broadcast(P)).then_inc(router_in, 16)
            act.dma_start(wq_sb[:, :, :], Wq.rearrange("(c p) n -> p c n", p=P)).then_inc(attnw_in, 16)
            act.dma_start(wv_sb[:, :, :], Wv.rearrange("(c p) n -> p c n", p=P)).then_inc(attnw_in, 16)
            act.dma_start(b2_row[:, :, :], b2.partition_broadcast(P)).then_inc(b2_in, 16)
            act.dma_start(bias_row[:, :, :],
                          biases.rearrange("(n two) d -> n two d", two=2)[:, 0, :].partition_broadcast(P)
                          ).then_inc(biasrow_in, 16)

            def copy_ctx(t):
                act.wait_ge(ctx_turned, t + 1)
                nc.scalar.copy(ctxT[:, :, t * P:(t + 1) * P],
                               bank[2 + t % 2][:, 0:D].rearrange("p (c s) -> p c s", c=DC)).then_inc(ctx_copied, 1)

            def copy_gates(g):
                act.wait_ge(gates_done, g + 1)
                act.wait_ge(gk_in, 64)
                nc.scalar.activation(gates_sb[:, g * GT:(g + 1) * GT], bank[4 + g % 2][0:2 * NH, :],
                                     ACT.Identity, bias=gate_bias[:, 0:1]).then_inc(gates_copied, 1)

            for t in range(NB):
                copy_ctx(t)
                if t % G == G - 1 and t > G:
                    copy_gates(t // G - 1)
            copy_gates(NG - 1)
            act.wait_ge(fabs_ready, 1)
            nc.scalar.activation(gsc[:, 3, :], gsc[:, 2, :], ACT.Exp).then_inc(fexp_ready, 1)
            act.wait_ge(fexp_ready, 1)
            nc.scalar.activation(gsc[:, 4, :], gsc[:, 3, :], ACT.Ln, bias=1.0).then_inc(fln_ready, 1)
            act.wait_ge(gsum_ready, 1)
            nc.scalar.activation(gsc[:, 2, :], gsc[:, 7, :], ACT.Exp, scale=-1.0).then_inc(lim_ready, 1)

            def v_with_ones(b):
                if b >= 2:
                    act.wait_ge(cv_done, 2 * (b - 1))
                act.wait_ge(consts, 8)
                nc.scalar.copy(v_aug[:, b % 2, :, 0:HD],
                               ctx_tok[:, b, :].rearrange("p (h d) -> p h d", h=NH)).then_inc(vaug_ready, 1)

            v_with_ones(0)
            for l in range(NL):
                act.wait_ge(wT_done, l + 1)
                nc.scalar.copy(wT[:, l, :, :], bank[l % 2][:, :].rearrange("p (c n) -> p c n", c=DC)).then_inc(wT_copied, 1)

            def decays(u):
                b = u // 2
                act.wait_ge(maxb_done, u + 1)
                act.wait_ge(glim_copied, 1)
                if u >= 2:
                    act.wait_ge(c_ready, u - 1)
                for h in range(HU):
                    col = (HU * (u % 2) + h) * NB + b
                    nc.scalar.activation(decay[:, u % 2, h, :], bank[u % 2][:, h * P:(h + 1) * P], ACT.Exp,
                                         bias=gT[:, col:col + 1]).then_inc(exp_done, 1)

            def squares(b):
                act.wait_ge(cv_done, 2 * b + 2)
                if b >= 1:
                    act.wait_ge(ms_ready, b)
                nc.scalar.activation(sq[:, :, :], bank[4 + b % 2][:, 0:NH * HA].rearrange("p (h d) -> p h d", h=NH)[:, :, 0:HD],
                                     ACT.Square).then_inc(sq_ready, 1)

            def copy_xn2T(b):
                act.wait_ge(xn2_turned, b + 1)
                if b >= 2:
                    act.wait_ge(logits_done, b - 1)
                nc.scalar.copy(xn2T[:, b % 2, :, :], bank[6][:, 0:D].rearrange("p (c s) -> p c s", c=DC)).then_inc(xn2T_copied, 1)

            def copy_vT(n):
                g, o = n // DC, n % DC
                act.wait_ge(vT_done, n + 1)
                act.wait_ge(cols_ready, 1)
                nc.scalar.activation(vT[:, o, g * GT:(g + 1) * GT], bank[n % 4][:, :], ACT.Identity,
                                     bias=cols[:, BV + o:BV + o + 1]).then_inc(vT_copied, 1)

            for i in range(LAST):
                if i < NB:
                    decays(2 * i)
                if 2 <= i < NB + 2:
                    squares(i - 2)
                if 3 <= i < NB + 3:
                    copy_xn2T(i - 3)
                if i < NB:
                    decays(2 * i + 1)
                if 1 <= i + 1 < NB:
                    v_with_ones(i + 1)
                for n in VT_AT.get(i - 1, ()):
                    copy_vT(n)
            act.wait_ge(topdiff_ready, 1)
            nc.scalar.activation(wtop[:, :, 0], wtop[:, :, 1], ACT.Exp).then_inc(topexp_ready, 1)
            for n in VT_AT[LAST - 1]:
                copy_vT(n)

            def hidden(e, j):
                if not isinstance(e, int) or e >= 2:
                    act.wait_ge(y_done, MT * e - MT)
                act.wait_ge(b1_ready, e + 1)
                for f in range(FC):
                    act.wait_ge(h_done, FC * e + (f + 1))
                    nc.scalar.activation(h_moe[j][:, f, :], bank[f % 4][:, 0:CAP], ACT.Relu,
                                         bias=b1_cur[:, j, f:f + 1]).then_inc(h_copied, 1)

            for e in range(2):
                hidden(e, e)
            with act.Fori(1, E // 2) as k:
                for j in range(2):
                    hidden(2 * k + j, j)

            for i in range(NB + 6):
                if 4 <= i < NB + 4:
                    b = i - 4
                    act.wait_ge(smax_ready, b + 1)
                    if b >= 2:
                        act.wait_ge(attn_turned, b - 1)
                    nc.scalar.activation(attn[:, b % 2, :], bank[b % 2][:, 0:P], ACT.Exp,
                                         bias=smax[:, 0, b % 2:b % 2 + 1],
                                         accum_out=smax[:, 1, b % 2:b % 2 + 1]).then_inc(attn_ready, 1)
                if i < NB:
                    act.wait_ge(xn3_turned, i + 1)
                    if i % G == 0 and i >= 2 * G:
                        act.wait_ge(q_done, DC * (i // G - 1))
                    nc.scalar.copy(xn3T[:, i // G % 2, :, i % G * P:(i % G + 1) * P],
                                   bank[4][:, 0:D].rearrange("p (c s) -> p c s", c=DC)).then_inc(xn3T_copied, 1)
                if i < NB and i % G == G - 1:
                    g = i // G
                    for o in range(DC):
                        act.wait_ge(q_done, DC * g + o + 1)
                        if g >= 2:
                            act.wait_ge(score_done, G * (g - 1))
                        nc.scalar.activation(qT[:, g % 2, o, :], bank[6 + o][:, :], ACT.Identity,
                                             bias=cols[:, BQ + o:BQ + o + 1]).then_inc(q_copied, 1)
                if 4 <= i < NB + 4:
                    b = i - 4
                    act.wait_ge(attn_turned, b + 1)
                    if b >= 2:
                        act.wait_ge(ctxv_done, b - 1)
                    nc.scalar.copy(attnT[:, b % 2, :], bank[2][:, 0:P]).then_inc(attnT_copied, 1)
                if i >= 6:
                    b = i - 6
                    act.wait_ge(xn4_turned, b + 1)
                    nc.scalar.copy(hT[:, :, b * P:(b + 1) * P],
                                   bank[5][:, 0:D].rearrange("p (c s) -> p c s", c=DC)).then_inc(h_ready, 1)

            with act.Fori(0, NBLK) as blk:
                act.wait_ge(affine_ready, 2 * blk + 2)
                for g in range(NG):
                    n = NG * blk + g
                    for c in range(DC):
                        act.wait_ge(zn_turned, DC * n + (c + 1))
                        nc.scalar.activation(aT[:, g % 2, c, :], bank[2 + c][:, :], ACT.Gelu,
                                             bias=affine[:, 1, c:c + 1],
                                             scale=affine[:, 0, c:c + 1]).then_inc(a_ready, 1)

        @block.vector
        def _(dve):
            steps = [0]
            vec = nc.vector

            def step(ins):
                steps[0] += 1
                ins.then_inc(dve_step, 1)

            def settle():
                dve.wait_ge(dve_step, steps[0])

            def link(ins):
                step(ins)
                settle()

            dve.wait_ge(consts, 8)
            i3 = ident[:, :].rearrange("p (h b) -> p h b", h=NH)
            vec.tensor_reduce(head_sel[:, :], i3, AX.X, ALU.add).then_inc(dve_consts, 1)
            vec.tensor_reduce(seq_sel[:, :], ident[:, :].rearrange("p (h b) -> p b h", h=NH), AX.X,
                              ALU.add).then_inc(dve_consts, 1)
            vec.tensor_copy(expert_no[:, :], expert_no_i[:, :]).then_inc(dve_consts, 1)
            vec.memset(qblk[:, :, :, :], 0.0).then_inc(dve_consts, 1)

            def norm1(t):
                dve.wait_ge(xrstd_ready, t // G + 1)
                if t >= 4:
                    dve.wait_ge(x_turned, t - 3)
                vec.tensor_scalar(xn[:, t % 4, :], xres[:, t, :], bag[:, t, 0:1], rstd[:, t:t + 1],
                                  ALU.subtract, ALU.mult).then_inc(xn_ready, 1)

            def copy_xT(t):
                dve.wait_ge(x_turned, t + 1)
                vec.tensor_copy(xnT[:, :, t * P:(t + 1) * P],
                                bank[t % 2][:, 0:D].rearrange("p (c s) -> p c s", c=DC)).then_inc(x_copied, 1)

            def stats1(g):
                dve.wait_ge(x_in[g], 16)
                for t in range(g * G, (g + 1) * G):
                    step(vec.bn_stats(bst[:, t, :], xres[:, t, :]))
                settle()
                for t in range(g * G, (g + 1) * G):
                    step(vec.bn_aggr(bag[:, t, :], bst[:, t, :]))
                settle()
                vec.tensor_scalar(veps[:, g * G:(g + 1) * G], bag[:, g * G:(g + 1) * G, 1], LN_EPS, None,
                                  ALU.add).then_inc(xvar_ready, 1)

            stats1(0)
            for g in range(NG):
                if g + 1 < NG:
                    stats1(g + 1)
                for t in range(g * G, (g + 1) * G):
                    norm1(t)
                    if t >= 1:
                        copy_xT(t - 1)
                if g == 0:
                    dve.wait_ge(gk_in, 64)
                    vec.tensor_tensor(gk_ctx[:, :, :], gk_raw[:, DC:2 * DC, :], gk_raw[:, 2 * DC:3 * DC, :],
                                      ALU.add).then_inc(gkctx_ready, 1)
                    dve.wait_ge(cols_turned, 1)
                    vec.tensor_copy(cols[:, :], bank[6][:, 0:NROWS]).then_inc(cols_ready, 1)
            copy_xT(NB - 1)

            def dequant(l):
                dve.wait_ge(q_in[l % 2], 16 * (l // 2 + 1))
                if l == 0:
                    dve.wait_ge(ffnw_in, 48)
                if l >= 2:
                    dve.wait_ge(wT_done, l - 1)
                vec.tensor_scalar(wdeq[:, l % 2, :, :], wraw[:, l % 2, :, :], 1.0 / LEVELS, -1.0,
                                  ALU.mult, ALU.add).then_inc(wdeq_ready, 1)
                dve.wait_ge(wdeq_ready, 2 * l + 1)
                w4 = wdeq[:, l % 2, :, :].rearrange("p c (s g) -> p (c s) g", g=GROUP)
                vec.tensor_tensor(w4, w4, scale_sb[:, l, :, :].rearrange("p c s -> p (c s)").unsqueeze(2)
                                  .to_broadcast([P, DC * NS, GROUP]), ALU.mult).then_inc(wdeq_ready, 1)

            def copy_lbT(l):
                dve.wait_ge(lb_turned, l + 1)
                if l >= 2:
                    dve.wait_ge(wT_done, l - 1)
                vec.tensor_copy(lbT[:, l % 2, :], bank[6 + l % 2][0:R, 0:D]).then_inc(lb_copied, 1)

            def make_weight(l):
                dequant(l)
                copy_lbT(l)

            make_weight(0)
            make_weight(1)

            dve.wait_ge(gates_back, 32)
            ig, fg, fabs, fl = gsc[:, 0, :], gsc[:, 1, :], gsc[:, 2, :], gsc[:, 4, :]
            lf, fsum, key_gate, gmax, fm = gsc[:, 3, :], gsc[:, 5, :], gsc[:, 6, :], gsc[:, 1, :], gsc[:, 7, :]
            vec.scalar_tensor_tensor(out=fabs, in0=fg, scalar=-1.0, in1=fg, op0=ALU.mult, op1=ALU.min).then_inc(fabs_ready, 1)
            dve.wait_ge(fln_ready, 1)
            link(vec.scalar_tensor_tensor(out=lf, in0=fg, scalar=0.0, in1=fl, op0=ALU.min, op1=ALU.subtract))
            link(vec.tensor_tensor_scan(fsum, ones[:, :], lf, 0.0, ALU.mult, ALU.add))
            link(vec.tensor_tensor(key_gate, ig, fsum, ALU.subtract))
            link(vec.tensor_tensor_scan(gmax, ones[:, :], key_gate, LOWEST, ALU.mult, ALU.max))
            vec.tensor_tensor(fm, fsum, gmax, ALU.add).then_inc(gsum_ready, 1)
            for h in range(NH):
                vec.tensor_scalar(neg_max[:, h, :], gmax, head_sel[:, h:h + 1], -1.0, ALU.mult,
                                  ALU.mult).then_inc(negmax_ready, 1)

            def query_blocks(u):
                b, c = u // 2, u % 2
                if u >= 2:
                    dve.wait_ge(qk_done, u - 1)
                for h in range(HU):
                    ins = vec.tensor_scalar(qblk[h * HD:(h + 1) * HD, u % 2, h, :],
                                            xnT[h * HD:(h + 1) * HD, c, b * P:(b + 1) * P],
                                            float(HD) ** -0.5, None, ALU.mult)
                ins.then_inc(qblk_ready, 1)

            def weigh(u):
                dve.wait_ge(qk_done, u + 1)
                dve.wait_ge(tri_done, u + 1)
                if u >= 2:
                    dve.wait_ge(cv_done, u - 1)
                vec.tensor_tensor(cmat[:, u % 2, :, :].rearrange("p h s -> p (h s)"), bank[2 + u % 2][:, :],
                                  decay[:, u % 2, :, :].rearrange("p h s -> p (h s)"), ALU.mult).then_inc(c_ready, 1)

            query_blocks(0)
            query_blocks(1)
            dve.wait_ge(glim_turned, 2)
            vec.tensor_copy(gT[:, :], bank[4][:, 0:P]).then_inc(dve_consts, 1)
            vec.tensor_copy(limT[:, :], bank[5][:, 0:P]).then_inc(glim_copied, 1)
            for l in range(2, NL):
                make_weight(l)

            def heads(b):
                o = bank[4 + b % 2][:, 0:NH * HA].rearrange("p (h d) -> p h d", h=NH)
                return o[:, :, 0:HD], o[:, :, HD]

            def rms1(b):
                num, tot = heads(b)
                den, ss, ms, rec = (small[:, k, :] for k in (0, 1, 2 + b % 2, 6 + b % 2))
                dve.wait_ge(sq_ready, b + 1)
                lim = limT[:, :].rearrange("p (h b) -> p b h", h=NH)[:, b, :]
                step(vec.tensor_tensor(den, tot, lim, ALU.max))
                step(vec.tensor_reduce(ss, sq[:, :, :], AX.X, ALU.add))
                settle()
                link(vec.scalar_tensor_tensor(out=den, in0=tot, scalar=-1.0, in1=den, op0=ALU.mult, op1=ALU.max))
                link(vec.tensor_scalar(den, den, HEAD_EPS, None, ALU.add))
                link(vec.reciprocal(rec, den))
                link(vec.tensor_tensor(ss, ss, rec, ALU.mult))
                link(vec.tensor_tensor(ss, ss, rec, ALU.mult))
                vec.tensor_scalar(ms, ss, 1.0 / HD, HEAD_EPS, ALU.mult, ALU.add).then_inc(ms_ready, 1)

            def rms2(b):
                num, _ = heads(b)
                rec, rr = small[:, 6 + b % 2, :], small[:, 4 + b % 2, :]
                dve.wait_ge(rms_ready, b + 1)
                link(vec.tensor_tensor(rec, rec, rr, ALU.mult))
                vec.tensor_tensor(yh[:, :, :], num, rec.unsqueeze(2).to_broadcast([P, NH, HD]),
                                  ALU.mult).then_inc(yh_ready, 1)
                dve.wait_ge(yh_ready, b + 1)
                link(vec.tensor_tensor(xres[:, b, :], xres[:, b, :], yh[:, :, :].rearrange("p h d -> p (h d)"), ALU.add))
                link(vec.bn_stats(bst2[:, b % 2, :], xres[:, b, :]))
                link(vec.bn_aggr(bag2[:, b % 2, :], bst2[:, b % 2, :]))
                vec.tensor_scalar(veps2[:, b % 2:b % 2 + 1], bag2[:, b % 2, 1:2], LN_EPS, None,
                                  ALU.add).then_inc(var2_ready, 1)

            def norm2(b):
                dve.wait_ge(rstd2_ready, b + 1)
                if b >= 4:
                    dve.wait_ge(scattered[b % 4], 32 * (b // 4))
                vec.tensor_scalar(xn2[:, b % 4, :], xres[:, b, :], bag2[:, b % 2, 0:1], rstd2[:, b % 2:b % 2 + 1],
                                  ALU.subtract, ALU.mult).then_inc(xn2_ready, 1)

            def choose(b):
                dve.wait_ge(logits_done, b + 1)
                vec.tensor_tensor(lg[:, :], bank[7][:, 0:E], router_b[:, :], ALU.add).then_inc(logits_read, 1)
                dve.wait_ge(logits_read, b + 1)
                link(vec.max(top_v[:, b % 2, :], lg[:, :]))
                step(vec.max_index(top_i[:, b % 2, :], top_v[:, b % 2, :], lg[:, :]))
                step(vec.tensor_copy(topv[:, b, :], top_v[:, b % 2, 0:2]))
                settle()
                link(vec.tensor_copy(topi[:, b, :], top_i[:, b % 2, 0:2]))
                for k in range(TOP_K):
                    step(vec.tensor_scalar(pick[:, b % 4, k, :], expert_no[:, :], topi[:, b, k:k + 1], None, ALU.is_equal))
                settle()
                vec.tensor_tensor(mask_bf[:, b % 4, :], pick[:, b % 4, 0, :], pick[:, b % 4, 1, :],
                                  ALU.add).then_inc(mask_ready, 1)
                dve.wait_ge(mask_ready, 2 * b + 1)
                vec.tensor_tensor(seen_bf[:, b + 1, :], seen_bf[:, b, :], mask_bf[:, b % 4, :],
                                  ALU.add).then_inc(mask_ready, 1)

            def slots(b):
                dve.wait_ge(rank_done, b + 1)
                rk = rank[:, b % 2, :]
                for k in range(TOP_K):
                    vec.tensor_tensor_reduce(ttr_out[:, k, :], pick[:, b % 4, k, :], bank[7][:, 64:64 + E], 1.0, 0.0,
                                             ALU.mult, ALU.add, rk[:, k:k + 1]).then_inc(rank_read, 1)
                dve.wait_ge(rank_read, 2 * b + 2)
                step(vec.tensor_scalar(over[:, b % 2, :], rk, float(CAP), DROPPED, ALU.is_gt, ALU.mult))
                step(vec.tensor_scalar(kept[:, b, :], rk, float(CAP), None, ALU.is_le))
                step(vec.scalar_tensor_tensor(out=base[:, b % 2, :], in0=topi[:, b, :], scalar=float(CAP), in1=rk,
                                              op0=ALU.mult, op1=ALU.add))
                settle()
                vec.scalar_tensor_tensor(out=dest[:, b, :], in0=base[:, b % 2, :], scalar=-1.0, in1=over[:, b % 2, :],
                                         op0=ALU.add, op1=ALU.add).then_inc(dest_ready, 1)

            link(vec.memset(seen_bf[:, 0, :], 0.0))
            dve.wait_ge(router_in, 32)
            for i in range(LAST):
                if 0 < 2 * i - 1 < 2 * NB:
                    weigh(2 * i - 1)
                if 2 * i + 2 < 2 * NB:
                    query_blocks(2 * i + 2)
                if 5 <= i:
                    slots(i - 5)
                if 2 <= i < NB + 2:
                    rms1(i - 2)
                if 2 * i + 3 < 2 * NB:
                    query_blocks(2 * i + 3)
                if i < NB:
                    weigh(2 * i)
                if 2 <= i < NB + 2:
                    rms2(i - 2)
                if 3 <= i < NB + 3:
                    choose(i - 3)
                if 2 <= i < NB + 2:
                    norm2(i - 2)

            link(vec.memset(gath[:, :, :, :], 0.0))
            vec.tensor_tensor(wtop[:, :, 1], topv[:, :, 1], topv[:, :, 0], ALU.subtract).then_inc(topdiff_ready, 1)
            dve.wait_ge(topexp_ready, 1)
            link(vec.tensor_scalar(wtop[:, :, 1], wtop[:, :, 0], 1.0, None, ALU.add))
            link(vec.reciprocal(veps[:, 0:NB], wtop[:, :, 1]))
            link(vec.tensor_tensor(wtop[:, :, 1], wtop[:, :, 0], veps[:, 0:NB], ALU.mult))
            link(vec.tensor_copy(wtop[:, :, 0], veps[:, 0:NB]))
            vec.tensor_tensor(wtop[:, :, :], wtop[:, :, :], kept[:, :, :], ALU.mult).then_inc(gath_zeroed, 1)

            for b in range(NB):
                dve.wait_ge(vtok_turned, b + 1)
                vec.tensor_copy(v_tok[:, b, :], bank[b % 4][:, 0:D]).then_inc(vtok_copied, 1)

            def copy_xinT(e, j):
                vec.tensor_copy(b1_cur[:, j, :], cols[:, bass.ds(B1 + FC * e, FC)]).then_inc(b1_ready, 1)
                for c in range(DC):
                    dve.wait_ge(xin_turned, DC * e + (c + 1))
                    vec.tensor_copy(xinT[:, j, c, :], bank[4 + c][:, 0:CAP]).then_inc(xinT_copied, 1)

            def results(e, j, first):
                if not first:
                    dve.wait_ge(y_out[j], 16 * e - 16 * j)
                for m in range(MT):
                    n = P if m < MT - 1 else MTAIL
                    dve.wait_ge(y_done, MT * e + (m + 1))
                    bb = b2_row[0:n, bass.ds(e, 1), :].rearrange("p a d -> p (a d)")
                    vec.tensor_tensor(y_sb[0:n, j, m, :], bank[6 + (MT * j + m) % 2][0:n, 0:D], bb, ALU.add).then_inc(y_ready, 1)

            dve.wait_ge(b2_in, 16)
            copy_xinT(0, 0)
            copy_xinT(1, 1)
            results(0, 0, True)
            copy_xinT(2, 0)
            results(1, 1, True)
            with dve.Fori(1, E // 2 - 1) as k:
                for j in range(2):
                    copy_xinT(2 * k + (j + 1), 1 - j)
                    results(2 * k + j, j, False)
            for e in range(E - 2, E):
                if e + 1 < E:
                    copy_xinT(e + 1, (e + 1) % 2)
                results(e, e % 2, False)

            def combine(b):
                dve.wait_ge(gathered[b % 2], 32 * (b // 2 + 1))
                link(vec.scalar_tensor_tensor(out=xres[:, b, :], in0=gath[:, b % 2, 0, :], scalar=wtop[:, b, 0:1],
                                              in1=xres[:, b, :], op0=ALU.mult, op1=ALU.add))
                vec.scalar_tensor_tensor(out=xres[:, b, :], in0=gath[:, b % 2, 1, :], scalar=wtop[:, b, 1:2],
                                         in1=xres[:, b, :], op0=ALU.mult, op1=ALU.add).then_inc(x2_ready, 1)
                dve.wait_ge(x2_ready, b + 1)
                link(vec.bn_stats(bst2[:, b % 2, :], xres[:, b, :]))
                link(vec.bn_aggr(bag2[:, b % 2, :], bst2[:, b % 2, :]))
                vec.tensor_scalar(veps2[:, b % 2:b % 2 + 1], bag2[:, b % 2, 1:2], LN_EPS, None,
                                  ALU.add).then_inc(var3_ready, 1)

            def score_max(b):
                dve.wait_ge(score_done, b + 1)
                if b >= 2:
                    dve.wait_ge(x3_ready, b - 1)
                vec.tensor_reduce(smax[:, 0, b % 2:b % 2 + 1], bank[b % 2][:, 0:P], AX.X, ALU.max,
                                  negate=True).then_inc(smax_ready, 1)

            def attend(b):
                dve.wait_ge(attn_ready, b + 1)
                link(vec.reciprocal(rank[:, b % 2, 0:1], smax[:, 1, b % 2:b % 2 + 1]))
                dve.wait_ge(ctxv_done, b + 1)
                vec.scalar_tensor_tensor(out=xres[:, b, :], in0=bank[3][:, 0:D], scalar=rank[:, b % 2, 0:1],
                                         in1=xres[:, b, :], op0=ALU.mult, op1=ALU.add).then_inc(x3_ready, 1)
                dve.wait_ge(x3_ready, b + 1)
                link(vec.bn_stats(bst5[:, b % 2, :], xres[:, b, :]))
                link(vec.bn_aggr(bag5[:, 0, b % 2, :], bst5[:, b % 2, :]))
                vec.tensor_scalar(veps5[:, 0, b % 2:b % 2 + 1], bag5[:, 0, b % 2, 1:2], LN_EPS, None,
                                  ALU.add).then_inc(var4_ready, 1)

            def norm3(b):
                dve.wait_ge(rstd3_ready, b + 1)
                if b >= 2:
                    dve.wait_ge(xn3_turned, b - 1)
                vec.tensor_scalar(xn3[:, b % 2, :], xres[:, b, :], bag2[:, b % 2, 0:1], rstd2[:, b % 2:b % 2 + 1],
                                  ALU.subtract, ALU.mult).then_inc(xn3_ready, 1)

            def norm4(b):
                dve.wait_ge(rstd4_ready, b + 1)
                if b >= 2:
                    dve.wait_ge(xn4_turned, b - 1)
                vec.tensor_scalar(xn4[:, b % 2, :], xres[:, b, :], bag5[:, 0, b % 2, 0:1],
                                  rstd5[:, 0, b % 2:b % 2 + 1], ALU.subtract, ALU.mult).then_inc(xn4_ready, 1)

            for i in range(NB + 5):
                if i < NB:
                    combine(i)
                if 4 <= i < NB + 4:
                    score_max(i - 4)
                if 5 <= i:
                    attend(i - 5)
                if i < NB:
                    norm3(i)
                if 5 <= i:
                    norm4(i - 5)

            dve.wait_ge(biasrow_in, 16)
            base_steps = steps[0]
            PER_GROUP = 2 * G
            PER_BLK = PER_GROUP * NG

            for k in range(2):
                vec.memset(veps5[:, k, :], 0.0).then_inc(yb_ready, 1)
            with dve.Fori(0, NBLK) as blk:
                vec.tensor_copy(w2cur[:, :, :], wT[:, bass.ds(2 * blk + 1, 1), :, :].rearrange("p a c n -> p (a c) n")
                                ).then_inc(w2cur_ready, 1)

                for k, at in ((0, GA), (1, BE)):
                    vec.tensor_copy(affine[:, k, :], cols[:, bass.ds(at + DC * blk, DC)]).then_inc(affine_ready, 1)

                def first_half(g):
                    n = NG * blk + g
                    at = base_steps + PER_GROUP * g + PER_BLK * blk
                    for t in range(G):
                        dve.wait_ge(yf_done, G * n + (t + 1))
                        vec.tensor_tensor(yb[:, (g % 2) * G + t, :], bank[t % 2][:, 0:D],
                                          bias_row[:, bass.ds(blk, 1), :].rearrange("p a d -> p (a d)"),
                                          ALU.add).then_inc(yb_ready, 1)
                        dve.wait_ge(yb_ready, G * n + (t + 3))
                        vec.bn_stats(bst5[:, t, :], yb[:, (g % 2) * G + t, :]).then_inc(dve_step, 1)
                    dve.wait_ge(dve_step, at + G)
                    vec.memset(rstd5[:, g % 2, :], 0.0).then_inc(memset_done, 1)
                    for t in range(G):
                        vec.bn_aggr(bag5[:, g % 2, t, :], bst5[:, t, :]).then_inc(dve_step, 1)
                    dve.wait_ge(dve_step, at + 2 * G)
                    vec.tensor_scalar(veps5[:, g % 2, :], bag5[:, g % 2, :, 1], LN_EPS, None,
                                      ALU.add).then_inc(var5_ready, 1)

                def normalise(g):
                    n = NG * blk + g
                    dve.wait_ge(rstd5_ready, n + 1)
                    for t in range(G):
                        vec.tensor_scalar(zn[:, (g % 2) * G + t, :], yb[:, (g % 2) * G + t, :],
                                          bag5[:, g % 2, t, 0:1], rstd5[:, g % 2, t:t + 1],
                                          ALU.subtract, ALU.mult).then_inc(zn_ready, 1)

                def update(g):
                    n = NG * blk + g
                    for o in range(DC):
                        dve.wait_ge(y2_done, DC * n + (o + 1))
                        h = hT[:, o, g * GT:(g + 1) * GT]
                        vec.scalar_tensor_tensor(out=h, in0=bank[4 + o][:, :],
                                                 scalar=cols[:, bass.ds(BI + DC + 2 * DC * blk + o, 1)], in1=h,
                                                 op0=ALU.add, op1=ALU.add).then_inc(h_ready, 1)

                for g in range(NG):
                    first_half(g)
                    if g >= 1:
                        update(g - 1)
                    normalise(g)
                update(NG - 1)

            for t in range(NB):
                dve.wait_ge(fin_turned, t + 1)
                if t >= 4:
                    dve.wait_ge(out_done, 16 * (t // 4 * 4))
                vec.tensor_tensor(o_sb[:, t % 4, :], bank[6 + t % 2][:, 0:D], xres[:, t, :],
                                  ALU.add).then_inc(fin_ready, 1)

        @block.tensor
        def _(pe):
            mm = pe.matmul

            def turn(dst, src, n=P):
                return pe.transpose(dst, src, ident[0:n, 0:n])

            pe.wait_ge(consts, 8)
            pe.wait_ge(rows_in, 96)
            turn(bank[6][:, 0:NROWS], rows[:, :], NROWS).then_inc(cols_turned, 1)

            def turn_ctx(t):
                pe.wait_ge(ctx_in[t // G], 16)
                if t >= 2:
                    pe.wait_ge(ctx_copied, t - 1)
                for c in range(DC):
                    ins = turn(bank[2 + t % 2][:, c * P:(c + 1) * P], ctx_tok[:, t, c * P:(c + 1) * P])
                ins.then_inc(ctx_turned, 1)

            def turn_x(t):
                pe.wait_ge(xn_ready, t + 1)
                if t >= 2:
                    pe.wait_ge(x_copied, t - 1)
                for c in range(DC):
                    ins = turn(bank[t % 2][:, c * P:(c + 1) * P], xn[:, t % 4, c * P:(c + 1) * P])
                ins.then_inc(x_turned, 1)

            def gates(g):
                pe.wait_ge(x_copied, G * (g + 1))
                pe.wait_ge(ctx_copied, G * (g + 1))
                pe.wait_ge(gkctx_ready, 1)
                if g >= 2:
                    pe.wait_ge(gates_copied, g - 1)
                at = slice(g * GT, (g + 1) * GT)
                dst = bank[4 + g % 2][0:2 * NH, :]
                for c in range(DC):
                    mm(dst, gk_raw[:, c, :], xnT[:, c, at], start=(c == 0), stop=False)
                for c in range(DC):
                    ins = mm(dst, gk_ctx[:, c, :], ctxT[:, c, at], start=False, stop=(c == DC - 1))
                ins.then_inc(gates_done, 1)

            for g in range(NG):
                for t in range(g * G, (g + 1) * G):
                    turn_ctx(t)
                    turn_x(t)
                if g >= 1:
                    gates(g - 1)
            gates(NG - 1)

            def weight(l):
                if l == 0:
                    pe.wait_ge(ffnw_in, 48)
                    pe.wait_ge(cols_ready, 1)
                if l >= 2:
                    pe.wait_ge(lb_copied, l - 1)
                for c in range(DC):
                    ins = turn(bank[6 + l % 2][0:R, c * P:(c + 1) * P], lb_sb[:, l, c, :])
                ins.then_inc(lb_turned, 1)
                pe.wait_ge(wdeq_ready, 2 * l + 2)
                pe.wait_ge(lb_copied, l + 1)
                if l >= 2:
                    pe.wait_ge(wT_copied, l - 1)
                for c in range(DC):
                    at = c * D
                    mm(bank[l % 2][:, at:at + D], la_sb[:, l, c * P:(c + 1) * P], lbT[:, l % 2, :],
                       start=True, stop=True)
                    for o in range(DC):
                        ins = mm(bank[l % 2][:, at + o * P:at + (o + 1) * P], wdeq[:, l % 2, o, c * P:(c + 1) * P],
                                 ident[:, :], start=False, stop=(o == DC - 1), skip_group_check=True)
                ins.then_inc(wT_done, 1)

            weight(0)
            weight(1)
            pe.wait_ge(negmax_ready, 1)
            pe.wait_ge(gates_copied, NG)
            turn(bank[4][:, 0:P], gsc[:, 6, :]).then_inc(glim_turned, 1)
            pe.wait_ge(lim_ready, 1)
            turn(bank[5][:, 0:P], gsc[:, 2, :]).then_inc(glim_turned, 1)
            for l in range(2, NL):
                weight(l)

            def max_rows(u):
                b = u // 2
                pe.wait_ge(negmax_ready, NH)
                if u < 2:
                    pe.wait_ge(wT_copied, NL)
                else:
                    pe.wait_ge(exp_done, HU * (u - 1))
                mm(bank[u % 2][:, :], seq_sel[:, b:b + 1].to_broadcast([P, P]),
                   neg_max[:, HU * (u % 2):HU * (u % 2 + 1), :].rearrange("p h i -> p (h i)"),
                   start=True, stop=True).then_inc(maxb_done, 1)

            def keys_queries(u):
                b = u // 2
                pe.wait_ge(qblk_ready, u + 1)
                if u >= 2:
                    pe.wait_ge(c_ready, u - 1)
                mm(bank[2 + u % 2][:, :], ctxT[:, u % 2, b * P:(b + 1) * P],
                   qblk[:, u % 2, :, :].rearrange("p h i -> p (h i)"),
                   start=True, stop=True).then_inc(qk_done, 1)

            def values(u, heads_of_u):
                b = u // 2
                if heads_of_u[0] == 0:
                    pe.wait_ge(c_ready, u + 1)
                    pe.wait_ge(vaug_ready, b + 1)
                    if b >= 2:
                        pe.wait_ge(yh_ready, b - 1)
                    else:
                        pe.wait_ge(glim_copied, 1)
                for h in heads_of_u:
                    hh = HU * (u % 2) + h
                    ins = mm(bank[4 + b % 2][:, hh * HA:(hh + 1) * HA], cmat[:, u % 2, h, :],
                             v_aug[:, b % 2, hh, :], start=True, stop=True)
                if heads_of_u[-1] == HU - 1:
                    ins.then_inc(cv_done, 1)

            def turn_xn2(b):
                pe.wait_ge(xn2_ready, b + 1)
                if b == 0:
                    pe.wait_ge(lb_copied, NL)
                else:
                    pe.wait_ge(xn2T_copied, b)
                for c in range(DC):
                    ins = turn(bank[6][:, c * P:(c + 1) * P], xn2[:, b % 4, c * P:(c + 1) * P])
                ins.then_inc(xn2_turned, 1)

            def logits(b):
                pe.wait_ge(xn2T_copied, b + 1)
                pe.wait_ge(router_in, 32)
                if b >= 1:
                    pe.wait_ge(logits_read, b)
                if b >= 2:
                    pe.wait_ge(rank_read, 2 * (b - 1))
                for c in range(DC):
                    ins = mm(bank[7][:, 0:E], xn2T[:, b % 2, c, :], router_w[:, c, :],
                             start=(c == 0), stop=(c == DC - 1))
                ins.then_inc(logits_done, 1)

            def ranks(b):
                pe.wait_ge(mask_ready, 2 * b + 1)
                pe.wait_ge(logits_read, min(b + 2, NB))
                if b >= 1:
                    pe.wait_ge(rank_read, 2 * b)
                ins = mm(bank[7][:, 64:64 + E], tri_bf[:, :], mask_bf[:, b % 4, :], start=True, stop=(b == 0))
                if b >= 1:
                    ins = mm(bank[7][:, 64:64 + E], ones_bf[:, :], seen_bf[:, b, :], start=False, stop=True)
                ins.then_inc(rank_done, 1)

            def attn_values(n):
                g, o = n // DC, n % DC
                if n == 0:
                    pe.wait_ge(attnw_in, 32)
                    pe.wait_ge(exp_done, 2 * NB * HU)
                    pe.wait_ge(c_ready, 2 * NB)
                if n >= 4:
                    pe.wait_ge(vT_copied, n - 3)
                for c in range(DC):
                    ins = mm(bank[n % 4][:, :], wv_sb[:, c, o * P:(o + 1) * P], ctxT[:, c, g * GT:(g + 1) * GT],
                             start=(c == 0), stop=(c == DC - 1))
                ins.then_inc(vT_done, 1)

            for i in range(LAST):
                if 5 <= i:
                    ranks(i - 5)
                if i < NB:
                    max_rows(2 * i)
                if 1 <= i <= NB:
                    values(2 * i - 2, (0, 1))
                if 3 <= i < NB + 3:
                    turn_xn2(i - 3)
                if i < NB:
                    keys_queries(2 * i)
                if 1 <= i <= NB:
                    values(2 * i - 2, (2, 3))
                if i < NB:
                    max_rows(2 * i + 1)
                if 1 <= i <= NB:
                    values(2 * i - 1, (0, 1))
                if 3 <= i < NB + 3:
                    logits(i - 3)
                if i < NB:
                    keys_queries(2 * i + 1)
                if 1 <= i <= NB:
                    values(2 * i - 1, (2, 3))
                for n in VT_AT.get(i, ()):
                    attn_values(n)
            pe.wait_ge(vT_copied, NG * DC)
            for b in range(NB):
                if b >= 4:
                    pe.wait_ge(vtok_copied, b - 3)
                for c in range(DC):
                    ins = turn(bank[b % 4][:, c * P:(c + 1) * P], vT[:, c, b * P:(b + 1) * P])
                ins.then_inc(vtok_turned, 1)

            def turn_slots(e, j, first=False):
                pe.wait_ge(xin_in[j], 16 * e - 16 * j + 32)
                for c in range(DC):
                    if first:
                        pe.wait_ge(yh_ready, NB)
                    else:
                        pe.wait_ge(xinT_copied, DC * e - DC + (c + 1))
                    for m in range(MT):
                        n = P if m < MT - 1 else MTAIL
                        ins = turn(bank[4 + c][:, m * P:m * P + n], xin[0:n, j, m, c * P:(c + 1) * P], n)
                    ins.then_inc(xin_turned, 1)

            def hidden(e, j, first=False):
                pe.wait_ge(w1_in[j], 8 * e - 8 * j + 16)
                pe.wait_ge(xinT_copied, DC * e + DC)
                for f in range(FC):
                    if first and f < 4:
                        pe.wait_ge(vtok_copied, NB)
                    else:
                        pe.wait_ge(h_copied, FC * e + f - 3)
                    for c in range(DC):
                        ins = mm(bank[f % 4][:, 0:CAP], w1_sb[:, j, c, f * P:(f + 1) * P], xinT[:, j, c, :],
                                 start=(c == 0), stop=(c == DC - 1))
                    ins.then_inc(h_done, 1)

            def results(e, j, first=False):
                pe.wait_ge(w2_in[j], 8 * e - 8 * j + 16)
                for m in range(MT):
                    n = P if m < MT - 1 else MTAIL
                    if first and m < 2:
                        pe.wait_ge(rank_read, 2 * NB)
                    else:
                        pe.wait_ge(y_ready, MT * e + m - 1)
                    dst = bank[6 + (MT * j + m) % 2][0:n, 0:D]
                    for f in range(FC):
                        if m == 0:
                            pe.wait_ge(h_copied, FC * e + (f + 1))
                        ins = mm(dst, h_moe[j][:, f, m * P:m * P + n], w2_sb[:, j, f, :],
                                 start=(f == 0), stop=(f == FC - 1))
                    ins.then_inc(y_done, 1)

            turn_slots(0, 0, True)
            hidden(0, 0, True)
            turn_slots(1, 1)
            results(0, 0, True)
            hidden(1, 1)
            turn_slots(2, 0)
            results(1, 1)
            with pe.Fori(1, E // 2 - 1) as k:
                for j in range(2):
                    hidden(2 * k + j, j)
                    turn_slots(2 * k + (j + 1), 1 - j)
                    results(2 * k + j, j)
            for e in range(E - 2, E):
                hidden(e, e % 2)
                if e + 1 < E:
                    turn_slots(e + 1, (e + 1) % 2)
                results(e, e % 2)

            def score(b):
                g = b // G
                pe.wait_ge(q_copied, DC * (g + 1))
                if b < 2:
                    pe.wait_ge(h_copied, E * FC)
                else:
                    pe.wait_ge(attn_ready, b - 1)
                for c in range(DC):
                    ins = mm(bank[b % 2][:, 0:P], qT[:, g % 2, c, b % G * P:(b % G + 1) * P],
                             vT[:, c, b * P:(b + 1) * P], start=(c == 0), stop=(c == DC - 1))
                ins.then_inc(score_done, 1)

            for i in range(NB + 6):
                if 4 <= i < NB + 4:
                    score(i - 4)
                if 5 <= i < NB + 5:
                    b = i - 5
                    pe.wait_ge(attnT_copied, b + 1)
                    pe.wait_ge(vtok_copied, NB)
                    if b >= 1:
                        pe.wait_ge(x3_ready, b)
                    mm(bank[3][:, 0:D], attnT[:, b % 2, :], v_tok[:, b, :], start=True, stop=True).then_inc(ctxv_done, 1)
                if i < NB:
                    pe.wait_ge(xn3_ready, i + 1)
                    if i == 0:
                        pe.wait_ge(xinT_copied, E * DC)
                    else:
                        pe.wait_ge(xn3T_copied, i)
                    for c in range(DC):
                        ins = turn(bank[4][:, c * P:(c + 1) * P], xn3[:, i % 2, c * P:(c + 1) * P])
                    ins.then_inc(xn3_turned, 1)
                if i >= 6:
                    b = i - 6
                    pe.wait_ge(xn4_ready, b + 1)
                    if b >= 1:
                        pe.wait_ge(h_ready, b)
                    for c in range(DC):
                        ins = turn(bank[5][:, c * P:(c + 1) * P], xn4[:, b % 2, c * P:(c + 1) * P])
                    ins.then_inc(xn4_turned, 1)
                if 4 <= i < NB + 4:
                    b = i - 4
                    pe.wait_ge(attn_ready, b + 1)
                    if b >= 1:
                        pe.wait_ge(attnT_copied, b)
                    turn(bank[2][:, 0:P], attn[:, b % 2, :]).then_inc(attn_turned, 1)
                if i < NB and i % G == G - 1:
                    g = i // G
                    pe.wait_ge(xn3T_copied, G * (g + 1))
                    for o in range(DC):
                        if g == 0:
                            pe.wait_ge(y_ready, E * MT)
                        else:
                            pe.wait_ge(q_copied, DC * (g - 1) + (o + 1))
                        for c in range(DC):
                            ins = mm(bank[6 + o][:, :], wq_sb[:, c, o * P:(o + 1) * P], xn3T[:, g % 2, c, :],
                                     start=(c == 0), stop=(c == DC - 1))
                        ins.then_inc(q_done, 1)

            pe.wait_ge(attn_ready, NB)
            pe.wait_ge(attnT_copied, NB)
            pe.wait_ge(x3_ready, NB)
            with pe.Fori(0, NBLK) as blk:
                def first(g):
                    n = NG * blk + g
                    pe.wait_ge(h_ready, NB - DC * NG + DC * (n + 1))
                    for t in range(G):
                        pe.wait_ge(yb_ready, G * n + (t + 1))
                        for c in range(DC):
                            ins = mm(bank[t % 2][:, 0:D], hT[:, c, (g * G + t) * P:(g * G + t + 1) * P],
                                     wT[:, bass.ds(2 * blk, 1), c, :].rearrange("p a n -> p (a n)"),
                                     start=(c == 0), stop=(c == DC - 1))
                        ins.then_inc(yf_done, 1)

                def second(g):
                    n = NG * blk + g
                    pe.wait_ge(zn_ready, G * n + G)
                    for c in range(DC):
                        for t in range(G):
                            ins = turn(bank[2 + c][:, t * P:(t + 1) * P], zn[:, (g % 2) * G + t, c * P:(c + 1) * P])
                        ins.then_inc(zn_turned, 1)
                    return n

                def product(g):
                    n = NG * blk + g
                    pe.wait_ge(w2cur_ready, blk + 1)
                    for o in range(DC):
                        pe.wait_ge(h_ready, NB - DC + DC * n + (o + 1))
                        for c in range(DC):
                            if o == 0:
                                pe.wait_ge(a_ready, DC * n + (c + 1))
                            ins = mm(bank[4 + o][:, :], w2cur[:, c, o * P:(o + 1) * P], aT[:, g % 2, c, :],
                                     start=(c == 0), stop=(c == DC - 1))
                        ins.then_inc(y2_done, 1)

                first(0)
                for g in range(NG):
                    if g + 1 < NG:
                        first(g + 1)
                    second(g)
                    product(g)
            for t in range(NB):
                pe.wait_ge(h_ready, NB + DC * NG * (NBLK - 1) + DC * (t // G + 1))
                if t < 2:
                    pe.wait_ge(q_copied, NG * DC)
                else:
                    pe.wait_ge(fin_ready, t - 1)
                for c in range(DC):
                    ins = turn(bank[6 + t % 2][:, c * P:(c + 1) * P], hT[:, c, t * P:(t + 1) * P])
                ins.then_inc(fin_turned, 1)


_INS = ["x", "ctx_1024", "L0_xattn_igate_kernel", "L0_xattn_igate_bias", "L0_xattn_fgate_kernel",
        "L0_xattn_fgate_bias", "L0_ffn_gate_w", "L0_ffn_gate_b", "L0_ffn_w1", "L0_ffn_b1", "L0_ffn_w2",
        "L0_ffn_b2", "L1_xattn_Wq", "L1_xattn_bq", "L1_xattn_Wv", "L1_xattn_bv", "L1_ffn_qweights",
        "L1_ffn_scales", "L1_ffn_biases", "L1_ffn_lora_a", "L1_ffn_lora_b", "L1_ffn_ln_gamma",
        "L1_ffn_ln_beta"]


def kernel(**inputs):
    import numpy as np
    import concourse.bacc as bacc
    from concourse.bass_utils import run_bass_kernel_spmd

    nc = bacc.Bacc("TRN2", target_bir_lowering=False, num_devices=1)
    arrays, args = {}, []
    for name in _INS:
        a = np.ascontiguousarray(inputs[name])
        arrays[f"in_{name}"] = a
        args.append(nc.dram_tensor(f"in_{name}", a.shape, mybir.dt.from_np(a.dtype), kind="ExternalInput").ap())
    out = nc.dram_tensor("out_x", tuple(inputs["x"].shape), F32, kind="ExternalOutput").ap()
    mega_kernel(nc, *args, out)
    r = run_bass_kernel_spmd(nc, [arrays], core_ids=[0])
    return r.results[0]["out_x"]
```

```python
from contextlib import ExitStack

import concourse.bass as bass
from concourse import mybir

P = 128
ALU = mybir.AluOpType
ACT = mybir.ActivationFunctionType
AX = mybir.AxisListType
F32 = mybir.dt.float32
F32R = mybir.dt.float32r
BF16 = mybir.dt.bfloat16
I32 = mybir.dt.int32
U32 = mybir.dt.uint32

CAP_FACTOR, TOP_K, LEVELS, GROUP = 1.25, 2, 7.5, 16
LN_EPS, HEAD_EPS = 1e-5, 1e-6
LOWEST = -3.0e38
DROPPED = 1.0e6
MASKED = -1.0e30


def mega_kernel(nc, x, ctx, igate_kernel, igate_bias, fgate_kernel, fgate_bias, gate_w, gate_b,
                w1, b1, w2, b2, Wq, bq, Wv, bv, qweights, scales, biases, lora_a, lora_b,
                ln_gamma, ln_beta, out):
    NB, S, D = x.shape
    NH = igate_kernel.shape[1]
    HD = D // NH
    E, _, FF = w1.shape
    NL, _, _ = qweights.shape
    NBLK = NL // 2
    R = lora_a.shape[1]
    T = NB * S
    DC, FC = D // P, FF // P
    CAP = int(CAP_FACTOR * T / E)
    SLOTS = E * CAP
    G = 4
    NG = NB // G
    GT = G * P
    HU = NH // 2
    HA = HD + 1
    MT = -(-CAP // P)
    MTAIL = CAP - (MT - 1) * P
    NS = D // GROUP
    assert S == P and NH * NB == P and DC == 2 and HU * HD == P and SLOTS % P == 0

    with ExitStack() as stack:
        def sb(name, shape, dt=F32):
            return stack.enter_context(nc.sbuf_tensor(name, shape, dt))

        def sem(name):
            return stack.enter_context(nc.semaphore(name))

        gates_dram = nc.dram_tensor("gates_dram", (2 * NH, T), F32).ap()
        slots_dram = nc.dram_tensor("slots_dram", (SLOTS, D), F32).ap()
        experts_dram = nc.dram_tensor("experts_dram", (SLOTS, D), F32).ap()

        xres = sb("xres", [P, NB, D])
        ctx_tok = sb("ctx_tok", [P, NB, D])
        v_tok = ctx_tok
        ctxT = sb("ctxT", [P, DC, T])
        xnT = sb("xnT", [P, DC, T])
        hT = xnT
        vT = sb("vT", [P, DC, T])

        wT = sb("wT", [P, NL, DC, D])
        w1_sb = sb("w1_sb", [P, 2, DC, FF])
        w2_sb = sb("w2_sb", [P, 2, FC, D])
        b2_row = sb("b2_row", [P, E, D])
        gk_raw = sb("gk_raw", [P, 3 * DC, 2 * NH])
        gk_ctx = sb("gk_ctx", [P, DC, 2 * NH])
        gate_bias = sb("gate_bias", [2 * NH, 1])
        router_w = sb("router_w", [P, DC, E])
        router_b = sb("router_b", [P, E])
        wq_sb = sb("wq_sb", [P, DC, D])
        wv_sb = sb("wv_sb", [P, DC, D])
        bias_row = sb("bias_row", [P, NBLK, D])
        scale_sb = sb("scale_sb", [P, NL, DC, NS])
        la_sb = sb("la_sb", [R, NL, D])
        lb_sb = sb("lb_sb", [P, NL, DC, R])
        lbT = sb("lbT", [R, 2, D])
        B1, GA, BE, BI, BQ, BV = 0, E * FC, E * FC + NBLK * DC, E * FC + 2 * NBLK * DC, \
            E * FC + (2 * NBLK + NL) * DC, E * FC + (2 * NBLK + NL) * DC + DC
        NROWS = BV + DC
        rows = sb("rows", [NROWS, P])
        cols = sb("cols", [P, NROWS])

        ident = sb("ident", [P, P])
        ones = sb("ones", [P, P])
        tri_bf = sb("tri_bf", [P, P], BF16)
        ones_bf = sb("ones_bf", [P, P], BF16)
        ident_bf = sb("ident_bf", [P, P], BF16)
        causal_bf = sb("causal_bf", [P, HU, P], BF16)
        seq_sel_f = sb("seq_sel_f", [P, NB])
        seq_sel = sb("seq_sel", [P, NB], F32R)
        head_sel = sb("head_sel", [P, NH])
        expert_no_i = sb("expert_no_i", [P, E], I32)
        expert_no = sb("expert_no", [P, E])
        mhalf = sb("mhalf", [P, 16])
        zero_row = sb("zero_row", [P, D])

        bst = sb("bst", [P, NB, 6])
        bag = sb("bag", [P, NB, 2])
        veps = sb("veps", [P, NB])
        rstd = sb("rstd", [P, NB])
        bst2 = sb("bst2", [P, 2, 6])
        bag2 = sb("bag2", [P, 2, 2])
        veps2 = sb("veps2", [P, 2])
        rstd2 = sb("rstd2", [P, 2])
        gates_xn2 = sb("gates_xn2", [P, T])
        gates_sb = gates_xn2[0:2 * NH, :]
        gT = sb("gT", [P, P])
        limT = sb("limT", [P, P])
        neg_hi = sb("neg_hi", [P, NH, P], F32R)
        neg_lo = sb("neg_lo", [P, NH, P], F32R)

        scratch = sb("scratch", [P, 8 * GT])

        def view(buf, at, *shape):
            n = 1
            for s in shape:
                n *= s
            flat = buf[:, at:at + n]
            if len(shape) == 1:
                return flat
            names = "abcd"[:len(shape)]
            return flat.rearrange(f"p ({' '.join(names)}) -> p {' '.join(names)}",
                                  **dict(zip(names, shape)))

        decay = view(scratch, 0, 2, HU, P)
        cmat = view(scratch, 2 * GT, 2, HU, P)
        qblk = view(scratch, 4 * GT, 4, HU, P)
        xn = view(scratch, 6 * GT, 4, D)
        neg_max = view(scratch, 0, NH, P)
        xn2 = view(gates_xn2, 0, 8, D)
        work = sb("work", [P, 8 * D])
        v_aug = sb("v_aug", [P, 2, NH, HA])
        sq = view(work, 0, NH, HD)
        yh = view(work, D, NH, HD)
        xn2T = view(work, 2 * D, 2, DC, P)
        heads_out = view(work, 4 * D, 2, NH, HA)
        gsc = sb("gsc", [P, 8, P])
        wraw = view(work.bitcast(I32), 0, 2, DC, D)
        wdeq = view(work, 4 * D, 2, DC, D)
        small = sb("small", [P, 8, NH])
        lg = sb("lg", [P, 2, E])
        top_v = sb("top_v", [P, NB, 8])
        top_i = sb("top_i", [P, NB, 8], U32)
        topi = sb("topi", [P, NB, 2])
        pick = sb("pick", [P, 2, 2, 2, E])
        picked = sb("picked", [P, 2, 2, E])
        mask_bf = sb("mask_bf", [P, 2, 2, E], BF16)
        seen_bf = sb("seen_bf", [P, NB + 1, E], BF16)
        rank = sb("rank", [P, 2, 2])
        over = sb("over", [P, 2, 2])
        base = sb("base", [P, 2, 2])
        kept = sb("kept", [P, NB, 2])
        dest = sb("dest", [P, NB, 2], U32)
        wtop = sb("wtop", [P, NB, 2])
        xin = view(scratch, 0, 2, MT, D)
        xinT = view(scratch, 2 * MT * D, 2, DC, CAP)
        y_sb = view(work, 0, 2, MT, D)
        h_moe = [view(xnT.rearrange("p c t -> p (c t)"), 0, FC, CAP),
                 view(ctxT.rearrange("p c t -> p (c t)"), 0, FC, CAP)]
        gath = view(scratch, 2 * MT * D + 2 * DC * CAP, 2, 2, D)
        ctx_flat = ctxT.rearrange("p c t -> p (c t)")
        xn3T = view(ctx_flat, 0, 2, DC, GT)
        qT = view(ctx_flat, 4 * GT, 2, DC, GT)
        xn3 = view(scratch, 0, 2, D)
        attn = view(scratch, 2 * D, 2, P)
        attnT = view(scratch, 3 * D, 2, P)
        xn4 = view(scratch, 4 * D, 2, D)
        smax = sb("smax", [P, 2, 2])
        b1_cur = sb("b1_cur", [P, 2, FC])
        affine = sb("affine", [P, 2, DC])
        w1_flat = w1_sb.rearrange("p a c f -> p (a c f)")
        yb = view(w1_flat, 0, 2 * G, D)
        zn = view(w1_flat, 2 * G * D, 2 * G, D)
        w2_flat = w2_sb.rearrange("p a c f -> p (a c f)")
        aT = view(w2_flat, 0, 2, DC, GT)
        w2cur = view(w2_flat, 4 * GT, DC, D)
        bst5 = sb("bst5", [P, G, 6])
        bag5 = sb("bag5", [P, 2, G, 2])
        veps5 = sb("veps5", [P, 2, G])
        rstd5 = sb("rstd5", [P, 2, G])
        o_sb = view(work, 0, 4, D)

        bank = [stack.enter_context(nc.psum_tensor(f"bank{i}", [P, 512], F32)) for i in range(8)]

        x_in = [sem(f"x_in{g}") for g in range(NG)]
        ctx_in = [sem(f"ctx_in{g}") for g in range(NG)]
        gk_in, rows_in, router_in, attnw_in, ffnw_in, b2_in, biasrow_in = (
            sem(n) for n in ("gk_in", "rows_in", "router_in", "attnw_in", "ffnw_in", "b2_in", "biasrow_in"))
        q_in = [sem(f"q_in{j}") for j in range(2)]
        w1_in = [sem(f"w1_in{j}") for j in range(2)]
        w2_in = [sem(f"w2_in{j}") for j in range(2)]
        slots_zeroed = sem("slots_zeroed")
        gates_out, gates_back = sem("gates_out"), sem("gates_back")
        xin_in = [sem(f"xin_in{j}") for j in range(2)]
        y_out = [sem(f"y_out{j}") for j in range(2)]
        scattered = [sem(f"scattered{j}") for j in range(8)]
        gathered = [sem(f"gathered{j}") for j in range(2)]
        out_done = sem("out_done")
        consts = sem("consts")
        pool_step, dve_step = sem("pool_step"), sem("dve_step")
        dve_consts, cols_turned, cols_ready = sem("dve_consts"), sem("cols_turned"), sem("cols_ready")
        xvar_ready, xrstd_ready, xn_ready = sem("xvar_ready"), sem("xrstd_ready"), sem("xn_ready")
        x_turned, x_copied = sem("x_turned"), sem("x_copied")
        ctx_turned, ctx_copied = sem("ctx_turned"), sem("ctx_copied")
        gkctx_ready, gates_done, gates_copied = sem("gkctx_ready"), sem("gates_done"), sem("gates_copied")
        fabs_ready, fexp_ready, fln_ready, gsum_ready, lim_ready = (
            sem(n) for n in ("fabs_ready", "fexp_ready", "fln_ready", "gsum_ready", "lim_ready"))
        negmax_ready, glim_turned, glim_copied = sem("negmax_ready"), sem("glim_turned"), sem("glim_copied")
        lb_turned, lb_copied, wdeq_ready, wT_done, wT_copied = (
            sem(n) for n in ("lb_turned", "lb_copied", "wdeq_ready", "wT_done", "wT_copied"))
        vT_done, vT_copied = sem("vT_done"), sem("vT_copied")
        qblk_ready, vaug_ready = [sem("qblk_even"), sem("qblk_odd")], sem("vaug_ready")
        maxb_done, qk_done, exp_done, qblk_zeroed, c_ready, cv_done, heads_copied = (
            sem(n) for n in ("maxb_done", "qk_done", "exp_done", "qblk_zeroed", "c_ready", "cv_done", "heads_copied"))
        sq_ready, ms_ready, rms_ready, yh_ready, var2_ready, rstd2_ready, xn2_ready = (
            sem(n) for n in ("sq_ready", "ms_ready", "rms_ready", "yh_ready", "var2_ready", "rstd2_ready", "xn2_ready"))
        xn2_turned, xn2T_copied, logits_done, logits_read, mask_ready, rank_done, rank_read, dest_ready = (
            sem(n) for n in ("xn2_turned", "xn2T_copied", "logits_done", "logits_read", "mask_ready",
                             "rank_done", "rank_read", "dest_ready"))
        topdiff_ready, topexp_ready = sem("topdiff_ready"), sem("topexp_ready")
        vtok_turned, vtok_copied = sem("vtok_turned"), sem("vtok_copied")
        xin_turned, xinT_copied, h_done, h_copied, y_done, y_ready = (
            sem(n) for n in ("xin_turned", "xinT_copied", "h_done", "h_copied", "y_done", "y_ready"))
        gath_zeroed, x2_ready = sem("gath_zeroed"), sem("x2_ready")
        var3_ready, rstd3_ready, xn3_ready, xn3_turned, xn3T_copied, q_done, q_copied = (
            sem(n) for n in ("var3_ready", "rstd3_ready", "xn3_ready", "xn3_turned", "xn3T_copied", "q_done", "q_copied"))
        score_done, smax_ready, attn_ready, attn_turned, attnT_copied, ctxv_done = (
            sem(n) for n in ("score_done", "smax_ready", "attn_ready", "attn_turned", "attnT_copied", "ctxv_done"))
        x3_ready, var4_ready, rstd4_ready, xn4_ready, xn4_turned, h_ready = (
            sem(n) for n in ("x3_ready", "var4_ready", "rstd4_ready", "xn4_ready", "xn4_turned", "h_ready"))
        w2cur_ready, yf_done, yb_ready, var5_ready, rstd5_ready, zn_ready, zn_turned, a_ready, y2_done, _unused = (
            sem(n) for n in ("w2cur_ready", "yf_done", "yb_ready", "var5_ready", "rstd5_ready", "zn_ready",
                             "zn_turned", "a_ready", "y2_done", "unused"))
        b1_ready, affine_ready, memset_done = sem("b1_ready"), sem("affine_ready"), sem("memset_done")
        fin_turned, fin_ready = sem("fin_turned"), sem("fin_ready")

        LAST = NB + 8
        VT_AT = {NB + 1: (0, 1), NB + 2: (2, 3), NB + 3: (4, 5), NB + 4: (6, 7)}
        VTOK_AT = {NB + 4: (0, 1, 2, 3), NB + 5: (4, 5, 6, 7), NB + 6: (8, 9, 10, 11), NB + 7: (12, 13, 14, 15)}
        assert sum(len(v) for v in VT_AT.values()) == NG * DC
        assert sum(len(v) for v in VTOK_AT.values()) == NB
        block = stack.enter_context(nc.Block())

        @block.sync
        def _(sp):
            xv = x.rearrange("t p d -> p t d")
            cv = ctx.rearrange("t p d -> p t d")
            for g in range(NG):
                sp.dma_start(xres[:, g * G:(g + 1) * G, :], xv[:, g * G:(g + 1) * G, :]).then_inc(x_in[g], 16)
                sp.dma_start(ctx_tok[:, g * G:(g + 1) * G, :], cv[:, g * G:(g + 1) * G, :]).then_inc(ctx_in[g], 16)
            sp.dma_start(la_sb[:, :, :], lora_a.rearrange("l r d -> r l d")).then_inc(ffnw_in, 16)
            sp.dma_start(lb_sb[:, :, :, :].rearrange("p l c r -> p (l c) r"),
                         lora_b.rearrange("l (c p) r -> p (l c) r", p=P)).then_inc(ffnw_in, 16)
            sp.dma_start(scale_sb[:, :, :, :].rearrange("p l c s -> p (l c) s"),
                         scales.rearrange("l (c p) s -> p (l c) s", p=P)).then_inc(ffnw_in, 16)
            def load_quantised(l):
                if l >= 2:
                    sp.wait_ge(wdeq_ready, 2 * (l - 2) + 1)
                sp.dma_start(wraw[:, l % 2, :, :],
                             qweights[l].rearrange("(c p) d -> p c d", p=P)).then_inc(q_in[l % 2], 16)

            for l in range(4):
                load_quantised(l)
            sp.wait_ge(gates_copied, NG)
            sp.dma_start(gates_dram, gates_sb[:, :]).then_inc(gates_out, 16)
            sp.wait_ge(gates_out, 16)
            gview = gates_dram.rearrange("(k h) (b s) -> k (h b) s", k=2, s=P)
            sp.dma_start(gsc[:, 0, :], gview[0]).then_inc(gates_back, 16)
            sp.dma_start(gsc[:, 1, :], gview[1]).then_inc(gates_back, 16)
            for l in range(4, NL):
                load_quantised(l)
            for e in range(2):
                sp.dma_start(w1_sb[:, e, :, :], w1[e].rearrange("(c p) f -> p c f", p=P)).then_inc(w1_in[e], 16)
                sp.dma_start(w2_sb[:, e, :, :], w2[e].rearrange("(c p) d -> p c d", p=P)).then_inc(w2_in[e], 16)

            def load_slots(e, j):
                rows_e = slots_dram[bass.ds(e * CAP, CAP), :]
                sp.dma_start(xin[:, j, 0:MT - 1, :],
                             rows_e[0:(MT - 1) * P, :].rearrange("(m p) d -> p m d", p=P)).then_inc(xin_in[j], 16)
                sp.dma_start(xin[0:MTAIL, j, MT - 1, :], rows_e[(MT - 1) * P:CAP, :]).then_inc(xin_in[j], 16)

            def store_rows(e, j):
                rows_e = experts_dram[bass.ds(e * CAP, CAP), :]
                sp.wait_ge(y_ready, MT * e + MT)
                sp.dma_start(rows_e[0:(MT - 1) * P, :].rearrange("(m p) d -> p m d", p=P),
                             y_sb[:, j, 0:MT - 1, :]).then_inc(y_out[j], 16)
                sp.dma_start(rows_e[(MT - 1) * P:CAP, :], y_sb[0:MTAIL, j, MT - 1, :]).then_inc(y_out[j], 16)

            for j in range(8):
                sp.wait_ge(scattered[j], 32 * (NB // 8))
            for e in range(2):
                load_slots(e, e)
            with sp.Fori(0, E // 2 - 1) as k:
                for j in range(2):
                    e = 2 * k + j
                    sp.wait_ge(xin_turned, DC * e + DC)
                    load_slots(e + 2, j)
                    sp.wait_ge(h_done, FC * e + FC)
                    sp.dma_start(w1_sb[:, j, :, :],
                                 w1[bass.ds(e + 2, 1)].rearrange("a (c p) f -> p (a c) f", p=P)).then_inc(w1_in[j], 16)
                    sp.wait_ge(y_done, MT * e + MT)
                    sp.dma_start(w2_sb[:, j, :, :],
                                 w2[bass.ds(e + 2, 1)].rearrange("a (c p) d -> p (a c) d", p=P)).then_inc(w2_in[j], 16)
                    store_rows(e, j)
            for e in range(E - 2, E):
                store_rows(e, e % 2)
            ov = out.rearrange("t p d -> p t d")
            for t in range(NB):
                sp.wait_ge(fin_ready, t + 1)
                sp.dma_start(ov[:, t, :], o_sb[:, t % 4, :]).then_inc(out_done, 16)
                if t % 4 == 3:
                    sp.wait_ge(out_done, 16 * (t + 1))

        @block.gpsimd
        def _(pool):
            steps = [0]

            def link(ins):
                steps[0] += 1
                ins.then_inc(pool_step, 1)
                pool.wait_ge(pool_step, steps[0])

            pool.memset(ident[:, :], 0.0).then_inc(pool_step, 1)
            pool.memset(tri_bf[:, :], 1.0).then_inc(pool_step, 1)
            steps[0] += 2
            pool.wait_ge(pool_step, 2)
            pool.affine_select(out=ident[:, :], in_=ident[:, :], compare_op=ALU.not_equal, fill=1.0,
                               base=0, pattern=[[-1, P]], channel_multiplier=1).then_inc(consts, 1)
            pool.memset(zero_row[:, :], 0.0).then_inc(consts, 1)
            pool.wait_ge(consts, 2)
            pool.dma_start(slots_dram.rearrange("(p r) d -> p r d", p=P),
                           zero_row[:, :].unsqueeze(1).to_broadcast([P, SLOTS // P, D])).then_inc(slots_zeroed, 16)
            pool.memset(mhalf[:, :], -0.5).then_inc(consts, 1)
            pool.affine_select(out=tri_bf[:, :], in_=tri_bf[:, :], compare_op=ALU.is_ge, fill=0.0,
                               base=0, pattern=[[1, P]], channel_multiplier=-1).then_inc(consts, 1)
            pool.memset(ones_bf[:, :], 1.0).then_inc(consts, 1)
            pool.memset(ones[:, :], 1.0).then_inc(consts, 1)
            pool.memset(v_aug[:, :, :, :], 1.0).then_inc(consts, 1)
            pool.iota(expert_no_i[:, :], pattern=[[1, E]], base=0, channel_multiplier=0).then_inc(consts, 1)
            pool.memset(causal_bf[:, :, :], 0.0).then_inc(consts, 1)
            pool.memset(ident_bf[:, :], 0.0).then_inc(consts, 1)
            pool.wait_ge(consts, 10)
            pool.affine_select(out=causal_bf[:, :, :], in_=causal_bf[:, :, :], compare_op=ALU.is_ge, fill=MASKED,
                               base=0, pattern=[[0, HU], [1, P]], channel_multiplier=-1).then_inc(consts, 1)
            pool.affine_select(out=ident_bf[:, :], in_=ident_bf[:, :], compare_op=ALU.not_equal, fill=1.0,
                               base=0, pattern=[[-1, P]], channel_multiplier=1).then_inc(consts, 1)
            for g in range(NG):
                pool.wait_ge(xvar_ready, g + 1)
                pool.tensor_tensor(rstd[:, g * G:(g + 1) * G], veps[:, g * G:(g + 1) * G],
                                   mhalf[:, 0:G], ALU.pow).then_inc(xrstd_ready, 1)

            pool.wait_ge(slots_zeroed, 16)

            def head_rms(b):
                pool.wait_ge(ms_ready, b + 1)
                pool.tensor_tensor(small[:, 4 + b % 2, :], small[:, 2 + b % 2, :], mhalf[:, 0:NH],
                                   ALU.pow).then_inc(rms_ready, 1)

            def norm2(b):
                pool.wait_ge(var2_ready, b + 1)
                pool.tensor_tensor(rstd2[:, b % 2:b % 2 + 1], veps2[:, b % 2:b % 2 + 1], mhalf[:, 0:1],
                                   ALU.pow).then_inc(rstd2_ready, 1)

            def scatter(b):
                pool.wait_ge(dest_ready, b // 2 + 1)
                for k in range(TOP_K):
                    pool.indirect_dma_start(
                        out=slots_dram[:, :],
                        out_offset=bass.IndirectOffsetOnAxis(ap=dest[:, b, k:k + 1], axis=0),
                        in_=xn2[:, b % 8, :], in_offset=None,
                        bounds_check=SLOTS - 1, oob_is_err=False).then_inc(scattered[b % 8], 16)

            for i in range(LAST):
                if 2 <= i < NB + 2:
                    head_rms(i - 2)
                if 3 <= i < NB + 3:
                    norm2(i - 3)
                if 8 <= i:
                    scatter(i - 8)

            pool.wait_ge(gath_zeroed, 1)
            for j in range(2):
                pool.wait_ge(y_out[j], 32 * (E // 2))

            def gather(b):
                if b >= 2:
                    pool.wait_ge(x2_ready, b - 1)
                for k in range(TOP_K):
                    pool.indirect_dma_start(
                        out=gath[:, b % 2, k, :], out_offset=None, in_=experts_dram[:, :],
                        in_offset=bass.IndirectOffsetOnAxis(ap=dest[:, b, k:k + 1], axis=0),
                        bounds_check=SLOTS - 1, oob_is_err=False).then_inc(gathered[b % 2], 16)

            gather(0)
            for i in range(NB + 5):
                if i + 1 < NB:
                    gather(i + 1)
                if i < NB:
                    pool.wait_ge(var3_ready, i + 1)
                    pool.tensor_tensor(rstd2[:, i % 2:i % 2 + 1], veps2[:, i % 2:i % 2 + 1],
                                       mhalf[:, 0:1], ALU.pow).then_inc(rstd3_ready, 1)
                if i >= 5:
                    pool.wait_ge(var4_ready, i - 4)
                    pool.tensor_tensor(rstd5[:, 0, (i - 5) % 2:(i - 5) % 2 + 1],
                                       veps5[:, 0, (i - 5) % 2:(i - 5) % 2 + 1],
                                       mhalf[:, 0:1], ALU.pow).then_inc(rstd4_ready, 1)
            with pool.Fori(0, NBLK) as blk:
                for g in range(NG):
                    pool.wait_ge(var5_ready, NG * blk + (g + 1))
                    pool.tensor_tensor(rstd5[:, g % 2, :], veps5[:, g % 2, :], mhalf[:, 0:G],
                                       ALU.pow).then_inc(rstd5_ready, 1)

        @block.scalar
        def _(act):
            act.dma_start(gk_raw[:, :, 0:NH], igate_kernel.rearrange("(c p) h -> p c h", p=P)).then_inc(gk_in, 16)
            act.dma_start(gk_raw[:, :, NH:2 * NH], fgate_kernel.rearrange("(c p) h -> p c h", p=P)).then_inc(gk_in, 16)
            act.dma_start(gate_bias[0:NH, :], igate_bias.unsqueeze(1)).then_inc(gk_in, 16)
            act.dma_start(gate_bias[NH:2 * NH, :], fgate_bias.unsqueeze(1)).then_inc(gk_in, 16)
            for at, src in ((B1, b1), (GA, ln_gamma), (BE, ln_beta), (BI, biases)):
                n = src.shape[0] * src.shape[1] // P
                act.dma_start(rows[at:at + n, :], src.rearrange("n (c p) -> (n c) p", p=P)).then_inc(rows_in, 16)
            act.dma_start(rows[BQ:BQ + DC, :], bq.rearrange("(c p) -> c p", p=P)).then_inc(rows_in, 16)
            act.dma_start(rows[BV:BV + DC, :], bv.rearrange("(c p) -> c p", p=P)).then_inc(rows_in, 16)
            act.dma_start(router_w[:, :, :], gate_w.rearrange("(c p) e -> p c e", p=P)).then_inc(router_in, 16)
            act.dma_start(router_b[:, :], gate_b.partition_broadcast(P)).then_inc(router_in, 16)
            act.dma_start(wq_sb[:, :, :], Wq.rearrange("(c p) n -> p c n", p=P)).then_inc(attnw_in, 16)
            act.dma_start(wv_sb[:, :, :], Wv.rearrange("(c p) n -> p c n", p=P)).then_inc(attnw_in, 16)
            act.dma_start(b2_row[:, :, :], b2.partition_broadcast(P)).then_inc(b2_in, 16)
            act.dma_start(bias_row[:, :, :],
                          biases.rearrange("(n two) d -> n two d", two=2)[:, 0, :].partition_broadcast(P)
                          ).then_inc(biasrow_in, 16)

            def copy_ctx(t):
                act.wait_ge(ctx_turned, t + 1)
                nc.scalar.copy(ctxT[:, :, t * P:(t + 1) * P],
                               bank[2 + t % 2][:, 0:D].rearrange("p (c s) -> p c s", c=DC)).then_inc(ctx_copied, 1)

            def copy_gates(g):
                act.wait_ge(gates_done, g + 1)
                act.wait_ge(gk_in, 64)
                nc.scalar.activation(gates_sb[:, g * GT:(g + 1) * GT], bank[4 + g % 2][0:2 * NH, :],
                                     ACT.Identity, bias=gate_bias[:, 0:1]).then_inc(gates_copied, 1)

            for t in range(NB):
                copy_ctx(t)
                if t % G == G - 1 and t > G:
                    copy_gates(t // G - 1)
            copy_gates(NG - 1)
            act.wait_ge(fabs_ready, 1)
            nc.scalar.activation(gsc[:, 3, :], gsc[:, 2, :], ACT.Exp).then_inc(fexp_ready, 1)
            act.wait_ge(fexp_ready, 1)
            nc.scalar.activation(gsc[:, 4, :], gsc[:, 3, :], ACT.Ln, bias=1.0).then_inc(fln_ready, 1)
            act.wait_ge(gsum_ready, 1)
            nc.scalar.activation(gsc[:, 2, :], gsc[:, 7, :], ACT.Exp, scale=-1.0).then_inc(lim_ready, 1)

            def v_with_ones(b):
                if b >= 2:
                    act.wait_ge(cv_done, 2 * (b - 1))
                act.wait_ge(consts, 12)
                nc.scalar.copy(v_aug[:, b % 2, :, 0:HD],
                               ctx_tok[:, b, :].rearrange("p (h d) -> p h d", h=NH)).then_inc(vaug_ready, 1)

            def query_blocks(u):
                b, c = u // 2, u % 2
                if u >= 4:
                    act.wait_ge(qk_done, u - 3)
                elif u == 0:
                    act.wait_ge(qblk_zeroed, 2)
                    act.wait_ge(x_copied, NB)
                for h in range(HU):
                    ins = nc.scalar.mul(qblk[h * HD:(h + 1) * HD, u % 4, h, :],
                                        xnT[h * HD:(h + 1) * HD, c, b * P:(b + 1) * P], float(HD) ** -0.5)
                ins.then_inc(qblk_ready[0], 1)

            v_with_ones(0)
            query_blocks(0)
            for l in range(NL):
                act.wait_ge(wT_done, l + 1)
                nc.scalar.copy(wT[:, l, :, :], bank[l % 2][:, :].rearrange("p (c n) -> p c n", c=DC)).then_inc(wT_copied, 1)

            def decays(u):
                b = u // 2
                act.wait_ge(maxb_done, u + 1)
                act.wait_ge(glim_copied, 1)
                if u >= 2:
                    act.wait_ge(c_ready, u - 1)
                for h in range(HU):
                    col = (HU * (u % 2) + h) * NB + b
                    nc.scalar.activation(decay[:, u % 2, h, :], bank[u % 2][:, h * P:(h + 1) * P], ACT.Exp,
                                         bias=gT[:, col:col + 1]).then_inc(exp_done, 1)

            def heads_from_psum(b):
                act.wait_ge(cv_done, 2 * b + 2)
                if b >= 2:
                    act.wait_ge(yh_ready, b - 1)
                nc.scalar.copy(heads_out[:, b % 2, :, :],
                               bank[4 + b % 2][:, 0:NH * HA].rearrange("p (h d) -> p h d", h=NH)).then_inc(heads_copied, 1)
                act.wait_ge(heads_copied, b + 1)
                if b >= 1:
                    act.wait_ge(ms_ready, b)
                nc.scalar.activation(sq[:, :, :], heads_out[:, b % 2, :, 0:HD], ACT.Square,
                                     scale=float(HD) ** -0.5).then_inc(sq_ready, 1)

            def copy_xn2T(b):
                act.wait_ge(xn2_turned, b + 1)
                if b >= 2:
                    act.wait_ge(logits_done, b - 1)
                nc.scalar.copy(xn2T[:, b % 2, :, :], bank[6][:, 0:D].rearrange("p (c s) -> p c s", c=DC)).then_inc(xn2T_copied, 1)

            def copy_vT(n):
                g, o = n // DC, n % DC
                act.wait_ge(vT_done, n + 1)
                act.wait_ge(cols_ready, 1)
                nc.scalar.activation(vT[:, o, g * GT:(g + 1) * GT], bank[n % 4][:, :], ACT.Identity,
                                     bias=cols[:, BV + o:BV + o + 1]).then_inc(vT_copied, 1)

            def copy_vtok(b):
                act.wait_ge(vtok_turned, b + 1)
                nc.scalar.copy(v_tok[:, b, :], bank[4 + b % 2][:, 0:D]).then_inc(vtok_copied, 1)

            for i in range(LAST):
                if i < NB:
                    decays(2 * i)
                if 2 <= i < NB + 2:
                    heads_from_psum(i - 2)
                if i + 1 < NB:
                    query_blocks(2 * i + 2)
                if i < NB:
                    decays(2 * i + 1)
                if 4 <= i < NB + 4:
                    copy_xn2T(i - 4)
                if i + 1 < NB:
                    v_with_ones(i + 1)
                for n in VT_AT.get(i - 1, ()):
                    copy_vT(n)
                for b in VTOK_AT.get(i - 1, ()):
                    copy_vtok(b)
            for b in VTOK_AT[LAST - 1]:
                copy_vtok(b)
            act.wait_ge(topdiff_ready, 1)
            nc.scalar.activation(wtop[:, :, 0], wtop[:, :, 1], ACT.Exp).then_inc(topexp_ready, 1)

            def hidden(e, j):
                if not isinstance(e, int) or e >= 2:
                    act.wait_ge(y_done, MT * e - MT)
                act.wait_ge(b1_ready, e + 1)
                for f in range(FC):
                    act.wait_ge(h_done, FC * e + (f + 1))
                    nc.scalar.activation(h_moe[j][:, f, :], bank[f % 4][:, 0:CAP], ACT.Relu,
                                         bias=b1_cur[:, j, f:f + 1]).then_inc(h_copied, 1)

            for e in range(2):
                hidden(e, e)
            with act.Fori(1, E // 2) as k:
                for j in range(2):
                    hidden(2 * k + j, j)

            for i in range(NB + 6):
                if 4 <= i < NB + 4:
                    b = i - 4
                    act.wait_ge(smax_ready, b + 1)
                    if b >= 2:
                        act.wait_ge(attn_turned, b - 1)
                    nc.scalar.activation(attn[:, b % 2, :], bank[b % 2][:, 0:P], ACT.Exp,
                                         bias=smax[:, 0, b % 2:b % 2 + 1],
                                         accum_out=smax[:, 1, b % 2:b % 2 + 1]).then_inc(attn_ready, 1)
                if i < NB:
                    act.wait_ge(xn3_turned, i + 1)
                    if i % G == 0 and i >= 2 * G:
                        act.wait_ge(q_done, DC * (i // G - 1))
                    nc.scalar.copy(xn3T[:, i // G % 2, :, i % G * P:(i % G + 1) * P],
                                   bank[4][:, 0:D].rearrange("p (c s) -> p c s", c=DC)).then_inc(xn3T_copied, 1)
                if i < NB and i % G == G - 1:
                    g = i // G
                    for o in range(DC):
                        act.wait_ge(q_done, DC * g + o + 1)
                        if g >= 2:
                            act.wait_ge(score_done, G * (g - 1))
                        nc.scalar.activation(qT[:, g % 2, o, :], bank[6 + o][:, :], ACT.Identity,
                                             bias=cols[:, BQ + o:BQ + o + 1]).then_inc(q_copied, 1)
                if 4 <= i < NB + 4:
                    b = i - 4
                    act.wait_ge(attn_turned, b + 1)
                    if b >= 2:
                        act.wait_ge(ctxv_done, b - 1)
                    nc.scalar.copy(attnT[:, b % 2, :], bank[2][:, 0:P]).then_inc(attnT_copied, 1)
                if i >= 6:
                    b = i - 6
                    act.wait_ge(xn4_turned, b + 1)
                    nc.scalar.copy(hT[:, :, b * P:(b + 1) * P],
                                   bank[5][:, 0:D].rearrange("p (c s) -> p c s", c=DC)).then_inc(h_ready, 1)

            with act.Fori(0, NBLK) as blk:
                act.wait_ge(affine_ready, 2 * blk + 2)
                for g in range(NG):
                    n = NG * blk + g
                    for c in range(DC):
                        act.wait_ge(zn_turned, DC * n + (c + 1))
                        nc.scalar.activation(aT[:, g % 2, c, :], bank[2 + c][:, :], ACT.Gelu,
                                             bias=affine[:, 1, c:c + 1],
                                             scale=affine[:, 0, c:c + 1]).then_inc(a_ready, 1)

        @block.vector
        def _(dve):
            steps = [0]
            vec = nc.vector

            def step(ins):
                steps[0] += 1
                ins.then_inc(dve_step, 1)

            def settle():
                dve.wait_ge(dve_step, steps[0])

            def link(ins):
                step(ins)
                settle()

            dve.wait_ge(consts, 12)
            i3 = ident[:, :].rearrange("p (h b) -> p h b", h=NH)
            vec.tensor_reduce(head_sel[:, :], i3, AX.X, ALU.add).then_inc(dve_consts, 1)
            link(vec.tensor_reduce(seq_sel_f[:, :], ident[:, :].rearrange("p (h b) -> p b h", h=NH), AX.X, ALU.add))
            vec.tensor_copy(seq_sel[:, :], seq_sel_f[:, :]).then_inc(dve_consts, 1)
            vec.tensor_copy(expert_no[:, :], expert_no_i[:, :]).then_inc(dve_consts, 1)
            vec.memset(qblk[:, 0:2, :, :], 0.0).then_inc(qblk_zeroed, 1)

            def norm1(t):
                dve.wait_ge(xrstd_ready, t // G + 1)
                if t >= 4:
                    dve.wait_ge(x_turned, t - 3)
                vec.tensor_scalar(xn[:, t % 4, :], xres[:, t, :], bag[:, t, 0:1], rstd[:, t:t + 1],
                                  ALU.subtract, ALU.mult).then_inc(xn_ready, 1)

            def copy_xT(t):
                dve.wait_ge(x_turned, t + 1)
                vec.tensor_copy(xnT[:, :, t * P:(t + 1) * P],
                                bank[t % 2][:, 0:D].rearrange("p (c s) -> p c s", c=DC)).then_inc(x_copied, 1)

            def stats1(g):
                dve.wait_ge(x_in[g], 16)
                for t in range(g * G, (g + 1) * G):
                    step(vec.bn_stats(bst[:, t, :], xres[:, t, :]))
                settle()
                for t in range(g * G, (g + 1) * G):
                    step(vec.bn_aggr(bag[:, t, :], bst[:, t, :]))
                settle()
                vec.tensor_scalar(veps[:, g * G:(g + 1) * G], bag[:, g * G:(g + 1) * G, 1], LN_EPS, None,
                                  ALU.add).then_inc(xvar_ready, 1)

            stats1(0)
            for g in range(NG):
                if g + 1 < NG:
                    stats1(g + 1)
                for t in range(g * G, (g + 1) * G):
                    norm1(t)
                    if t >= 1:
                        copy_xT(t - 1)
                if g == 0:
                    dve.wait_ge(gk_in, 64)
                    vec.tensor_tensor(gk_ctx[:, :, :], gk_raw[:, DC:2 * DC, :], gk_raw[:, 2 * DC:3 * DC, :],
                                      ALU.add).then_inc(gkctx_ready, 1)
                    dve.wait_ge(cols_turned, 1)
                    vec.tensor_copy(cols[:, :], bank[6][:, 0:NROWS]).then_inc(cols_ready, 1)
            copy_xT(NB - 1)

            def dequant(l):
                dve.wait_ge(q_in[l % 2], 16 * (l // 2 + 1))
                if l == 0:
                    dve.wait_ge(ffnw_in, 48)
                if l >= 2:
                    dve.wait_ge(wT_done, l - 1)
                vec.tensor_scalar(wdeq[:, l % 2, :, :], wraw[:, l % 2, :, :], 1.0 / LEVELS, -1.0,
                                  ALU.mult, ALU.add).then_inc(wdeq_ready, 1)
                dve.wait_ge(wdeq_ready, 2 * l + 1)
                w4 = wdeq[:, l % 2, :, :].rearrange("p c (s g) -> p (c s) g", g=GROUP)
                vec.tensor_tensor(w4, w4, scale_sb[:, l, :, :].rearrange("p c s -> p (c s)").unsqueeze(2)
                                  .to_broadcast([P, DC * NS, GROUP]), ALU.mult).then_inc(wdeq_ready, 1)

            def copy_lbT(l):
                dve.wait_ge(lb_turned, l + 1)
                if l >= 2:
                    dve.wait_ge(wT_done, l - 1)
                vec.tensor_copy(lbT[:, l % 2, :], bank[6 + l % 2][0:R, 0:D]).then_inc(lb_copied, 1)

            def make_weight(l):
                dequant(l)
                copy_lbT(l)

            make_weight(0)
            make_weight(1)

            dve.wait_ge(gates_back, 32)
            ig, fg, fabs, fl = gsc[:, 0, :], gsc[:, 1, :], gsc[:, 2, :], gsc[:, 4, :]
            lf, fsum, key_gate, gmax, fm = gsc[:, 3, :], gsc[:, 5, :], gsc[:, 6, :], gsc[:, 1, :], gsc[:, 7, :]
            vec.scalar_tensor_tensor(out=fabs, in0=fg, scalar=-1.0, in1=fg, op0=ALU.mult, op1=ALU.min).then_inc(fabs_ready, 1)
            dve.wait_ge(fln_ready, 1)
            link(vec.scalar_tensor_tensor(out=lf, in0=fg, scalar=0.0, in1=fl, op0=ALU.min, op1=ALU.subtract))
            link(vec.tensor_tensor_scan(fsum, ones[:, :], lf, 0.0, ALU.mult, ALU.add))
            link(vec.tensor_tensor(key_gate, ig, fsum, ALU.subtract))
            link(vec.tensor_tensor_scan(gmax, ones[:, :], key_gate, LOWEST, ALU.mult, ALU.max))
            vec.tensor_tensor(fm, fsum, gmax, ALU.add).then_inc(gsum_ready, 1)
            for h in range(NH):
                step(vec.tensor_scalar(neg_max[:, h, :], gmax, head_sel[:, h:h + 1], -1.0, ALU.mult, ALU.mult))
            settle()
            vec.tensor_copy(neg_hi[:, :, :], neg_max[:, :, :]).then_inc(negmax_ready, 1)
            dve.wait_ge(negmax_ready, 1)
            vec.tensor_tensor(neg_lo[:, :, :], neg_max[:, :, :], neg_hi[:, :, :].bitcast(F32),
                              ALU.subtract).then_inc(negmax_ready, 1)
            dve.wait_ge(x_turned, NB)
            vec.memset(qblk[:, 2:4, :, :], 0.0).then_inc(qblk_zeroed, 1)

            def query_blocks(u, which):
                b, c = u // 2, u % 2
                if u >= 4:
                    dve.wait_ge(qk_done, u - 3)
                for h in which:
                    ins = vec.tensor_scalar(qblk[h * HD:(h + 1) * HD, u % 4, h, :],
                                            xnT[h * HD:(h + 1) * HD, c, b * P:(b + 1) * P],
                                            float(HD) ** -0.5, None, ALU.mult)
                    if h == HU - 1:
                        ins.then_inc(qblk_ready[1], 1)

            def weigh(u):
                dve.wait_ge(qk_done, u + 1)
                dve.wait_ge(exp_done, HU * (u + 1))
                if u >= 2:
                    dve.wait_ge(cv_done, u - 1)
                vec.tensor_tensor(cmat[:, u % 2, :, :].rearrange("p h s -> p (h s)"), bank[2 + u % 2][:, :],
                                  decay[:, u % 2, :, :].rearrange("p h s -> p (h s)"), ALU.mult).then_inc(c_ready, 1)

            dve.wait_ge(qblk_zeroed, 2)
            query_blocks(1, range(HU))
            dve.wait_ge(glim_turned, 2)
            vec.tensor_copy(gT[:, :], bank[4][:, 0:P]).then_inc(dve_consts, 1)
            vec.tensor_scalar(limT[:, :], bank[5][:, 0:P], HEAD_EPS, None, ALU.add).then_inc(glim_copied, 1)
            for l in range(2, NL):
                make_weight(l)

            done = {}

            def mark(name, ins):
                step(ins)
                done[name] = steps[0]

            def need(*names):
                dve.wait_ge(dve_step, max(done[n] for n in names))

            den_abs, den, den2, ss = (small[:, k, :] for k in (0, 1, 6, 7))

            def sum_squares(b):
                dve.wait_ge(sq_ready, b + 1)
                mark("ss", vec.tensor_reduce(ss, sq[:, :, :], AX.X, ALU.add))

            def den_1(b):
                tot = heads_out[:, b % 2, :, HD]
                mark("den_abs", vec.scalar_tensor_tensor(out=den_abs, in0=tot, scalar=-1.0, in1=tot,
                                                         op0=ALU.mult, op1=ALU.max))

            def den_2(b):
                need("den_abs")
                lim = limT[:, :].rearrange("p (h b) -> p b h", h=NH)[:, b, :]
                mark("den", vec.scalar_tensor_tensor(out=den, in0=den_abs, scalar=HEAD_EPS, in1=lim,
                                                     op0=ALU.add, op1=ALU.max))

            def den_3(b):
                need("den")
                mark("den2", vec.tensor_tensor(den2, den, den, ALU.mult))

            def mean_square(b):
                need("den2", "ss")
                vec.scalar_tensor_tensor(out=small[:, 2 + b % 2, :], in0=den2, scalar=HEAD_EPS, in1=ss,
                                         op0=ALU.mult, op1=ALU.add).then_inc(ms_ready, 1)

            def scale_heads(b):
                dve.wait_ge(rms_ready, b + 1)
                vec.tensor_tensor(yh[:, :, :], heads_out[:, b % 2, :, 0:HD],
                                  small[:, 4 + b % 2, :].unsqueeze(2).to_broadcast([P, NH, HD]),
                                  ALU.mult).then_inc(yh_ready, 1)

            def add_heads(b):
                dve.wait_ge(yh_ready, b + 1)
                mark("x1", vec.tensor_tensor(xres[:, b, :], xres[:, b, :], yh[:, :, :].rearrange("p h d -> p (h d)"), ALU.add))

            def stats2(b):
                need("x1")
                mark("bst2", vec.bn_stats(bst2[:, b % 2, :], xres[:, b, :]))

            def aggr2(b):
                need("bst2")
                mark("bag2", vec.bn_aggr(bag2[:, b % 2, :], bst2[:, b % 2, :]))

            def var2(b):
                need("bag2")
                vec.tensor_scalar(veps2[:, b % 2:b % 2 + 1], bag2[:, b % 2, 1:2], LN_EPS, None,
                                  ALU.add).then_inc(var2_ready, 1)

            def norm2(b):
                dve.wait_ge(rstd2_ready, b + 1)
                if b >= 8:
                    dve.wait_ge(scattered[b % 8], 32 * (b // 8))
                vec.tensor_scalar(xn2[:, b % 8, :], xres[:, b, :], bag2[:, b % 2, 0:1], rstd2[:, b % 2:b % 2 + 1],
                                  ALU.subtract, ALU.mult).then_inc(xn2_ready, 1)

            def add_router_bias(j):
                dve.wait_ge(logits_done, 2 * j + 2)
                vec.tensor_tensor(lg[:, :, :], bank[7][:, 0:2 * E].rearrange("p (b e) -> p b e", b=2),
                                  router_b[:, :].unsqueeze(1).to_broadcast([P, 2, E]), ALU.add).then_inc(logits_read, 1)

            def largest(j):
                dve.wait_ge(logits_read, j + 1)
                for k in range(2):
                    mark("max", vec.max(top_v[:, 2 * j + k, :], lg[:, k, :]))

            def largest_at(j):
                need("max")
                for k in range(2):
                    mark("at", vec.max_index(top_i[:, 2 * j + k, :], top_v[:, 2 * j + k, :], lg[:, k, :]))

            def chosen_no(j):
                need("at")
                mark("topi", vec.tensor_copy(topi[:, 2 * j:2 * j + 2, :], top_i[:, 2 * j:2 * j + 2, 0:2]))

            def chosen_mask(j):
                need("topi")
                mark("pick", vec.tensor_tensor(pick[:, j % 2, :, :, :].rearrange("p b k e -> p (b k) e"),
                                               expert_no[:, :].unsqueeze(1).to_broadcast([P, 4, E]),
                                               topi[:, 2 * j:2 * j + 2, :].rearrange("p b k -> p (b k)").unsqueeze(2)
                                               .to_broadcast([P, 4, E]), ALU.is_equal))

            def both_masks(j):
                need("pick")
                mark("mask", vec.tensor_tensor(mask_bf[:, j % 2, :, :], pick[:, j % 2, :, 0, :],
                                               pick[:, j % 2, :, 1, :], ALU.add))

            def seen_1(j):
                need("mask")
                vec.tensor_tensor(seen_bf[:, 2 * j + 1, :], seen_bf[:, 2 * j, :], mask_bf[:, j % 2, 0, :],
                                  ALU.add).then_inc(mask_ready, 1)

            def seen_2(j):
                dve.wait_ge(mask_ready, j + 1)
                step(vec.tensor_tensor(seen_bf[:, 2 * j + 2, :], seen_bf[:, 2 * j + 1, :], mask_bf[:, j % 2, 1, :],
                                       ALU.add))

            def rank_1(j):
                dve.wait_ge(rank_done, j + 1)
                ranks = bank[7][:, 64:64 + 2 * E].rearrange("p (b e) -> p b e", b=2)
                for k in range(TOP_K):
                    ins = vec.tensor_tensor(picked[:, :, k, :], pick[:, j % 2, :, k, :], ranks, ALU.mult)
                ins.then_inc(rank_read, 1)

            def rank_2(j):
                dve.wait_ge(rank_read, j + 1)
                mark("rank", vec.tensor_reduce(rank[:, :, :], picked[:, :, :, :], AX.X, ALU.add))

            def slot_1(j):
                need("rank")
                two = slice(2 * j, 2 * j + 2)
                step(vec.tensor_scalar(over[:, :, :], rank[:, :, :], float(CAP), DROPPED, ALU.is_gt, ALU.mult))
                mark("slot", vec.scalar_tensor_tensor(out=base[:, :, :], in0=topi[:, two, :], scalar=float(CAP),
                                                      in1=rank[:, :, :], op0=ALU.mult, op1=ALU.add))
                step(vec.tensor_scalar(kept[:, two, :], rank[:, :, :], float(CAP), None, ALU.is_le))

            def slot_2(j):
                need("slot")
                vec.scalar_tensor_tensor(out=dest[:, 2 * j:2 * j + 2, :], in0=base[:, :, :], scalar=-1.0,
                                         in1=over[:, :, :], op0=ALU.add, op1=ALU.add).then_inc(dest_ready, 1)

            link(vec.memset(seen_bf[:, 0, :], 0.0))
            dve.wait_ge(router_in, 32)
            for i in range(LAST):
                one = 2 <= i < NB + 2
                two = 3 <= i < NB + 3
                route = i % 2 == 0 and 6 <= i < NB + 6
                place = i % 2 == 1 and 7 <= i < NB + 7
                jr, jp = (i - 6) // 2, (i - 7) // 2
                if 0 < 2 * i - 1 < 2 * NB:
                    weigh(2 * i - 1)
                if 4 <= i < NB + 4:
                    norm2(i - 4)
                if route:
                    add_router_bias(jr)
                if one:
                    sum_squares(i - 2)
                if route:
                    largest(jr)
                if one:
                    den_1(i - 2)
                if two:
                    scale_heads(i - 3)
                if route:
                    largest_at(jr)
                if one:
                    den_2(i - 2)
                if i + 1 < NB:
                    query_blocks(2 * i + 3, (0, 1))
                if one:
                    den_3(i - 2)
                if two:
                    add_heads(i - 3)
                if route:
                    chosen_no(jr)
                if i < NB:
                    weigh(2 * i)
                if one:
                    mean_square(i - 2)
                if route:
                    chosen_mask(jr)
                if two:
                    stats2(i - 3)
                if place:
                    rank_1(jp)
                if i + 1 < NB:
                    query_blocks(2 * i + 3, (2, 3))
                if route:
                    both_masks(jr)
                if place:
                    rank_2(jp)
                if two:
                    aggr2(i - 3)
                if route:
                    seen_1(jr)
                if place:
                    slot_1(jp)
                if two:
                    var2(i - 3)
                if route:
                    seen_2(jr)
                if place:
                    slot_2(jp)

            link(vec.memset(gath[:, :, :, :], 0.0))
            vec.tensor_tensor(wtop[:, :, 1], top_v[:, :, 1], top_v[:, :, 0], ALU.subtract).then_inc(topdiff_ready, 1)
            dve.wait_ge(topexp_ready, 1)
            link(vec.tensor_scalar(wtop[:, :, 1], wtop[:, :, 0], 1.0, None, ALU.add))
            link(vec.reciprocal(veps[:, 0:NB], wtop[:, :, 1]))
            link(vec.tensor_tensor(wtop[:, :, 1], wtop[:, :, 0], veps[:, 0:NB], ALU.mult))
            link(vec.tensor_copy(wtop[:, :, 0], veps[:, 0:NB]))
            vec.tensor_tensor(wtop[:, :, :], wtop[:, :, :], kept[:, :, :], ALU.mult).then_inc(gath_zeroed, 1)

            def copy_xinT(e, j):
                vec.tensor_copy(b1_cur[:, j, :], cols[:, bass.ds(B1 + FC * e, FC)]).then_inc(b1_ready, 1)
                for c in range(DC):
                    dve.wait_ge(xin_turned, DC * e + (c + 1))
                    vec.tensor_copy(xinT[:, j, c, :], bank[4 + c][:, 0:CAP]).then_inc(xinT_copied, 1)

            def results(e, j, first):
                if not first:
                    dve.wait_ge(y_out[j], 16 * e - 16 * j)
                for m in range(MT):
                    n = P if m < MT - 1 else MTAIL
                    dve.wait_ge(y_done, MT * e + (m + 1))
                    bb = b2_row[0:n, bass.ds(e, 1), :].rearrange("p a d -> p (a d)")
                    vec.tensor_tensor(y_sb[0:n, j, m, :], bank[6 + (MT * j + m) % 2][0:n, 0:D], bb, ALU.add).then_inc(y_ready, 1)

            dve.wait_ge(b2_in, 16)
            copy_xinT(0, 0)
            copy_xinT(1, 1)
            results(0, 0, True)
            copy_xinT(2, 0)
            results(1, 1, True)
            with dve.Fori(1, E // 2 - 1) as k:
                for j in range(2):
                    copy_xinT(2 * k + (j + 1), 1 - j)
                    results(2 * k + j, j, False)
            for e in range(E - 2, E):
                if e + 1 < E:
                    copy_xinT(e + 1, (e + 1) % 2)
                results(e, e % 2, False)

            def combine(b):
                dve.wait_ge(gathered[b % 2], 32 * (b // 2 + 1))
                link(vec.scalar_tensor_tensor(out=xres[:, b, :], in0=gath[:, b % 2, 0, :], scalar=wtop[:, b, 0:1],
                                              in1=xres[:, b, :], op0=ALU.mult, op1=ALU.add))
                vec.scalar_tensor_tensor(out=xres[:, b, :], in0=gath[:, b % 2, 1, :], scalar=wtop[:, b, 1:2],
                                         in1=xres[:, b, :], op0=ALU.mult, op1=ALU.add).then_inc(x2_ready, 1)
                dve.wait_ge(x2_ready, b + 1)
                link(vec.bn_stats(bst2[:, b % 2, :], xres[:, b, :]))
                link(vec.bn_aggr(bag2[:, b % 2, :], bst2[:, b % 2, :]))
                vec.tensor_scalar(veps2[:, b % 2:b % 2 + 1], bag2[:, b % 2, 1:2], LN_EPS, None,
                                  ALU.add).then_inc(var3_ready, 1)

            def score_max(b):
                dve.wait_ge(score_done, b + 1)
                if b >= 2:
                    dve.wait_ge(x3_ready, b - 1)
                vec.tensor_reduce(smax[:, 0, b % 2:b % 2 + 1], bank[b % 2][:, 0:P], AX.X, ALU.max,
                                  negate=True).then_inc(smax_ready, 1)

            def attend(b):
                dve.wait_ge(attn_ready, b + 1)
                link(vec.reciprocal(rank[:, b % 2, 0:1], smax[:, 1, b % 2:b % 2 + 1]))
                dve.wait_ge(ctxv_done, b + 1)
                vec.scalar_tensor_tensor(out=xres[:, b, :], in0=bank[3][:, 0:D], scalar=rank[:, b % 2, 0:1],
                                         in1=xres[:, b, :], op0=ALU.mult, op1=ALU.add).then_inc(x3_ready, 1)
                dve.wait_ge(x3_ready, b + 1)
                link(vec.bn_stats(bst5[:, b % 2, :], xres[:, b, :]))
                link(vec.bn_aggr(bag5[:, 0, b % 2, :], bst5[:, b % 2, :]))
                vec.tensor_scalar(veps5[:, 0, b % 2:b % 2 + 1], bag5[:, 0, b % 2, 1:2], LN_EPS, None,
                                  ALU.add).then_inc(var4_ready, 1)

            def norm3(b):
                dve.wait_ge(rstd3_ready, b + 1)
                if b >= 2:
                    dve.wait_ge(xn3_turned, b - 1)
                vec.tensor_scalar(xn3[:, b % 2, :], xres[:, b, :], bag2[:, b % 2, 0:1], rstd2[:, b % 2:b % 2 + 1],
                                  ALU.subtract, ALU.mult).then_inc(xn3_ready, 1)

            def norm4(b):
                dve.wait_ge(rstd4_ready, b + 1)
                if b >= 2:
                    dve.wait_ge(xn4_turned, b - 1)
                vec.tensor_scalar(xn4[:, b % 2, :], xres[:, b, :], bag5[:, 0, b % 2, 0:1],
                                  rstd5[:, 0, b % 2:b % 2 + 1], ALU.subtract, ALU.mult).then_inc(xn4_ready, 1)

            for i in range(NB + 5):
                if i < NB:
                    combine(i)
                if 4 <= i < NB + 4:
                    score_max(i - 4)
                if 5 <= i:
                    attend(i - 5)
                if i < NB:
                    norm3(i)
                if 5 <= i:
                    norm4(i - 5)

            dve.wait_ge(biasrow_in, 16)
            base_steps = steps[0]
            PER_GROUP = 2 * G
            PER_BLK = PER_GROUP * NG

            for k in range(2):
                vec.memset(veps5[:, k, :], 0.0).then_inc(yb_ready, 1)
            with dve.Fori(0, NBLK) as blk:
                vec.tensor_copy(w2cur[:, :, :], wT[:, bass.ds(2 * blk + 1, 1), :, :].rearrange("p a c n -> p (a c) n")
                                ).then_inc(w2cur_ready, 1)

                for k, at in ((0, GA), (1, BE)):
                    vec.tensor_copy(affine[:, k, :], cols[:, bass.ds(at + DC * blk, DC)]).then_inc(affine_ready, 1)

                def first_half(g):
                    n = NG * blk + g
                    at = base_steps + PER_GROUP * g + PER_BLK * blk
                    for t in range(G):
                        dve.wait_ge(yf_done, G * n + (t + 1))
                        vec.tensor_tensor(yb[:, (g % 2) * G + t, :], bank[t % 2][:, 0:D],
                                          bias_row[:, bass.ds(blk, 1), :].rearrange("p a d -> p (a d)"),
                                          ALU.add).then_inc(yb_ready, 1)
                        dve.wait_ge(yb_ready, G * n + (t + 3))
                        vec.bn_stats(bst5[:, t, :], yb[:, (g % 2) * G + t, :]).then_inc(dve_step, 1)
                    dve.wait_ge(dve_step, at + G)
                    vec.memset(rstd5[:, g % 2, :], 0.0).then_inc(memset_done, 1)
                    for t in range(G):
                        vec.bn_aggr(bag5[:, g % 2, t, :], bst5[:, t, :]).then_inc(dve_step, 1)
                    dve.wait_ge(dve_step, at + 2 * G)
                    vec.tensor_scalar(veps5[:, g % 2, :], bag5[:, g % 2, :, 1], LN_EPS, None,
                                      ALU.add).then_inc(var5_ready, 1)

                def normalise(g):
                    n = NG * blk + g
                    dve.wait_ge(rstd5_ready, n + 1)
                    for t in range(G):
                        vec.tensor_scalar(zn[:, (g % 2) * G + t, :], yb[:, (g % 2) * G + t, :],
                                          bag5[:, g % 2, t, 0:1], rstd5[:, g % 2, t:t + 1],
                                          ALU.subtract, ALU.mult).then_inc(zn_ready, 1)

                def update(g):
                    n = NG * blk + g
                    for o in range(DC):
                        dve.wait_ge(y2_done, DC * n + (o + 1))
                        h = hT[:, o, g * GT:(g + 1) * GT]
                        vec.scalar_tensor_tensor(out=h, in0=bank[4 + o][:, :],
                                                 scalar=cols[:, bass.ds(BI + DC + 2 * DC * blk + o, 1)], in1=h,
                                                 op0=ALU.add, op1=ALU.add).then_inc(h_ready, 1)

                for g in range(NG):
                    first_half(g)
                    if g >= 1:
                        update(g - 1)
                    normalise(g)
                update(NG - 1)

            for t in range(NB):
                dve.wait_ge(fin_turned, t + 1)
                if t >= 4:
                    dve.wait_ge(out_done, 16 * (t // 4 * 4))
                vec.tensor_tensor(o_sb[:, t % 4, :], bank[6 + t % 2][:, 0:D], xres[:, t, :],
                                  ALU.add).then_inc(fin_ready, 1)

        @block.tensor
        def _(pe):
            mm = pe.matmul

            def turn(dst, src, n=P):
                return pe.transpose(dst, src, ident[0:n, 0:n])

            pe.wait_ge(consts, 12)
            pe.wait_ge(rows_in, 96)
            turn(bank[6][:, 0:NROWS], rows[:, :], NROWS).then_inc(cols_turned, 1)

            def turn_ctx(t):
                pe.wait_ge(ctx_in[t // G], 16)
                if t >= 2:
                    pe.wait_ge(ctx_copied, t - 1)
                for c in range(DC):
                    ins = turn(bank[2 + t % 2][:, c * P:(c + 1) * P], ctx_tok[:, t, c * P:(c + 1) * P])
                ins.then_inc(ctx_turned, 1)

            def turn_x(t):
                pe.wait_ge(xn_ready, t + 1)
                if t >= 2:
                    pe.wait_ge(x_copied, t - 1)
                for c in range(DC):
                    ins = turn(bank[t % 2][:, c * P:(c + 1) * P], xn[:, t % 4, c * P:(c + 1) * P])
                ins.then_inc(x_turned, 1)

            def gates(g):
                pe.wait_ge(x_copied, G * (g + 1))
                pe.wait_ge(ctx_copied, G * (g + 1))
                pe.wait_ge(gkctx_ready, 1)
                if g >= 2:
                    pe.wait_ge(gates_copied, g - 1)
                at = slice(g * GT, (g + 1) * GT)
                dst = bank[4 + g % 2][0:2 * NH, :]
                for c in range(DC):
                    mm(dst, gk_raw[:, c, :], xnT[:, c, at], start=(c == 0), stop=False)
                for c in range(DC):
                    ins = mm(dst, gk_ctx[:, c, :], ctxT[:, c, at], start=False, stop=(c == DC - 1))
                ins.then_inc(gates_done, 1)

            for g in range(NG):
                for t in range(g * G, (g + 1) * G):
                    turn_ctx(t)
                    turn_x(t)
                if g >= 1:
                    gates(g - 1)
            gates(NG - 1)

            def weight(l):
                if l == 0:
                    pe.wait_ge(ffnw_in, 48)
                    pe.wait_ge(cols_ready, 1)
                if l >= 2:
                    pe.wait_ge(lb_copied, l - 1)
                for c in range(DC):
                    ins = turn(bank[6 + l % 2][0:R, c * P:(c + 1) * P], lb_sb[:, l, c, :])
                ins.then_inc(lb_turned, 1)
                pe.wait_ge(wdeq_ready, 2 * l + 2)
                pe.wait_ge(lb_copied, l + 1)
                if l >= 2:
                    pe.wait_ge(wT_copied, l - 1)
                for c in range(DC):
                    at = c * D
                    mm(bank[l % 2][:, at:at + D], la_sb[:, l, c * P:(c + 1) * P], lbT[:, l % 2, :],
                       start=True, stop=True)
                    for o in range(DC):
                        ins = mm(bank[l % 2][:, at + o * P:at + (o + 1) * P], wdeq[:, l % 2, o, c * P:(c + 1) * P],
                                 ident[:, :], start=False, stop=(o == DC - 1), skip_group_check=True)
                ins.then_inc(wT_done, 1)

            weight(0)
            weight(1)
            pe.wait_ge(gsum_ready, 1)
            pe.wait_ge(gates_copied, NG)
            turn(bank[4][:, 0:P], gsc[:, 6, :]).then_inc(glim_turned, 1)
            pe.wait_ge(lim_ready, 1)
            turn(bank[5][:, 0:P], gsc[:, 2, :]).then_inc(glim_turned, 1)
            for l in range(2, NL):
                weight(l)

            def max_rows(u):
                b = u // 2
                pe.wait_ge(negmax_ready, 2)
                if u < 2:
                    pe.wait_ge(wT_copied, NL)
                else:
                    pe.wait_ge(exp_done, HU * (u - 1))
                mm(bank[u % 2][:, :], ident_bf[:, :], causal_bf[:, :, :].rearrange("p h i -> p (h i)"),
                   start=True, stop=False)
                for k, part in enumerate((neg_hi, neg_lo)):
                    ins = mm(bank[u % 2][:, :], seq_sel[:, b:b + 1].to_broadcast([P, P]),
                             part[:, HU * (u % 2):HU * (u % 2 + 1), :].rearrange("p h i -> p (h i)"),
                             start=False, stop=(k == 1))
                ins.then_inc(maxb_done, 1)

            def keys_queries(u):
                b = u // 2
                pe.wait_ge(qblk_ready[u % 2], u // 2 + 1)
                if u >= 2:
                    pe.wait_ge(c_ready, u - 1)
                mm(bank[2 + u % 2][:, :], ctxT[:, u % 2, b * P:(b + 1) * P],
                   qblk[:, u % 4, :, :].rearrange("p h i -> p (h i)"),
                   start=True, stop=True).then_inc(qk_done, 1)

            def values(u):
                b = u // 2
                pe.wait_ge(c_ready, u + 1)
                pe.wait_ge(vaug_ready, b + 1)
                if b >= 2:
                    pe.wait_ge(heads_copied, b - 1)
                else:
                    pe.wait_ge(glim_copied, 1)
                for h in range(HU):
                    hh = HU * (u % 2) + h
                    ins = mm(bank[4 + b % 2][:, hh * HA:(hh + 1) * HA], cmat[:, u % 2, h, :],
                             v_aug[:, b % 2, hh, :], start=True, stop=True)
                ins.then_inc(cv_done, 1)

            def turn_xn2(b):
                pe.wait_ge(xn2_ready, b + 1)
                if b == 0:
                    pe.wait_ge(lb_copied, NL)
                else:
                    pe.wait_ge(xn2T_copied, b)
                for c in range(DC):
                    ins = turn(bank[6][:, c * P:(c + 1) * P], xn2[:, b % 8, c * P:(c + 1) * P])
                ins.then_inc(xn2_turned, 1)

            def logits(b):
                pe.wait_ge(xn2T_copied, b + 1)
                pe.wait_ge(router_in, 32)
                if b >= 2 and b % 2 == 0:
                    pe.wait_ge(logits_read, b // 2)
                if b >= 3 and b % 2 == 1:
                    pe.wait_ge(rank_read, b // 2)
                at = b % 2 * E
                for c in range(DC):
                    ins = mm(bank[7][:, at:at + E], xn2T[:, b % 2, c, :], router_w[:, c, :],
                             start=(c == 0), stop=(c == DC - 1))
                ins.then_inc(logits_done, 1)

            def ranks(j):
                pe.wait_ge(mask_ready, j + 1)
                dst = bank[7][:, 64:64 + 2 * E]
                mm(dst, tri_bf[:, :], mask_bf[:, j % 2, :, :].rearrange("p b e -> p (b e)"), start=True, stop=False)
                mm(dst, ones_bf[:, :], seen_bf[:, 2 * j:2 * j + 2, :].rearrange("p b e -> p (b e)"),
                   start=False, stop=True).then_inc(rank_done, 1)

            def attn_values(n):
                g, o = n // DC, n % DC
                if n == 0:
                    pe.wait_ge(attnw_in, 32)
                    pe.wait_ge(exp_done, 2 * NB * HU)
                    pe.wait_ge(c_ready, 2 * NB)
                if n >= 4:
                    pe.wait_ge(vT_copied, n - 3)
                for c in range(DC):
                    ins = mm(bank[n % 4][:, :], wv_sb[:, c, o * P:(o + 1) * P], ctxT[:, c, g * GT:(g + 1) * GT],
                             start=(c == 0), stop=(c == DC - 1))
                ins.then_inc(vT_done, 1)

            def turn_vT(b):
                pe.wait_ge(vT_copied, DC * (b // G + 1))
                if b >= 2:
                    pe.wait_ge(vtok_copied, b - 1)
                else:
                    pe.wait_ge(heads_copied, NB)
                for c in range(DC):
                    ins = turn(bank[4 + b % 2][:, c * P:(c + 1) * P], vT[:, c, b * P:(b + 1) * P])
                ins.then_inc(vtok_turned, 1)

            for i in range(LAST):
                if i < NB:
                    max_rows(2 * i)
                if 1 <= i <= NB:
                    values(2 * i - 2)
                if 5 <= i < NB + 5:
                    logits(i - 5)
                if i % 2 == 1 and 7 <= i < NB + 7:
                    ranks((i - 7) // 2)
                if i < NB:
                    keys_queries(2 * i)
                    max_rows(2 * i + 1)
                if 1 <= i <= NB:
                    values(2 * i - 1)
                if 4 <= i < NB + 4:
                    turn_xn2(i - 4)
                if i < NB:
                    keys_queries(2 * i + 1)
                for n in VT_AT.get(i, ()):
                    attn_values(n)
                for b in VTOK_AT.get(i, ()):
                    turn_vT(b)

            def turn_slots(e, j, first=False):
                pe.wait_ge(xin_in[j], 16 * e - 16 * j + 32)
                for c in range(DC):
                    if first:
                        pe.wait_ge(vtok_copied, NB)
                    else:
                        pe.wait_ge(xinT_copied, DC * e - DC + (c + 1))
                    for m in range(MT):
                        n = P if m < MT - 1 else MTAIL
                        ins = turn(bank[4 + c][:, m * P:m * P + n], xin[0:n, j, m, c * P:(c + 1) * P], n)
                    ins.then_inc(xin_turned, 1)

            def hidden(e, j, first=False):
                pe.wait_ge(w1_in[j], 8 * e - 8 * j + 16)
                pe.wait_ge(xinT_copied, DC * e + DC)
                for f in range(FC):
                    if first and f < 4:
                        pe.wait_ge(vT_copied, NG * DC)
                    else:
                        pe.wait_ge(h_copied, FC * e + f - 3)
                    for c in range(DC):
                        ins = mm(bank[f % 4][:, 0:CAP], w1_sb[:, j, c, f * P:(f + 1) * P], xinT[:, j, c, :],
                                 start=(c == 0), stop=(c == DC - 1))
                    ins.then_inc(h_done, 1)

            def results(e, j, first=False):
                pe.wait_ge(w2_in[j], 8 * e - 8 * j + 16)
                for m in range(MT):
                    n = P if m < MT - 1 else MTAIL
                    if first and m < 2:
                        pe.wait_ge(rank_read, NB // 2)
                    else:
                        pe.wait_ge(y_ready, MT * e + m - 1)
                    dst = bank[6 + (MT * j + m) % 2][0:n, 0:D]
                    for f in range(FC):
                        if m == 0:
                            pe.wait_ge(h_copied, FC * e + (f + 1))
                        ins = mm(dst, h_moe[j][:, f, m * P:m * P + n], w2_sb[:, j, f, :],
                                 start=(f == 0), stop=(f == FC - 1))
                    ins.then_inc(y_done, 1)

            turn_slots(0, 0, True)
            hidden(0, 0, True)
            turn_slots(1, 1)
            results(0, 0, True)
            hidden(1, 1)
            turn_slots(2, 0)
            results(1, 1)
            with pe.Fori(1, E // 2 - 1) as k:
                for j in range(2):
                    hidden(2 * k + j, j)
                    turn_slots(2 * k + (j + 1), 1 - j)
                    results(2 * k + j, j)
            for e in range(E - 2, E):
                hidden(e, e % 2)
                if e + 1 < E:
                    turn_slots(e + 1, (e + 1) % 2)
                results(e, e % 2)

            def score(b):
                g = b // G
                pe.wait_ge(q_copied, DC * (g + 1))
                if b < 2:
                    pe.wait_ge(h_copied, E * FC)
                else:
                    pe.wait_ge(attn_ready, b - 1)
                for c in range(DC):
                    ins = mm(bank[b % 2][:, 0:P], qT[:, g % 2, c, b % G * P:(b % G + 1) * P],
                             vT[:, c, b * P:(b + 1) * P], start=(c == 0), stop=(c == DC - 1))
                ins.then_inc(score_done, 1)

            for i in range(NB + 6):
                if 4 <= i < NB + 4:
                    score(i - 4)
                if 5 <= i < NB + 5:
                    b = i - 5
                    pe.wait_ge(attnT_copied, b + 1)
                    pe.wait_ge(vtok_copied, NB)
                    if b >= 1:
                        pe.wait_ge(x3_ready, b)
                    mm(bank[3][:, 0:D], attnT[:, b % 2, :], v_tok[:, b, :], start=True, stop=True).then_inc(ctxv_done, 1)
                if i < NB:
                    pe.wait_ge(xn3_ready, i + 1)
                    if i == 0:
                        pe.wait_ge(xinT_copied, E * DC)
                    else:
                        pe.wait_ge(xn3T_copied, i)
                    for c in range(DC):
                        ins = turn(bank[4][:, c * P:(c + 1) * P], xn3[:, i % 2, c * P:(c + 1) * P])
                    ins.then_inc(xn3_turned, 1)
                if i >= 6:
                    b = i - 6
                    pe.wait_ge(xn4_ready, b + 1)
                    if b >= 1:
                        pe.wait_ge(h_ready, b)
                    for c in range(DC):
                        ins = turn(bank[5][:, c * P:(c + 1) * P], xn4[:, b % 2, c * P:(c + 1) * P])
                    ins.then_inc(xn4_turned, 1)
                if 4 <= i < NB + 4:
                    b = i - 4
                    pe.wait_ge(attn_ready, b + 1)
                    if b >= 1:
                        pe.wait_ge(attnT_copied, b)
                    turn(bank[2][:, 0:P], attn[:, b % 2, :]).then_inc(attn_turned, 1)
                if i < NB and i % G == G - 1:
                    g = i // G
                    pe.wait_ge(xn3T_copied, G * (g + 1))
                    for o in range(DC):
                        if g == 0:
                            pe.wait_ge(y_ready, E * MT)
                        else:
                            pe.wait_ge(q_copied, DC * (g - 1) + (o + 1))
                        for c in range(DC):
                            ins = mm(bank[6 + o][:, :], wq_sb[:, c, o * P:(o + 1) * P], xn3T[:, g % 2, c, :],
                                     start=(c == 0), stop=(c == DC - 1))
                        ins.then_inc(q_done, 1)

            pe.wait_ge(attn_ready, NB)
            pe.wait_ge(attnT_copied, NB)
            pe.wait_ge(x3_ready, NB)
            with pe.Fori(0, NBLK) as blk:
                def first(g):
                    n = NG * blk + g
                    pe.wait_ge(h_ready, NB - DC * NG + DC * (n + 1))
                    for t in range(G):
                        pe.wait_ge(yb_ready, G * n + (t + 1))
                        for c in range(DC):
                            ins = mm(bank[t % 2][:, 0:D], hT[:, c, (g * G + t) * P:(g * G + t + 1) * P],
                                     wT[:, bass.ds(2 * blk, 1), c, :].rearrange("p a n -> p (a n)"),
                                     start=(c == 0), stop=(c == DC - 1))
                        ins.then_inc(yf_done, 1)

                def second(g):
                    n = NG * blk + g
                    pe.wait_ge(zn_ready, G * n + G)
                    for c in range(DC):
                        for t in range(G):
                            ins = turn(bank[2 + c][:, t * P:(t + 1) * P], zn[:, (g % 2) * G + t, c * P:(c + 1) * P])
                        ins.then_inc(zn_turned, 1)
                    return n

                def product(g):
                    n = NG * blk + g
                    pe.wait_ge(w2cur_ready, blk + 1)
                    for o in range(DC):
                        pe.wait_ge(h_ready, NB - DC + DC * n + (o + 1))
                        for c in range(DC):
                            if o == 0:
                                pe.wait_ge(a_ready, DC * n + (c + 1))
                            ins = mm(bank[4 + o][:, :], w2cur[:, c, o * P:(o + 1) * P], aT[:, g % 2, c, :],
                                     start=(c == 0), stop=(c == DC - 1))
                        ins.then_inc(y2_done, 1)

                first(0)
                for g in range(NG):
                    if g + 1 < NG:
                        first(g + 1)
                    second(g)
                    product(g)
            for t in range(NB):
                pe.wait_ge(h_ready, NB + DC * NG * (NBLK - 1) + DC * (t // G + 1))
                if t < 2:
                    pe.wait_ge(q_copied, NG * DC)
                else:
                    pe.wait_ge(fin_ready, t - 1)
                for c in range(DC):
                    ins = turn(bank[6 + t % 2][:, c * P:(c + 1) * P], hT[:, c, t * P:(t + 1) * P])
                ins.then_inc(fin_turned, 1)


_INS = ["x", "ctx_1024", "L0_xattn_igate_kernel", "L0_xattn_igate_bias", "L0_xattn_fgate_kernel",
        "L0_xattn_fgate_bias", "L0_ffn_gate_w", "L0_ffn_gate_b", "L0_ffn_w1", "L0_ffn_b1", "L0_ffn_w2",
        "L0_ffn_b2", "L1_xattn_Wq", "L1_xattn_bq", "L1_xattn_Wv", "L1_xattn_bv", "L1_ffn_qweights",
        "L1_ffn_scales", "L1_ffn_biases", "L1_ffn_lora_a", "L1_ffn_lora_b", "L1_ffn_ln_gamma",
        "L1_ffn_ln_beta"]


def kernel(**inputs):
    import numpy as np
    import concourse.bacc as bacc
    from concourse.bass_utils import run_bass_kernel_spmd

    nc = bacc.Bacc("TRN2", target_bir_lowering=False, num_devices=1)
    arrays, args = {}, []
    for name in _INS:
        a = np.ascontiguousarray(inputs[name])
        arrays[f"in_{name}"] = a
        args.append(nc.dram_tensor(f"in_{name}", a.shape, mybir.dt.from_np(a.dtype), kind="ExternalInput").ap())
    out = nc.dram_tensor("out_x", tuple(inputs["x"].shape), F32, kind="ExternalOutput").ap()
    mega_kernel(nc, *args, out)
    r = run_bass_kernel_spmd(nc, [arrays], core_ids=[0])
    return r.results[0]["out_x"]
```

```python
from contextlib import ExitStack

import concourse.bass as bass
from concourse import mybir

P = 128
ALU = mybir.AluOpType
ACT = mybir.ActivationFunctionType
AX = mybir.AxisListType
F32 = mybir.dt.float32
F32R = mybir.dt.float32r
BF16 = mybir.dt.bfloat16
I32 = mybir.dt.int32
U32 = mybir.dt.uint32

CAP_FACTOR, TOP_K, LEVELS, GROUP = 1.25, 2, 7.5, 16
LN_EPS, HEAD_EPS = 1e-5, 1e-6
LOWEST = -3.0e38
DROPPED = 1.0e6
MASKED = -1.0e30


def mega_kernel(nc, x, ctx, igate_kernel, igate_bias, fgate_kernel, fgate_bias, gate_w, gate_b,
                w1, b1, w2, b2, Wq, bq, Wv, bv, qweights, scales, biases, lora_a, lora_b,
                ln_gamma, ln_beta, out):
    NB, S, D = x.shape
    NH = igate_kernel.shape[1]
    HD = D // NH
    E, _, FF = w1.shape
    NL, _, _ = qweights.shape
    NBLK = NL // 2
    R = lora_a.shape[1]
    T = NB * S
    DC, FC = D // P, FF // P
    CAP = int(CAP_FACTOR * T / E)
    SLOTS = E * CAP
    G = 4
    NG = NB // G
    GT = G * P
    HU = NH // 2
    HA = HD + 1
    MT = -(-CAP // P)
    MTAIL = CAP - (MT - 1) * P
    NS = D // GROUP
    assert S == P and NH * NB == P and DC == 2 and HU * HD == P and SLOTS % P == 0

    with ExitStack() as stack:
        def sb(name, shape, dt=F32):
            return stack.enter_context(nc.sbuf_tensor(name, shape, dt))

        def region(name, kilobytes):
            first = -(-nc.sbuf_base // 32) * 32
            sb(name, [P, kilobytes * 256])
            return first

        def place(name, first, shape, dt=F32):
            return nc.alloc_sbuf_tensor_at(name, shape, dt, offset=first)

        def sem(name):
            return stack.enter_context(nc.semaphore(name))

        slots_dram = nc.dram_tensor("slots_dram", (SLOTS, D), F32).ap()
        experts_dram = nc.dram_tensor("experts_dram", (SLOTS, D), F32).ap()

        xres = sb("xres", [P, NB, D])
        ctx_tok = sb("ctx_tok", [P, NB, D])
        v_tok = ctx_tok
        KB = 1024
        features, weights, raw, mixed = region("features", 48), region("weights", 32), region("raw", 16), region("mixed", 16)
        xnT = place("xnT", features, [P, DC, T])
        vT = place("vT", features + 16 * KB, [P, DC, T])
        ctxT = place("ctxT", features + 32 * KB, [P, DC, T])
        hT = xnT

        wT_hi = sb("wT_hi", [P, NL, DC, D], F32R)
        wT_lo = sb("wT_lo", [P, NL, DC, D], F32R)
        b2_row = sb("b2_row", [P, E, D])
        gk_raw = sb("gk_raw", [P, 3 * DC, 2 * NH])
        gk_ctx = sb("gk_ctx", [P, DC, 2 * NH])
        gate_bias = sb("gate_bias", [2 * NH, 1])
        router_w = sb("router_w", [P, DC, E])
        router_b = sb("router_b", [P, E])
        wq_sb = sb("wq_sb", [P, DC, D])
        wv_sb = sb("wv_sb", [P, DC, D])
        bias_row = sb("bias_row", [P, NBLK, D])
        scale_sb = sb("scale_sb", [P, NL, DC, NS])
        la_sb = sb("la_sb", [R, NL, D])
        lb_sb = sb("lb_sb", [P, NL, DC, R])
        lbT = place("lbT", features + 30 * KB, [R, 2, D])
        B1, GA, BE, BI, BQ, BV = 0, E * FC, E * FC + NBLK * DC, E * FC + 2 * NBLK * DC, \
            E * FC + (2 * NBLK + NL) * DC, E * FC + (2 * NBLK + NL) * DC + DC
        NROWS = BV + DC
        rows = sb("rows", [NROWS, P])
        cols = sb("cols", [P, NROWS])

        ident = sb("ident", [P, P])
        ones = sb("ones", [P, P])
        tri_bf = sb("tri_bf", [P, P], BF16)
        ones_bf = sb("ones_bf", [P, P], BF16)
        ident_bf = sb("ident_bf", [P, P], BF16)
        causal_bf = sb("causal_bf", [P, HU, P], BF16)
        seq_sel_f = sb("seq_sel_f", [P, NB])
        seq_sel = sb("seq_sel", [P, NB], F32R)
        head_sel_p = sb("head_sel_p", [P, NH])
        head_sel = sb("head_sel", [P, NH])
        expert_no_i = sb("expert_no_i", [P, E], I32)
        expert_no = sb("expert_no", [P, E])
        mhalf = sb("mhalf", [P, 16])
        zero_row = sb("zero_row", [P, D])

        bst = sb("bst", [P, NB, 6])
        bag = sb("bag", [P, NB, 2])
        veps = sb("veps", [P, NB])
        rstd = sb("rstd", [P, NB])
        bst2 = sb("bst2", [P, 2, 6])
        bag2 = sb("bag2", [P, 2, 2])
        veps2 = sb("veps2", [P, 2])
        rstd2 = sb("rstd2", [P, 2])
        gates_sb = place("gates_sb", mixed, [2 * NH, 2, GT])
        gates_tok = sb("gates_tok", [P, 2 * NH, NB])
        gmax_hi = sb("gmax_hi", [P, P], F32R)
        gmax_lo = sb("gmax_lo", [P, P], F32R)
        gT = sb("gT", [P, P])
        limT = sb("limT", [P, P])
        neg_hi = place("neg_hi", mixed + 8 * KB, [P, NH, P], F32R)
        neg_lo = place("neg_lo", mixed + 12 * KB, [P, NH, P], F32R)

        scratch = place("scratch", weights, [P, 8 * GT])

        def view(buf, at, *shape):
            n = 1
            for s in shape:
                n *= s
            flat = buf[:, at:at + n]
            if len(shape) == 1:
                return flat
            names = "abcd"[:len(shape)]
            return flat.rearrange(f"p ({' '.join(names)}) -> p {' '.join(names)}",
                                  **dict(zip(names, shape)))

        decay = view(scratch, 0, 2, HU, P)
        cmat = view(scratch, 2 * GT, 2, HU, P)
        qblk = view(scratch, 4 * GT, 4, HU, P)
        xn = view(scratch, 6 * GT, 4, D)
        xn2 = place("xn2", mixed, [P, 8, D])
        work = place("work", weights + 16 * KB, [P, 8 * D])
        v_aug = sb("v_aug", [P, 2, NH, HA])
        sq = view(work, 0, NH, HD)
        yh = view(work, D, NH, HD)
        xn2T = view(work, 2 * D, 2, DC, P)
        heads_out = view(work, 4 * D, 2, NH, HA)
        gsc = place("gsc", weights + 24 * KB, [P, 8, P])
        wraw = place("wraw", features + 16 * KB, [P, NL, DC, D], I32)
        wdeq = place("wdeq", features + 16 * KB, [P, NL, DC, D])
        small = sb("small", [P, 8, NH])
        lg = sb("lg", [P, 2, E])
        top_v = sb("top_v", [P, NB, 8])
        top_i = sb("top_i", [P, NB, 8], U32)
        topi = sb("topi", [P, NB, 2])
        pick = sb("pick", [P, 2, 2, 2, E])
        picked = sb("picked", [P, 2, 2, E])
        mask_bf = sb("mask_bf", [P, 2, 2, E], BF16)
        seen_bf = sb("seen_bf", [P, NB + 1, E], BF16)
        rank = sb("rank", [P, 2, 2])
        over = sb("over", [P, 2, 2])
        base = sb("base", [P, 2, 2])
        kept = sb("kept", [P, NB, 2])
        dest = sb("dest", [P, NB, 2], U32)
        wtop = sb("wtop", [P, NB, 2])
        xin = place("xin", features, [P, 2, MT, D])
        xT_hi = place("xT_hi", features + 6 * KB, [P, DC, CAP], F32R)
        xT_lo = place("xT_lo", features + 9 * KB, [P, DC, CAP], F32R)
        h_hi = place("h_hi", features + 12 * KB, [P, FC, CAP], F32R)
        h_lo = place("h_lo", features + 22 * KB, [P, FC, CAP], F32R)
        w1_raw = place("w1_raw", raw, [P, DC, FF])
        w2_raw = place("w2_raw", raw + 8 * KB, [P, FC, D])
        w1_hi = place("w1_hi", weights, [P, DC, FF], F32R)
        w1_lo = place("w1_lo", weights + 8 * KB, [P, DC, FF], F32R)
        w2_hi = place("w2_hi", weights + 16 * KB, [P, FC, D], F32R)
        w2_lo = place("w2_lo", weights + 24 * KB, [P, FC, D], F32R)
        y_sb = place("y_sb", mixed, [P, 2, MT, D])
        h_ring = place("h_ring", mixed + 8 * KB, [P, 4, CAP])
        H2 = FC // 2
        FIRST_BANK = (6, 7, 0, 1)
        TO_SCORE, TO_ATTEND, TO_NORM = 3, 4, 5
        gath = place("gath", raw, [P, 4, 2, D])
        xn3T = place("xn3T", weights + 16 * KB, [P, 2, DC, P])
        qT = place("qT", weights + 18 * KB, [P, 2, DC, P])
        xn3 = view(scratch, 0, 2, D)
        attn = view(scratch, 2 * D, 2, P)
        attnT = view(scratch, 3 * D, 2, P)
        xn4 = view(scratch, 4 * D, 2, D)
        smax = sb("smax", [P, 2, 2])
        inv_sum = sb("inv_sum", [P, 2])
        bst34 = sb("bst34", [P, 2, 6])
        bag34 = sb("bag34", [P, 2, 2, 2])
        veps34 = sb("veps34", [P, 2, 2])
        rstd34 = sb("rstd34", [P, 2, 2])
        b1_cur = sb("b1_cur", [P, 2, FC])
        affine = sb("affine", [P, 2, DC])
        yb = place("yb", weights, [P, 2 * G, D])
        zn = place("zn", weights + 8 * KB, [P, 2 * G, D])
        a_f = place("a_f", weights + 16 * KB, [P, 2, DC, GT])
        w2c_hi = place("w2c_hi", weights + 24 * KB, [P, DC, D], F32R)
        w2c_lo = place("w2c_lo", weights + 26 * KB, [P, DC, D], F32R)
        hg_hi = place("hg_hi", mixed, [P, 2, DC, GT], F32R)
        hg_lo = place("hg_lo", mixed + 8 * KB, [P, 2, DC, GT], F32R)
        a_hi = place("a_hi", raw, [P, 2, DC, GT], F32R)
        a_lo = place("a_lo", raw + 8 * KB, [P, 2, DC, GT], F32R)
        bst5 = sb("bst5", [P, G, 6])
        bag5 = sb("bag5", [P, 2, G, 2])
        veps5 = sb("veps5", [P, 2, G])
        rstd5 = sb("rstd5", [P, 2, G])
        shift5 = sb("shift5", [P, 2, G])
        o_sb = place("o_sb", features + 16 * KB, [P, NB, D])

        bank = [stack.enter_context(nc.psum_tensor(f"bank{i}", [P, 512], F32)) for i in range(8)]

        x_in = [sem(f"x_in{g}") for g in range(NG)]
        ctx_in = [sem(f"ctx_in{g}") for g in range(NG)]
        gk_in, rows_in, router_in, attnw_in, ffnw_in, b2_in, biasrow_in = (
            sem(n) for n in ("gk_in", "rows_in", "router_in", "attnw_in", "ffnw_in", "b2_in", "biasrow_in"))
        q_in = sem("q_in")
        w1_in, w2_in = sem("w1_in"), sem("w2_in")
        w1_hi_ready, w1_lo_ready, w2_hi_ready, w2_lo_ready = (
            sem(n) for n in ("w1_hi_ready", "w1_lo_ready", "w2_hi_ready", "w2_lo_ready"))
        slots_zeroed = sem("slots_zeroed")
        xin_in = [sem(f"xin_in{j}") for j in range(2)]
        y_out = [sem(f"y_out{j}") for j in range(2)]
        scattered = [sem(f"scattered{j}") for j in range(8)]
        gathered = [sem(f"gathered{j}") for j in range(4)]
        out_done = sem("out_done")
        consts = sem("consts")
        pool_step, dve_step = sem("pool_step"), sem("dve_step")
        dve_consts, cols_turned, cols_ready = sem("dve_consts"), sem("cols_turned"), sem("cols_ready")
        xvar_ready, xrstd_ready, xn_ready = sem("xvar_ready"), sem("xrstd_ready"), sem("xn_ready")
        x_turned, x_copied = sem("x_turned"), sem("x_copied")
        ctx_turned, ctx_copied = sem("ctx_turned"), sem("ctx_copied")
        gkctx_ready, gates_done, gates_copied = sem("gkctx_ready"), sem("gates_done"), sem("gates_copied")
        gates_tok_done, gates_tok_copied, gates_turned, unscaled_ready, split_ready = (
            sem(n) for n in ("gates_tok_done", "gates_tok_copied", "gates_turned", "unscaled_ready", "split_ready"))
        fabs_ready, fexp_ready, fln_ready, gsum_ready, lim_ready = (
            sem(n) for n in ("fabs_ready", "fexp_ready", "fln_ready", "gsum_ready", "lim_ready"))
        negmax_ready, glim_turned, glim_copied = sem("negmax_ready"), sem("glim_turned"), sem("glim_copied")
        lb_turned, lb_copied, wdeq_ready, wT_done, wT_copied = (
            sem(n) for n in ("lb_turned", "lb_copied", "wdeq_ready", "wT_done", "wT_copied"))
        vT_done, vT_copied = sem("vT_done"), sem("vT_copied")
        qblk_ready, vaug_ready = [sem("qblk_even"), sem("qblk_odd")], sem("vaug_ready")
        maxb_done, qk_done, exp_done, qblk_zeroed, c_ready, cv_done, heads_copied = (
            sem(n) for n in ("maxb_done", "qk_done", "exp_done", "qblk_zeroed", "c_ready", "cv_done", "heads_copied"))
        sq_ready, ms_ready, rms_ready, yh_ready, var2_ready, rstd2_ready, xn2_ready = (
            sem(n) for n in ("sq_ready", "ms_ready", "rms_ready", "yh_ready", "var2_ready", "rstd2_ready", "xn2_ready"))
        xn2_turned, xn2T_copied, logits_done, logits_read, mask_ready, rank_done, rank_read, dest_ready = (
            sem(n) for n in ("xn2_turned", "xn2T_copied", "logits_done", "logits_read", "mask_ready",
                             "rank_done", "rank_read", "dest_ready"))
        topdiff_ready, topexp_ready = sem("topdiff_ready"), sem("topexp_ready")
        vtok_copied = sem("vtok_copied")
        xin_turned, xT_hi_ready, xT_lo_ready, h_done, relu_ready, y_done, y_ready = (
            sem(n) for n in ("xin_turned", "xT_hi_ready", "xT_lo_ready", "h_done", "relu_ready", "y_done", "y_ready"))
        h_hi_act, h_hi_dve, h_lo_ready = sem("h_hi_act"), sem("h_hi_dve"), sem("h_lo_ready")
        gath_zeroed, x2_ready, wtop_ready = sem("gath_zeroed"), sem("x2_ready"), sem("wtop_ready")
        var34_ready, rstd34_ready, xn3_ready, xn3_turned, xn3T_copied, q_done, q_copied = (
            sem(n) for n in ("var34_ready", "rstd34_ready", "xn3_ready", "xn3_turned", "xn3T_copied", "q_done", "q_copied"))
        score_done, smax_ready, attn_ready, attn_turned, attnT_copied, ctxv_done = (
            sem(n) for n in ("score_done", "smax_ready", "attn_ready", "attn_turned", "attnT_copied", "ctxv_done"))
        x3_ready, xn4_ready, xn4_turned, h_ready = (
            sem(n) for n in ("x3_ready", "xn4_ready", "xn4_turned", "h_ready"))
        wT_lo_ready, hg_hi_ready, hg_lo_ready, a_hi_ready, a_lo_ready, shift5_ready = (
            sem(n) for n in ("wT_lo_ready", "hg_hi_ready", "hg_lo_ready", "a_hi_ready", "a_lo_ready", "shift5_ready"))
        zn_last_ready = sem("zn_last_ready")
        w2cur_ready, yf_done, yb_ready, var5_ready, rstd5_ready, zn_ready, zn_turned, a_ready, y2_done = (
            sem(n) for n in ("w2cur_ready", "yf_done", "yb_ready", "var5_ready", "rstd5_ready", "zn_ready",
                             "zn_turned", "a_ready", "y2_done"))
        b1_ready, affine_ready, memset_done = sem("b1_ready"), sem("affine_ready"), sem("memset_done")
        fin_turned, fin_ready = sem("fin_turned"), sem("fin_ready")

        LAST = NB + 8
        block = stack.enter_context(nc.Block())

        @block.sync
        def _(sp):
            xv = x.rearrange("t p d -> p t d")
            cv = ctx.rearrange("t p d -> p t d")
            for g in range(NG):
                sp.dma_start(xres[:, g * G:(g + 1) * G, :], xv[:, g * G:(g + 1) * G, :]).then_inc(x_in[g], 16)
                sp.dma_start(ctx_tok[:, g * G:(g + 1) * G, :], cv[:, g * G:(g + 1) * G, :]).then_inc(ctx_in[g], 16)
            for at, src in ((B1, b1), (GA, ln_gamma), (BE, ln_beta), (BI, biases)):
                n = src.shape[0] * src.shape[1] // P
                sp.dma_start(rows[at:at + n, :], src.rearrange("n (c p) -> (n c) p", p=P)).then_inc(rows_in, 16)
            sp.dma_start(rows[BQ:BQ + DC, :], bq.rearrange("(c p) -> c p", p=P)).then_inc(rows_in, 16)
            sp.dma_start(rows[BV:BV + DC, :], bv.rearrange("(c p) -> c p", p=P)).then_inc(rows_in, 16)
            sp.dma_start(la_sb[:, :, :], lora_a.rearrange("l r d -> r l d")).then_inc(ffnw_in, 16)
            sp.dma_start(lb_sb[:, :, :, :].rearrange("p l c r -> p (l c) r"),
                         lora_b.rearrange("l (c p) r -> p (l c) r", p=P)).then_inc(ffnw_in, 16)
            sp.dma_start(scale_sb[:, :, :, :].rearrange("p l c s -> p (l c) s"),
                         scales.rearrange("l (c p) s -> p (l c) s", p=P)).then_inc(ffnw_in, 16)
            sp.dma_start(router_w[:, :, :], gate_w.rearrange("(c p) e -> p c e", p=P)).then_inc(router_in, 16)
            sp.dma_start(router_b[:, :], gate_b.partition_broadcast(P)).then_inc(router_in, 16)
            sp.dma_start(wq_sb[:, :, :], Wq.rearrange("(c p) n -> p c n", p=P)).then_inc(attnw_in, 16)
            sp.dma_start(wv_sb[:, :, :], Wv.rearrange("(c p) n -> p c n", p=P)).then_inc(attnw_in, 16)
            sp.dma_start(b2_row[:, :, :], b2.partition_broadcast(P)).then_inc(b2_in, 16)
            sp.dma_start(bias_row[:, :, :],
                          biases.rearrange("(n two) d -> n two d", two=2)[:, 0, :].partition_broadcast(P)
                          ).then_inc(biasrow_in, 16)

            for l in range(NL):
                sp.dma_start(wraw[:, l, :, :], qweights[l].rearrange("(c p) d -> p c d", p=P)).then_inc(q_in, 16)

            def load_w1(e):
                sp.dma_start(w1_raw[:, :, :], w1[bass.ds(e, 1)].rearrange("a (c p) f -> p (a c) f", p=P)).then_inc(w1_in, 16)

            def load_w2(e):
                sp.dma_start(w2_raw[:, :, :], w2[bass.ds(e, 1)].rearrange("a (c p) d -> p (a c) d", p=P)).then_inc(w2_in, 16)

            load_w1(0)
            load_w2(0)

            def load_slots(e, j):
                rows_e = slots_dram[bass.ds(e * CAP, CAP), :]
                sp.dma_start(xin[:, j, 0:MT - 1, :],
                             rows_e[0:(MT - 1) * P, :].rearrange("(m p) d -> p m d", p=P)).then_inc(xin_in[j], 16)
                sp.dma_start(xin[0:MTAIL, j, MT - 1, :], rows_e[(MT - 1) * P:CAP, :]).then_inc(xin_in[j], 16)

            def store_rows(e, j):
                rows_e = experts_dram[bass.ds(e * CAP, CAP), :]
                sp.wait_ge(y_ready, MT * e + MT)
                sp.dma_start(rows_e[0:(MT - 1) * P, :].rearrange("(m p) d -> p m d", p=P),
                             y_sb[:, j, 0:MT - 1, :]).then_inc(y_out[j], 16)
                sp.dma_start(rows_e[(MT - 1) * P:CAP, :], y_sb[0:MTAIL, j, MT - 1, :]).then_inc(y_out[j], 16)

            def next_w1(e):
                sp.wait_ge(w1_lo_ready, DC * e)
                load_w1(e)

            def next_w2(e):
                sp.wait_ge(w2_lo_ready, 2 * e)
                load_w2(e)

            for j in range(8):
                sp.wait_ge(scattered[j], 32 * (NB // 8))
            for e in range(2):
                load_slots(e, e)
            next_w1(1)

            def expert(e, j, slots=True, w1_too=True, w2_too=True):
                if w2_too:
                    next_w2(e + 1)
                if w1_too:
                    next_w1(e + 2)
                if slots:
                    sp.wait_ge(xin_turned, DC * e + DC)
                    load_slots(e + 2, j)
                store_rows(e, j)

            with sp.Fori(0, E // 2 - 1) as k:
                for j in range(2):
                    expert(2 * k + j, j)
            expert(E - 2, 0, slots=False, w1_too=False)
            expert(E - 1, 1, slots=False, w1_too=False, w2_too=False)
            ov = out.rearrange("t p d -> p t d")
            for g in range(NG - 1):
                sp.wait_ge(fin_ready, G * (g + 1))
                sp.dma_start(ov[:, g * G:(g + 1) * G, :], o_sb[:, g * G:(g + 1) * G, :]).then_inc(out_done, 16)
            for k in range(2):
                t = NB - G + k * G // 2
                sp.wait_ge(fin_ready, t + G // 2)
                sp.dma_start(ov[:, t:t + G // 2, :], o_sb[:, t:t + G // 2, :]).then_inc(out_done, 16)
            sp.wait_ge(out_done, 16 * (NG + 1))

        @block.gpsimd
        def _(pool):
            steps = [0]

            def link(ins):
                steps[0] += 1
                ins.then_inc(pool_step, 1)
                pool.wait_ge(pool_step, steps[0])

            pool.memset(ident[:, :], 0.0).then_inc(pool_step, 1)
            pool.memset(tri_bf[:, :], 1.0).then_inc(pool_step, 1)
            steps[0] += 2
            pool.wait_ge(pool_step, 2)
            pool.affine_select(out=ident[:, :], in_=ident[:, :], compare_op=ALU.not_equal, fill=1.0,
                               base=0, pattern=[[-1, P]], channel_multiplier=1).then_inc(consts, 1)
            pool.memset(zero_row[:, :], 0.0).then_inc(consts, 1)
            pool.memset(mhalf[:, :], -0.5).then_inc(consts, 1)
            pool.affine_select(out=tri_bf[:, :], in_=tri_bf[:, :], compare_op=ALU.is_ge, fill=0.0,
                               base=0, pattern=[[1, P]], channel_multiplier=-1).then_inc(consts, 1)
            pool.memset(ones_bf[:, :], 1.0).then_inc(consts, 1)
            pool.memset(ones[:, :], 1.0).then_inc(consts, 1)
            pool.memset(v_aug[:, :, :, :], 1.0).then_inc(consts, 1)
            pool.iota(expert_no_i[:, :], pattern=[[1, E]], base=0, channel_multiplier=0).then_inc(consts, 1)
            pool.memset(causal_bf[:, :, :], 0.0).then_inc(consts, 1)
            pool.memset(ident_bf[:, :], 0.0).then_inc(consts, 1)
            pool.wait_ge(consts, 10)
            pool.affine_select(out=causal_bf[:, :, :], in_=causal_bf[:, :, :], compare_op=ALU.is_ge, fill=MASKED,
                               base=0, pattern=[[0, HU], [1, P]], channel_multiplier=-1).then_inc(consts, 1)
            pool.affine_select(out=ident_bf[:, :], in_=ident_bf[:, :], compare_op=ALU.not_equal, fill=1.0,
                               base=0, pattern=[[-1, P]], channel_multiplier=1).then_inc(consts, 1)
            for g in range(NG):
                pool.wait_ge(xvar_ready, g + 1)
                pool.tensor_tensor(rstd[:, g * G:(g + 1) * G], veps[:, g * G:(g + 1) * G],
                                   mhalf[:, 0:G], ALU.pow).then_inc(xrstd_ready, 1)
            pool.wait_ge(ctx_in[NG - 1], 16)
            pool.dma_start(slots_dram.rearrange("(p r) d -> p r d", p=P),
                           zero_row[:, :].unsqueeze(1).to_broadcast([P, SLOTS // P, D])).then_inc(slots_zeroed, 16)
            pool.wait_ge(q_in, 16 * NL)
            for l in range(NL):
                pool.tensor_scalar(wdeq[:, l, :, :], wraw[:, l, :, :], 1.0 / LEVELS, -1.0,
                                   ALU.mult, ALU.add).then_inc(unscaled_ready, 1)

            pool.wait_ge(slots_zeroed, 16)

            def head_rms(b):
                pool.wait_ge(ms_ready, b + 1)
                pool.tensor_tensor(small[:, 4 + b % 2, :], small[:, 2 + b % 2, :], mhalf[:, 0:NH],
                                   ALU.pow).then_inc(rms_ready, 1)

            def norm2(b):
                pool.wait_ge(var2_ready, b + 1)
                pool.tensor_tensor(rstd2[:, b % 2:b % 2 + 1], veps2[:, b % 2:b % 2 + 1], mhalf[:, 0:1],
                                   ALU.pow).then_inc(rstd2_ready, 1)

            def scatter(b):
                pool.wait_ge(dest_ready, b // 2 + 1)
                for k in range(TOP_K):
                    pool.indirect_dma_start(
                        out=slots_dram[:, :],
                        out_offset=bass.IndirectOffsetOnAxis(ap=dest[:, b, k:k + 1], axis=0),
                        in_=xn2[:, b % 8, :], in_offset=None,
                        bounds_check=SLOTS - 1, oob_is_err=False).then_inc(scattered[b % 8], 16)

            for i in range(LAST):
                if 2 <= i < NB + 2:
                    head_rms(i - 2)
                if 3 <= i < NB + 3:
                    norm2(i - 3)
                if 7 <= i < NB + 7:
                    scatter(i - 7)

            def split_w2(e):
                for k in range(2):
                    pool.wait_ge(w2_hi_ready, 2 * e + (k + 1))
                    half = slice(k * H2, (k + 1) * H2)
                    pool.tensor_tensor(w2_lo[:, half, :], w2_raw[:, half, :], w2_hi[:, half, :].bitcast(F32),
                                       ALU.subtract).then_inc(w2_lo_ready, 1)

            with pool.Fori(0, E) as e:
                split_w2(e)

            pool.wait_ge(gath_zeroed, 1)
            for j in range(2):
                pool.wait_ge(y_out[j], 32 * (E // 2))

            def gather(b):
                if b >= 4:
                    pool.wait_ge(x2_ready, b - 3)
                for k in range(TOP_K):
                    pool.indirect_dma_start(
                        out=gath[:, b % 4, k, :], out_offset=None, in_=experts_dram[:, :],
                        in_offset=bass.IndirectOffsetOnAxis(ap=dest[:, b, k:k + 1], axis=0),
                        bounds_check=SLOTS - 1, oob_is_err=False).then_inc(gathered[b % 4], 16)

            for b in range(3):
                gather(b)
            def split_h(q, g, halves=(0, 1)):
                for c in halves:
                    pool.wait_ge(hg_hi_ready, DC * q + (c + 1))
                    pool.tensor_tensor(hg_lo[:, g % 2, c, :], hT[:, c, g * GT:(g + 1) * GT],
                                       hg_hi[:, g % 2, c, :].bitcast(F32), ALU.subtract).then_inc(hg_lo_ready, 1)

            for i in range(NB + TO_ATTEND):
                pool.wait_ge(var34_ready, i + 1)
                pool.tensor_tensor(rstd34[:, i % 2, :], veps34[:, i % 2, :], mhalf[:, 0:2],
                                   ALU.pow).then_inc(rstd34_ready, 1)
                if i + 3 < NB:
                    gather(i + 3)
                if i == NB - 2:
                    split_h(0, 0)
                if i == NB:
                    split_h(1, 1)
            def roots5(n, g):
                pool.wait_ge(var5_ready, n + 1)
                pool.tensor_tensor(rstd5[:, g % 2, :], veps5[:, g % 2, :], mhalf[:, 0:G],
                                   ALU.pow).then_inc(rstd5_ready, 1)

            def normalise_last(n, g):
                if isinstance(n, int):
                    pool.wait_ge(shift5_ready, n + 1)
                    if n >= 2:
                        pool.wait_ge(zn_turned, DC * n - DC)
                at = (g % 2) * G + G - 1
                pool.tensor_scalar(zn[:, at, :], yb[:, at, :], rstd5[:, g % 2, G - 1:G], shift5[:, g % 2, G - 1:G],
                                   ALU.mult, ALU.add).then_inc(zn_last_ready, 1)

            def block_steps(blk, last):
                for g in range(NG):
                    n = NG * blk + g
                    if not last or g == 0:
                        pool.wait_ge(shift5_ready, n + 2)
                        split_h(n + 3, (g + 3) % NG, (0,))
                    if not last or g + 1 < NG:
                        normalise_last(n + 1, (g + 1) % NG)
                    if not last or g == 0:
                        split_h(n + 3, (g + 3) % NG, (1,))
                    if not last or g + 2 < NG:
                        roots5(n + 2, g)

            roots5(0, 0)
            normalise_last(0, 0)
            split_h(2, 2)
            roots5(1, 1)
            with pool.Fori(0, NBLK - 1) as blk:
                block_steps(blk, False)
            block_steps(NBLK - 1, True)

        @block.scalar
        def _(act):
            act.dma_start(gk_raw[:, :, 0:NH], igate_kernel.rearrange("(c p) h -> p c h", p=P)).then_inc(gk_in, 16)
            act.dma_start(gk_raw[:, :, NH:2 * NH], fgate_kernel.rearrange("(c p) h -> p c h", p=P)).then_inc(gk_in, 16)
            act.dma_start(gate_bias[0:NH, :], igate_bias.unsqueeze(1)).then_inc(gk_in, 16)
            act.dma_start(gate_bias[NH:2 * NH, :], fgate_bias.unsqueeze(1)).then_inc(gk_in, 16)

            def copy_ctx(t):
                act.wait_ge(ctx_turned, t + 1)
                nc.scalar.copy(ctxT[:, :, t * P:(t + 1) * P],
                               bank[2 + t % 2][:, 0:D].rearrange("p (c s) -> p c s", c=DC)).then_inc(ctx_copied, 1)

            def copy_xT(t):
                act.wait_ge(x_turned, t + 1)
                nc.scalar.copy(xnT[:, :, t * P:(t + 1) * P],
                               bank[t % 2][:, 0:D].rearrange("p (c s) -> p c s", c=DC)).then_inc(x_copied, 1)

            def copy_gates(g):
                act.wait_ge(gates_done, g + 1)
                if g == 0:
                    act.wait_ge(gk_in, 64)
                else:
                    act.wait_ge(gates_tok_done, G * max(g - 1, 1))
                nc.scalar.activation(gates_sb[:, g % 2, :], bank[4 + g % 2][0:2 * NH, :],
                                     ACT.Identity, bias=gate_bias[:, 0:1]).then_inc(gates_copied, 1)

            for t in range(NB):
                copy_ctx(t)
                copy_xT(t)
                if t % G == 1 and t > 2 * G:
                    copy_gates(t // G - 2)
            copy_gates(NG - 2)
            copy_gates(NG - 1)

            def lora(l):
                act.wait_ge(lb_turned, l + 1)
                if l >= 2:
                    act.wait_ge(wT_done, l - 1)
                nc.scalar.copy(lbT[:, l % 2, :], bank[2 + l % 2][0:R, 0:D]).then_inc(lb_copied, 1)

            def ffn_weight(l):
                act.wait_ge(wT_done, l + 1)
                nc.scalar.copy(wT_hi[:, l, :, :], bank[l % 2][:, :].rearrange("p (c n) -> p c n", c=DC)).then_inc(wT_copied, 1)

            def v_with_ones(b):
                if b >= 2:
                    act.wait_ge(cv_done, 2 * (b - 1))
                act.wait_ge(consts, 12)
                nc.scalar.copy(v_aug[:, b % 2, :, 0:HD],
                               ctx_tok[:, b, :].rearrange("p (h d) -> p h d", h=NH)).then_inc(vaug_ready, 1)

            def query_blocks(u):
                b, c = u // 2, u % 2
                if u >= 4:
                    act.wait_ge(qk_done, u - 3)
                elif u == 0:
                    act.wait_ge(qblk_zeroed, 2)
                    act.wait_ge(x_copied, NB)
                for h in range(HU):
                    ins = nc.scalar.mul(qblk[h * HD:(h + 1) * HD, u % 4, h, :],
                                        xnT[h * HD:(h + 1) * HD, c, b * P:(b + 1) * P], float(HD) ** -0.5)
                ins.then_inc(qblk_ready[0], 1)

            act.wait_ge(fabs_ready, 1)
            nc.scalar.activation(gsc[:, 3, :], gsc[:, 2, :], ACT.Exp).then_inc(fexp_ready, 1)
            act.wait_ge(fexp_ready, 1)
            nc.scalar.activation(gsc[:, 4, :], gsc[:, 3, :], ACT.Ln, bias=1.0).then_inc(fln_ready, 1)
            v_with_ones(0)
            query_blocks(0)
            act.wait_ge(gsum_ready, 1)
            nc.scalar.activation(gsc[:, 0, :], gsc[:, 7, :], ACT.Exp, scale=-1.0).then_inc(lim_ready, 1)

            def decays(u):
                b = u // 2
                act.wait_ge(maxb_done, u + 1)
                act.wait_ge(glim_copied, 1)
                if u >= 2:
                    act.wait_ge(c_ready, u - 1)
                for h in range(HU):
                    col = (HU * (u % 2) + h) * NB + b
                    nc.scalar.activation(decay[:, u % 2, h, :], bank[u % 2][:, h * P:(h + 1) * P], ACT.Exp,
                                         bias=gT[:, col:col + 1]).then_inc(exp_done, 1)

            def heads_from_psum(b):
                act.wait_ge(cv_done, 2 * b + 2)
                if b >= 2:
                    act.wait_ge(yh_ready, b - 1)
                nc.scalar.copy(heads_out[:, b % 2, :, :],
                               bank[4 + b % 2][:, 0:NH * HA].rearrange("p (h d) -> p h d", h=NH)).then_inc(heads_copied, 1)
                act.wait_ge(heads_copied, b + 1)
                if b >= 1:
                    act.wait_ge(ms_ready, b)
                nc.scalar.activation(sq[:, :, :], heads_out[:, b % 2, :, 0:HD], ACT.Square,
                                     scale=float(HD) ** -0.5).then_inc(sq_ready, 1)

            def copy_xn2T(b):
                act.wait_ge(xn2_turned, b + 1)
                if b >= 2:
                    act.wait_ge(logits_done, b - 1)
                nc.scalar.copy(xn2T[:, b % 2, :, :], bank[6][:, 0:D].rearrange("p (c s) -> p c s", c=DC)).then_inc(xn2T_copied, 1)

            def w1_first(e):
                act.wait_ge(w1_in, 16 * e + 16)
                if isinstance(e, int) and e == 0:
                    act.wait_ge(cv_done, 2 * NB)
                else:
                    act.wait_ge(h_done, FC * e)
                for c in range(DC):
                    nc.scalar.copy(w1_hi[:, c, :], w1_raw[:, c, :]).then_inc(w1_hi_ready, 1)

            for i in range(LAST):
                if 2 <= i < NB + 2:
                    heads_from_psum(i - 2)
                if i < NB:
                    decays(2 * i)
                if i + 1 < NB:
                    query_blocks(2 * i + 2)
                if i < NB:
                    decays(2 * i + 1)
                if 4 <= i < NB + 4:
                    copy_xn2T(i - 4)
                if i + 1 < NB:
                    v_with_ones(i + 1)
                if i == NB:
                    lora(0)
                    lora(1)
                elif NB < i <= NB + 3:
                    ffn_weight(i - NB - 1)
                    if i <= NB + 2:
                        lora(i - NB + 1)
                if i == NB + 5:
                    w1_first(0)
            act.wait_ge(topdiff_ready, 1)
            nc.scalar.activation(wtop[:, :, 0], wtop[:, :, 1], ACT.Exp).then_inc(topexp_ready, 1)
            for l in range(3, NL):
                if l + 1 < NL:
                    lora(l + 1)
                ffn_weight(l)

            def slots_hi(e):
                for c in range(DC):
                    act.wait_ge(xin_turned, DC * e + (c + 1))
                    nc.scalar.copy(xT_hi[:, c, :], bank[4 + c][:, 0:CAP]).then_inc(xT_hi_ready, 1)

            def w2_first(e, k):
                act.wait_ge(w2_in, 16 * e + 16)
                if k == 0:
                    if isinstance(e, int) and e == 0:
                        act.wait_ge(logits_done, NB)
                    else:
                        act.wait_ge(y_done, MT * e)
                half = slice(k * H2, (k + 1) * H2)
                nc.scalar.copy(w2_hi[:, half, :], w2_raw[:, half, :]).then_inc(w2_hi_ready, 1)

            def hidden(e, j):
                act.wait_ge(b1_ready, e + 1)
                for f in range(FC):
                    act.wait_ge(h_done, FC * e + (f + 1))
                    if not isinstance(e, int) or e or f >= 4:
                        act.wait_ge(h_lo_ready, FC * e + (f + 1) - 4)
                    nc.scalar.activation(h_ring[:, f % 4, :], bank[f % 4][:, 0:CAP], ACT.Relu,
                                         bias=b1_cur[:, j, f:f + 1]).then_inc(relu_ready, 1)
                    if f % 4 == 3:
                        act.wait_ge(relu_ready, FC * e + (f + 1))
                        nc.scalar.copy(h_hi[:, f, :], h_ring[:, f % 4, :]).then_inc(h_hi_act, 1)
                    if f == 1:
                        w2_first(e, 1)

            def expert(e, j, follows=True):
                w2_first(e, 0)
                hidden(e, j)
                if follows:
                    slots_hi(e + 1)
                    w1_first(e + 1)

            slots_hi(0)
            expert(0, 0)
            expert(1, 1)
            with act.Fori(1, E // 2 - 1) as k:
                for j in range(2):
                    expert(2 * k + j, j)
            expert(E - 2, 0)
            expert(E - 1, 1, follows=False)

            def split_h(q, g, source):
                act.wait_ge(h_ready, source)
                if not isinstance(q, int) or q >= 2:
                    act.wait_ge(yf_done, G * q - G)
                for c in range(DC):
                    nc.scalar.copy(hg_hi[:, g % 2, c, :], hT[:, c, g * GT:(g + 1) * GT]).then_inc(hg_hi_ready, 1)

            def copy_vT(n):
                g, o = n // DC, n % DC
                act.wait_ge(vT_done, n + 1)
                act.wait_ge(cols_ready, 1)
                nc.scalar.activation(vT[:, o, g * GT:(g + 1) * GT], bank[7][:, :], ACT.Identity,
                                     bias=cols[:, BV + o:BV + o + 1]).then_inc(vT_copied, 1)

            copy_vT(0)
            copy_vT(1)
            for j in range(2):
                act.wait_ge(y_out[j], 32 * (E // 2))
            for i in range(NB + TO_NORM):
                if i % 2 == 1 and 3 <= i <= NB - G + 1:
                    copy_vT(i // 2 + 1)
                if TO_SCORE <= i < NB + TO_SCORE:
                    b = i - TO_SCORE
                    act.wait_ge(smax_ready, b + 1)
                    if b >= 2:
                        act.wait_ge(attn_turned, b - 1)
                    nc.scalar.activation(attn[:, b % 2, :], bank[b % 2][:, 0:P], ACT.Exp,
                                         bias=smax[:, 0, b % 2:b % 2 + 1],
                                         accum_out=smax[:, 1, b % 2:b % 2 + 1]).then_inc(attn_ready, 1)
                if 2 <= i < NB + 2:
                    b = i - 2
                    act.wait_ge(q_done, b + 1)
                    if b >= 2:
                        act.wait_ge(score_done, b - 1)
                    for o in range(DC):
                        nc.scalar.activation(qT[:, b % 2, o, :], bank[6][:, o * P:(o + 1) * P], ACT.Identity,
                                             bias=cols[:, BQ + o:BQ + o + 1]).then_inc(q_copied, 1)
                    nc.scalar.copy(v_tok[:, b, :], bank[6][:, D:2 * D]).then_inc(vtok_copied, 1)
                if 1 <= i <= NB:
                    b = i - 1
                    act.wait_ge(xn3_turned, b + 1)
                    if b >= 2:
                        act.wait_ge(q_done, b - 1)
                    nc.scalar.copy(xn3T[:, b % 2, :, :],
                                   bank[4][:, 0:D].rearrange("p (c s) -> p c s", c=DC)).then_inc(xn3T_copied, 1)
                if TO_SCORE <= i < NB + TO_SCORE:
                    b = i - TO_SCORE
                    act.wait_ge(attn_turned, b + 1)
                    if b >= 2:
                        act.wait_ge(ctxv_done, b - 1)
                    nc.scalar.copy(attnT[:, b % 2, :], bank[2][:, 0:P]).then_inc(attnT_copied, 1)
                if TO_NORM <= i:
                    b = i - TO_NORM
                    act.wait_ge(xn4_turned, b + 1)
                    nc.scalar.copy(hT[:, :, b * P:(b + 1) * P],
                                   bank[5][:, 0:D].rearrange("p (c s) -> p c s", c=DC)).then_inc(h_ready, 1)
                    if b == G or b == 2 * G:
                        split_h(b // G - 1, b // G - 1, b)

            def normalise(n, g):
                act.wait_ge(shift5_ready, n + 1)
                for t in range(G - 1):
                    nc.scalar.activation(zn[:, (g % 2) * G + t, :], yb[:, (g % 2) * G + t, :], ACT.Identity,
                                         bias=shift5[:, g % 2, t:t + 1],
                                         scale=rstd5[:, g % 2, t:t + 1]).then_inc(zn_ready, 1)

            def gelu(n, g, c):
                act.wait_ge(zn_turned, DC * n + (c + 1))
                nc.scalar.activation(a_f[:, g % 2, c, :], bank[2 + c][:, :], ACT.Gelu,
                                     bias=affine[:, 1, c:c + 1],
                                     scale=affine[:, 0, c:c + 1]).then_inc(a_ready, 1)

            def round_a(n, g, c):
                act.wait_ge(a_ready, DC * n + (c + 1))
                nc.scalar.copy(a_hi[:, g % 2, c, :], a_f[:, g % 2, c, :]).then_inc(a_hi_ready, 1)

            def block_steps(blk, last):
                for g in range(NG):
                    n = NG * blk + g
                    if g == 0:
                        act.wait_ge(affine_ready, 2 * blk + 2)
                    for c in range(DC):
                        gelu(n, g, c)
                        round_a(n, g, c)
                    if not last or g == 0:
                        split_h(n + 3, (g + 3) % NG, NB + DC * n)
                    if not last or g + 1 < NG:
                        normalise(n + 1, (g + 1) % NG)

            act.wait_ge(x2_ready, NB)
            split_h(2, 2, 3 * G)
            normalise(0, 0)
            with act.Fori(0, NBLK - 1) as blk:
                block_steps(blk, False)
            block_steps(NBLK - 1, True)

        @block.vector
        def _(dve):
            steps = [0]
            vec = nc.vector

            def step(ins):
                steps[0] += 1
                ins.then_inc(dve_step, 1)

            def settle():
                dve.wait_ge(dve_step, steps[0])

            def link(ins):
                step(ins)
                settle()

            dve.wait_ge(consts, 12)
            i3 = ident[:, :].rearrange("p (h b) -> p h b", h=NH)
            vec.tensor_reduce(head_sel_p[:, :], i3, AX.X, ALU.add).then_inc(dve_consts, 1)
            link(vec.tensor_reduce(seq_sel_f[:, :], ident[:, :].rearrange("p (h b) -> p b h", h=NH), AX.X, ALU.add))
            vec.tensor_copy(seq_sel[:, :], seq_sel_f[:, :]).then_inc(dve_consts, 1)
            vec.tensor_copy(expert_no[:, :], expert_no_i[:, :]).then_inc(dve_consts, 1)

            def norm1(t):
                dve.wait_ge(xrstd_ready, t // G + 1)
                if t >= 4:
                    dve.wait_ge(x_turned, t - 3)
                vec.tensor_scalar(xn[:, t % 4, :], xres[:, t, :], bag[:, t, 0:1], rstd[:, t:t + 1],
                                  ALU.subtract, ALU.mult).then_inc(xn_ready, 1)

            def stats1(g):
                dve.wait_ge(x_in[g], 16)
                for t in range(g * G, (g + 1) * G):
                    step(vec.bn_stats(bst[:, t, :], xres[:, t, :]))
                settle()
                for t in range(g * G, (g + 1) * G):
                    step(vec.bn_aggr(bag[:, t, :], bst[:, t, :]))
                settle()
                vec.tensor_scalar(veps[:, g * G:(g + 1) * G], bag[:, g * G:(g + 1) * G, 1], LN_EPS, None,
                                  ALU.add).then_inc(xvar_ready, 1)

            stats1(0)
            link(vec.tensor_scalar(head_sel[:, :], head_sel_p[:, :], -1.0, None, ALU.mult))
            for g in range(NG):
                if g + 1 < NG:
                    stats1(g + 1)
                for t in range(g * G, (g + 1) * G):
                    norm1(t)
                if g == 0:
                    dve.wait_ge(gk_in, 64)
                    vec.tensor_tensor(gk_ctx[:, :, :], gk_raw[:, DC:2 * DC, :], gk_raw[:, 2 * DC:3 * DC, :],
                                      ALU.add).then_inc(gkctx_ready, 1)
            vec.memset(qblk[:, 0:2, :, :], 0.0).then_inc(qblk_zeroed, 1)
            dve.wait_ge(cols_turned, 1)
            vec.tensor_copy(cols[:, :], bank[6][:, 0:NROWS]).then_inc(cols_ready, 1)
            dve.wait_ge(x_turned, NB)
            vec.memset(qblk[:, 2:4, :, :], 0.0).then_inc(qblk_zeroed, 1)
            dve.wait_ge(gates_tok_done, NB)
            vec.tensor_copy(gates_tok[:, :, :],
                            bank[7][:, 0:2 * NH * NB].rearrange("p (b k) -> p k b", b=NB)).then_inc(gates_tok_copied, 1)

            def dequant(l):
                dve.wait_ge(unscaled_ready, l + 1)
                if l == 0:
                    dve.wait_ge(ffnw_in, 48)
                w4 = wdeq[:, l, :, :].rearrange("p c (s g) -> p (c s) g", g=GROUP)
                vec.tensor_tensor(w4, w4, scale_sb[:, l, :, :].rearrange("p c s -> p (c s)").unsqueeze(2)
                                  .to_broadcast([P, DC * NS, GROUP]), ALU.mult).then_inc(wdeq_ready, 1)

            def query_blocks(u, which):
                b, c = u // 2, u % 2
                if u >= 4:
                    dve.wait_ge(qk_done, u - 3)
                for h in which:
                    ins = vec.tensor_scalar(qblk[h * HD:(h + 1) * HD, u % 4, h, :],
                                            xnT[h * HD:(h + 1) * HD, c, b * P:(b + 1) * P],
                                            float(HD) ** -0.5, None, ALU.mult)
                    if h == HU - 1:
                        ins.then_inc(qblk_ready[1], 1)

            def weigh(u):
                dve.wait_ge(qk_done, u + 1)
                dve.wait_ge(exp_done, HU * (u + 1))
                if u >= 2:
                    dve.wait_ge(cv_done, u - 1)
                vec.tensor_tensor(cmat[:, u % 2, :, :].rearrange("p h s -> p (h s)"), bank[2 + u % 2][:, :],
                                  decay[:, u % 2, :, :].rearrange("p h s -> p (h s)"), ALU.mult).then_inc(c_ready, 1)

            dve.wait_ge(gates_turned, 2)
            ig, fg = bank[5][:, 0:P], bank[5][:, P:2 * P]
            gmax, fabs, lf, fl, fsum, key_gate, fm, lim = (gsc[:, k, :] for k in (1, 2, 0, 4, 5, 6, 7, 0))
            step(vec.tensor_copy(lf, fg))
            settle()
            vec.scalar_tensor_tensor(out=fabs, in0=lf, scalar=-1.0, in1=lf, op0=ALU.mult, op1=ALU.min).then_inc(fabs_ready, 1)
            dve.wait_ge(qblk_zeroed, 2)
            dve.wait_ge(x_copied, NB)
            query_blocks(1, range(HU))
            dve.wait_ge(fln_ready, 1)
            link(vec.scalar_tensor_tensor(out=lf, in0=lf, scalar=0.0, in1=fl, op0=ALU.min, op1=ALU.subtract))
            step(vec.tensor_tensor_scan(fsum, ones[:, :], lf, 0.0, ALU.mult, ALU.add))
            settle()
            link(vec.tensor_tensor(key_gate, ig, fsum, ALU.subtract))
            link(vec.tensor_tensor_scan(gmax, ones[:, :], key_gate, LOWEST, ALU.mult, ALU.max))
            vec.tensor_tensor(fm, fsum, gmax, ALU.add).then_inc(gsum_ready, 1)
            vec.tensor_copy(gmax_hi[:, :], gmax).then_inc(split_ready, 1)
            dve.wait_ge(split_ready, 1)
            vec.tensor_tensor(gmax_lo[:, :], gmax, gmax_hi[:, :].bitcast(F32), ALU.subtract).then_inc(split_ready, 1)
            for part, src, k in ((neg_hi, gmax_hi, 1), (neg_lo, gmax_lo, 2)):
                dve.wait_ge(split_ready, k)
                vec.tensor_tensor(part[:, :, :], src[:, :].bitcast(F32).unsqueeze(1).to_broadcast([P, NH, P]),
                                  head_sel[:, :].unsqueeze(2).to_broadcast([P, NH, P]), ALU.mult).then_inc(negmax_ready, 1)
            def weight_lo(l):
                dve.wait_ge(wT_copied, l + 1)
                vec.tensor_tensor(wT_lo[:, l, :, :], bank[l % 2][:, :].rearrange("p (c n) -> p c n", c=DC),
                                  wT_hi[:, l, :, :].bitcast(F32), ALU.subtract).then_inc(wT_lo_ready, 1)

            dve.wait_ge(glim_turned, 2)
            vec.tensor_copy(gT[:, :], bank[4][:, 0:P]).then_inc(dve_consts, 1)
            vec.tensor_scalar(limT[:, :], bank[5][:, 0:P], HEAD_EPS, None, ALU.add).then_inc(glim_copied, 1)

            done = {}

            def mark(name, ins):
                step(ins)
                done[name] = steps[0]

            def need(*names):
                dve.wait_ge(dve_step, max(done[n] for n in names))

            den_abs, den, den2, ss = (small[:, k, :] for k in (0, 1, 6, 7))

            def sum_squares(b):
                dve.wait_ge(sq_ready, b + 1)
                mark("ss", vec.tensor_reduce(ss, sq[:, :, :], AX.X, ALU.add))

            def den_1(b):
                tot = heads_out[:, b % 2, :, HD]
                mark("den_abs", vec.scalar_tensor_tensor(out=den_abs, in0=tot, scalar=-1.0, in1=tot,
                                                         op0=ALU.mult, op1=ALU.max))

            def den_2(b):
                need("den_abs")
                lim = limT[:, :].rearrange("p (h b) -> p b h", h=NH)[:, b, :]
                mark("den", vec.scalar_tensor_tensor(out=den, in0=den_abs, scalar=HEAD_EPS, in1=lim,
                                                     op0=ALU.add, op1=ALU.max))

            def den_3(b):
                need("den")
                mark("den2", vec.tensor_tensor(den2, den, den, ALU.mult))

            def mean_square(b):
                need("den2", "ss")
                vec.scalar_tensor_tensor(out=small[:, 2 + b % 2, :], in0=den2, scalar=HEAD_EPS, in1=ss,
                                         op0=ALU.mult, op1=ALU.add).then_inc(ms_ready, 1)

            def scale_heads(b):
                dve.wait_ge(rms_ready, b + 1)
                vec.tensor_tensor(yh[:, :, :], heads_out[:, b % 2, :, 0:HD],
                                  small[:, 4 + b % 2, :].unsqueeze(2).to_broadcast([P, NH, HD]),
                                  ALU.mult).then_inc(yh_ready, 1)

            def add_heads(b):
                dve.wait_ge(yh_ready, b + 1)
                mark("x1", vec.tensor_tensor(xres[:, b, :], xres[:, b, :], yh[:, :, :].rearrange("p h d -> p (h d)"), ALU.add))

            def stats2(b):
                need("x1")
                mark("bst2", vec.bn_stats(bst2[:, b % 2, :], xres[:, b, :]))

            def aggr2(b):
                need("bst2")
                mark("bag2", vec.bn_aggr(bag2[:, b % 2, :], bst2[:, b % 2, :]))

            def var2(b):
                need("bag2")
                vec.tensor_scalar(veps2[:, b % 2:b % 2 + 1], bag2[:, b % 2, 1:2], LN_EPS, None,
                                  ALU.add).then_inc(var2_ready, 1)

            def norm2(b):
                dve.wait_ge(rstd2_ready, b + 1)
                if b >= 8:
                    dve.wait_ge(scattered[b % 8], 32 * (b // 8))
                vec.tensor_scalar(xn2[:, b % 8, :], xres[:, b, :], bag2[:, b % 2, 0:1], rstd2[:, b % 2:b % 2 + 1],
                                  ALU.subtract, ALU.mult).then_inc(xn2_ready, 1)

            def add_router_bias(j):
                dve.wait_ge(logits_done, 2 * j + 2)
                vec.tensor_tensor(lg[:, :, :], bank[7][:, 0:2 * E].rearrange("p (b e) -> p b e", b=2),
                                  router_b[:, :].unsqueeze(1).to_broadcast([P, 2, E]), ALU.add).then_inc(logits_read, 1)

            def largest(j):
                dve.wait_ge(logits_read, j + 1)
                for k in range(2):
                    mark("max", vec.max(top_v[:, 2 * j + k, :], lg[:, k, :]))

            def largest_at(j):
                need("max")
                for k in range(2):
                    mark("at", vec.max_index(top_i[:, 2 * j + k, :], top_v[:, 2 * j + k, :], lg[:, k, :]))

            def chosen_no(j):
                need("at")
                mark("topi", vec.tensor_copy(topi[:, 2 * j:2 * j + 2, :], top_i[:, 2 * j:2 * j + 2, 0:2]))

            def chosen_mask(j):
                need("topi")
                mark("pick", vec.tensor_tensor(pick[:, j % 2, :, :, :].rearrange("p b k e -> p (b k) e"),
                                               expert_no[:, :].unsqueeze(1).to_broadcast([P, 4, E]),
                                               topi[:, 2 * j:2 * j + 2, :].rearrange("p b k -> p (b k)").unsqueeze(2)
                                               .to_broadcast([P, 4, E]), ALU.is_equal))

            def both_masks(j):
                need("pick")
                mark("mask", vec.tensor_tensor(mask_bf[:, j % 2, :, :], pick[:, j % 2, :, 0, :],
                                               pick[:, j % 2, :, 1, :], ALU.add))

            def seen_1(j):
                need("mask")
                vec.tensor_tensor(seen_bf[:, 2 * j + 1, :], seen_bf[:, 2 * j, :], mask_bf[:, j % 2, 0, :],
                                  ALU.add).then_inc(mask_ready, 1)

            def seen_2(j):
                dve.wait_ge(mask_ready, j + 1)
                step(vec.tensor_tensor(seen_bf[:, 2 * j + 2, :], seen_bf[:, 2 * j + 1, :], mask_bf[:, j % 2, 1, :],
                                       ALU.add))

            def rank_1(j):
                dve.wait_ge(rank_done, j + 1)
                ranks = bank[7][:, 64:64 + 2 * E].rearrange("p (b e) -> p b e", b=2)
                for k in range(TOP_K):
                    ins = vec.tensor_tensor(picked[:, :, k, :], pick[:, j % 2, :, k, :], ranks, ALU.mult)
                ins.then_inc(rank_read, 1)

            def rank_2(j):
                dve.wait_ge(rank_read, j + 1)
                mark("rank", vec.tensor_reduce(rank[:, :, :], picked[:, :, :, :], AX.X, ALU.add))

            def slot_1(j):
                need("rank")
                two = slice(2 * j, 2 * j + 2)
                step(vec.tensor_scalar(over[:, :, :], rank[:, :, :], float(CAP), DROPPED, ALU.is_gt, ALU.mult))
                mark("slot", vec.scalar_tensor_tensor(out=base[:, :, :], in0=topi[:, two, :], scalar=float(CAP),
                                                      in1=rank[:, :, :], op0=ALU.mult, op1=ALU.add))
                step(vec.tensor_scalar(kept[:, two, :], rank[:, :, :], float(CAP), None, ALU.is_le))

            def slot_2(j):
                need("slot")
                vec.scalar_tensor_tensor(out=dest[:, 2 * j:2 * j + 2, :], in0=base[:, :, :], scalar=-1.0,
                                         in1=over[:, :, :], op0=ALU.add, op1=ALU.add).then_inc(dest_ready, 1)

            def w1_second(e, c):
                dve.wait_ge(w1_hi_ready, DC * e + (c + 1))
                vec.tensor_tensor(w1_lo[:, c, :], w1_raw[:, c, :], w1_hi[:, c, :].bitcast(F32),
                                  ALU.subtract).then_inc(w1_lo_ready, 1)

            link(vec.memset(seen_bf[:, 0, :], 0.0))
            dve.wait_ge(router_in, 32)
            for i in range(LAST):
                one = 2 <= i < NB + 2
                two = 3 <= i < NB + 3
                route = i % 2 == 0 and 6 <= i < NB + 6
                place = i % 2 == 1 and 7 <= i < NB + 7
                jr, jp = (i - 6) // 2, (i - 7) // 2
                if 0 < 2 * i - 1 < 2 * NB:
                    weigh(2 * i - 1)
                if 4 <= i < NB + 4:
                    norm2(i - 4)
                if route:
                    add_router_bias(jr)
                if one:
                    sum_squares(i - 2)
                if route:
                    largest(jr)
                if one:
                    den_1(i - 2)
                if two:
                    scale_heads(i - 3)
                if route:
                    largest_at(jr)
                if one:
                    den_2(i - 2)
                if i + 1 < NB:
                    query_blocks(2 * i + 3, (0, 1))
                if one:
                    den_3(i - 2)
                if two:
                    add_heads(i - 3)
                if route:
                    chosen_no(jr)
                if i < NB:
                    weigh(2 * i)
                if one:
                    mean_square(i - 2)
                if route:
                    chosen_mask(jr)
                if two:
                    stats2(i - 3)
                if place:
                    rank_1(jp)
                if i + 1 < NB:
                    query_blocks(2 * i + 3, (2, 3))
                if route:
                    both_masks(jr)
                if place:
                    rank_2(jp)
                if two:
                    aggr2(i - 3)
                if route:
                    seen_1(jr)
                if place:
                    slot_1(jp)
                if two:
                    var2(i - 3)
                if route:
                    seen_2(jr)
                if place:
                    slot_2(jp)
                if NB - 1 <= i <= NB + NL - 2:
                    dequant(i - NB + 1)
                if NB + 1 <= i <= NB + 3:
                    weight_lo(i - NB - 1)
                if i == NB + 7:
                    w1_second(0, 0)
                    w1_second(0, 1)

            vec.tensor_tensor(wtop[:, :, 1], top_v[:, :, 1], top_v[:, :, 0], ALU.subtract).then_inc(topdiff_ready, 1)
            dve.wait_ge(topexp_ready, 1)
            link(vec.tensor_scalar(wtop[:, :, 1], wtop[:, :, 0], 1.0, None, ALU.add))
            link(vec.reciprocal(veps[:, 0:NB], wtop[:, :, 1]))
            link(vec.tensor_tensor(wtop[:, :, 1], wtop[:, :, 0], veps[:, 0:NB], ALU.mult))
            link(vec.tensor_copy(wtop[:, :, 0], veps[:, 0:NB]))
            vec.tensor_tensor(wtop[:, :, :], wtop[:, :, :], kept[:, :, :], ALU.mult).then_inc(wtop_ready, 1)
            for l in range(3, NL):
                weight_lo(l)

            def slots_lo(e, j):
                vec.tensor_copy(b1_cur[:, j, :], cols[:, bass.ds(B1 + FC * e, FC)]).then_inc(b1_ready, 1)
                for c in range(DC):
                    dve.wait_ge(xT_hi_ready, DC * e + (c + 1))
                    vec.tensor_tensor(xT_lo[:, c, :], bank[4 + c][:, 0:CAP], xT_hi[:, c, :].bitcast(F32),
                                      ALU.subtract).then_inc(xT_lo_ready, 1)

            VEC_HI = [f for f in range(FC) if f % 4 != 3]

            def hidden(e):
                def second(f):
                    if f in VEC_HI:
                        dve.wait_ge(h_hi_dve, len(VEC_HI) * e + (VEC_HI.index(f) + 1))
                    else:
                        dve.wait_ge(h_hi_act, FC // 4 * e + (f // 4 + 1))
                    vec.tensor_tensor(h_lo[:, f, :], h_ring[:, f % 4, :], h_hi[:, f, :].bitcast(F32),
                                      ALU.subtract).then_inc(h_lo_ready, 1)

                for f in range(FC):
                    if f in VEC_HI:
                        dve.wait_ge(relu_ready, FC * e + (f + 1))
                        vec.tensor_copy(h_hi[:, f, :], h_ring[:, f % 4, :]).then_inc(h_hi_dve, 1)
                    if f >= 1:
                        second(f - 1)
                second(FC - 1)

            def result(e, j, m):
                n = P if m < MT - 1 else MTAIL
                dve.wait_ge(y_done, MT * e + (m + 1))
                bb = b2_row[0:n, bass.ds(e, 1), :].rearrange("p a d -> p (a d)")
                vec.tensor_tensor(y_sb[0:n, j, m, :], bank[6 + (MT * j + m) % 2][0:n, 0:D], bb, ALU.add).then_inc(y_ready, 1)

            def expert(e, j, first=False, follows=True):
                hidden(e)
                if follows:
                    slots_lo(e + 1, 1 - j)
                    w1_second(e + 1, 0)
                if not first:
                    dve.wait_ge(y_out[j], 16 * e - 16 * j)
                result(e, j, 0)
                if follows:
                    w1_second(e + 1, 1)
                result(e, j, 1)
                result(e, j, 2)

            dve.wait_ge(b2_in, 16)
            slots_lo(0, 0)
            expert(0, 0, first=True)
            expert(1, 1, first=True)
            with dve.Fori(1, E // 2 - 1) as k:
                for j in range(2):
                    expert(2 * k + j, j)
            expert(E - 2, 0)
            dve.wait_ge(w1_lo_ready, DC * E)
            vec.memset(gath[:, :, :, :], 0.0).then_inc(gath_zeroed, 1)
            expert(E - 1, 1, follows=False)

            def add_expert(b, k):
                if k == 0:
                    dve.wait_ge(gathered[b % 4], 32 * (b // 4 + 1))
                else:
                    need("x2 half")
                ins = vec.scalar_tensor_tensor(out=xres[:, b, :], in0=gath[:, b % 4, k, :], scalar=wtop[:, b, k:k + 1],
                                               in1=xres[:, b, :], op0=ALU.mult, op1=ALU.add)
                if k == 0:
                    mark("x2 half", ins)
                else:
                    ins.then_inc(x2_ready, 1)

            def score_max(b):
                dve.wait_ge(score_done, b + 1)
                vec.tensor_reduce(smax[:, 0, b % 2:b % 2 + 1], bank[b % 2][:, 0:P], AX.X, ALU.max,
                                  negate=True).then_inc(smax_ready, 1)

            def invert_sum(b):
                dve.wait_ge(attn_ready, b + 1)
                mark("inv_sum", vec.reciprocal(inv_sum[:, b % 2:b % 2 + 1], smax[:, 1, b % 2:b % 2 + 1]))

            def attend(b):
                need("inv_sum")
                dve.wait_ge(ctxv_done, b + 1)
                vec.scalar_tensor_tensor(out=xres[:, b, :], in0=bank[3][:, 0:D], scalar=inv_sum[:, b % 2:b % 2 + 1],
                                         in1=xres[:, b, :], op0=ALU.mult, op1=ALU.add).then_inc(x3_ready, 1)

            def stats(k, b, ready):
                dve.wait_ge(ready, b + 1)
                mark(("stats", k), vec.bn_stats(bst34[:, k, :], xres[:, b, :]))

            def aggr(k, i):
                need(("stats", k))
                mark(("aggr", k), vec.bn_aggr(bag34[:, i % 2, k, :], bst34[:, k, :]))

            def norm3(b):
                dve.wait_ge(rstd34_ready, b + 1)
                if b >= 2:
                    dve.wait_ge(xn3_turned, b - 1)
                vec.tensor_scalar(xn3[:, b % 2, :], xres[:, b, :], bag34[:, b % 2, 0, 0:1], rstd34[:, b % 2, 0:1],
                                  ALU.subtract, ALU.mult).then_inc(xn3_ready, 1)

            def norm4(b):
                dve.wait_ge(rstd34_ready, b + TO_ATTEND + 1)
                if b >= 2:
                    dve.wait_ge(xn4_turned, b - 1)
                vec.tensor_scalar(xn4[:, b % 2, :], xres[:, b, :], bag34[:, b % 2, 1, 0:1], rstd34[:, b % 2, 1:2],
                                  ALU.subtract, ALU.mult).then_inc(xn4_ready, 1)

            mark(("aggr", 0), vec.memset(bag34[:, :, :, :], 1.0))
            done["aggr", 1] = done["aggr", 0]
            for k in range(4):
                vec.memset(shift5[:, 0, k:k + 1], 0.0).then_inc(yb_ready, 1)
            for i in range(NB + TO_NORM):
                new, old = i < NB, TO_ATTEND <= i < NB + TO_ATTEND
                if new:
                    add_expert(i, 0)
                if old:
                    invert_sum(i - TO_ATTEND)
                if TO_SCORE <= i < NB + TO_SCORE:
                    score_max(i - TO_SCORE)
                if new:
                    add_expert(i, 1)
                if 1 <= i <= NB:
                    norm3(i - 1)
                if old:
                    attend(i - TO_ATTEND)
                if new:
                    stats(0, i, x2_ready)
                if TO_NORM <= i:
                    norm4(i - TO_NORM)
                if old:
                    stats(1, i - TO_ATTEND, x3_ready)
                if new:
                    aggr(0, i)
                if old:
                    aggr(1, i)
                if i < NB + TO_ATTEND:
                    need(("aggr", 0), ("aggr", 1))
                    vec.tensor_scalar(veps34[:, i % 2, :], bag34[:, i % 2, :, 1], LN_EPS, None,
                                      ALU.add).then_inc(var34_ready, 1)

            dve.wait_ge(biasrow_in, 16)
            base_steps = steps[0]
            PER_GROUP = 2 * G

            def add_bias(blk, n, g, t):
                dve.wait_ge(yf_done, G * n + (t + 1))
                if t == 0 and (not isinstance(n, int) or n >= 2):
                    dve.wait_ge(zn_ready, (G - 1) * (n - 1))
                if t == G - 1 and (not isinstance(n, int) or n >= 2):
                    dve.wait_ge(zn_last_ready, n - 1)
                vec.tensor_tensor(yb[:, (g % 2) * G + t, :], bank[FIRST_BANK[t]][:, 0:D],
                                  bias_row[:, bass.ds(blk, 1), :].rearrange("p a d -> p (a d)"),
                                  ALU.add).then_inc(yb_ready, 1)

            def stats5(n, g, t):
                dve.wait_ge(yb_ready, G * n + (t + 5))
                vec.bn_stats(bst5[:, t, :], yb[:, (g % 2) * G + t, :]).then_inc(dve_step, 1)

            def variance5(n, g):
                at = base_steps + PER_GROUP * n
                dve.wait_ge(dve_step, at + G)
                vec.memset(rstd5[:, g % 2, :], 0.0).then_inc(memset_done, 1)
                for t in range(G):
                    vec.bn_aggr(bag5[:, g % 2, t, :], bst5[:, t, :]).then_inc(dve_step, 1)
                dve.wait_ge(dve_step, at + 2 * G)
                vec.tensor_scalar(veps5[:, g % 2, :], bag5[:, g % 2, :, 1], LN_EPS, None,
                                  ALU.add).then_inc(var5_ready, 1)

            def shift(n, g):
                dve.wait_ge(rstd5_ready, n + 1)
                vec.scalar_tensor_tensor(out=shift5[:, g % 2, :], in0=bag5[:, g % 2, :, 0], scalar=-1.0,
                                         in1=rstd5[:, g % 2, :], op0=ALU.mult, op1=ALU.mult).then_inc(shift5_ready, 1)

            def split_a(n, g, c):
                dve.wait_ge(a_hi_ready, DC * n + (c + 1))
                vec.tensor_tensor(a_lo[:, g % 2, c, :], a_f[:, g % 2, c, :], a_hi[:, g % 2, c, :].bitcast(F32),
                                  ALU.subtract).then_inc(a_lo_ready, 1)

            def update(blk, n, g):
                for o in range(DC):
                    dve.wait_ge(y2_done, DC * n + (o + 1))
                    h = hT[:, o, g * GT:(g + 1) * GT]
                    vec.scalar_tensor_tensor(out=h, in0=bank[4 + o][:, :],
                                             scalar=cols[:, bass.ds(BI + DC + 2 * DC * blk + o, 1)], in1=h,
                                             op0=ALU.add, op1=ALU.add).then_inc(h_ready, 1)

            def finish(g):
                for t in range(g * G, (g + 1) * G):
                    dve.wait_ge(fin_turned, t + 1)
                    vec.tensor_tensor(o_sb[:, t, :], bank[FIRST_BANK[t % G]][:, 0:D], xres[:, t, :],
                                      ALU.add).then_inc(fin_ready, 1)

            def set_affine(blk):
                for k, at in ((0, GA), (1, BE)):
                    vec.tensor_copy(affine[:, k, :], cols[:, bass.ds(at + DC * blk, DC)]).then_inc(affine_ready, 1)

            def block_steps(blk, last):
                for now, kept_w in ((w2c_hi, wT_hi), (w2c_lo, wT_lo)):
                    vec.tensor_copy(now[:, :, :], kept_w[:, bass.ds(2 * blk + 1, 1), :, :].rearrange("p a c n -> p (a c) n")
                                    ).then_inc(w2cur_ready, 1)
                for g in range(NG):
                    n = NG * blk + g
                    g1, g2 = (g + 1) % NG, (g + 2) % NG
                    comes, follows = not last or g + 2 < NG, not last or g + 1 < NG
                    if comes:
                        add_bias(blk + (g + 2) // NG, n + 2, g2, 0)
                    taken = last and g >= 2
                    if follows and not taken:
                        shift(n + 1, g1)
                    if comes:
                        stats5(n + 2, g2, 0)
                        add_bias(blk + (g + 2) // NG, n + 2, g2, 1)
                    if not taken:
                        split_a(n, g, 0)
                    if comes:
                        stats5(n + 2, g2, 1)
                        add_bias(blk + (g + 2) // NG, n + 2, g2, 2)
                    if not taken:
                        split_a(n, g, 1)
                    if comes:
                        add_bias(blk + (g + 2) // NG, n + 2, g2, 3)
                        stats5(n + 2, g2, 2)
                        stats5(n + 2, g2, 3)
                    if comes:
                        variance5(n + 2, g2)
                    if last and 1 <= g < NG - 1:
                        if g + 2 < NG:
                            shift(n + 2, g2)
                        for c in range(DC):
                            split_a(n + 1, g1, c)
                    update(blk, n, g)
                    if last and g >= 1:
                        finish(g - 1)
                    if g == NG - 1 and not last:
                        set_affine(blk + 1)
                if last:
                    finish(NG - 1)

            set_affine(0)
            for g in range(2):
                for t in range(G):
                    add_bias(0, g, g, t)
                    if g == 1 and t == 1:
                        shift(0, 0)
                    if t >= 1:
                        stats5(g, g, t - 1)
                stats5(g, g, G - 1)
                variance5(g, g)
            with dve.Fori(0, NBLK - 1) as blk:
                block_steps(blk, False)
            block_steps(NBLK - 1, True)

        @block.tensor
        def _(pe):
            mm = pe.matmul

            def turn(dst, src, n=P):
                return pe.transpose(dst, src, ident[0:n, 0:n])

            pe.wait_ge(consts, 12)

            def turn_ctx(t):
                pe.wait_ge(ctx_in[t // G], 16)
                if t >= 2:
                    pe.wait_ge(ctx_copied, t - 1)
                for c in range(DC):
                    ins = turn(bank[2 + t % 2][:, c * P:(c + 1) * P], ctx_tok[:, t, c * P:(c + 1) * P])
                ins.then_inc(ctx_turned, 1)

            def turn_x(t):
                pe.wait_ge(xn_ready, t + 1)
                if t >= 2:
                    pe.wait_ge(x_copied, t - 1)
                for c in range(DC):
                    ins = turn(bank[t % 2][:, c * P:(c + 1) * P], xn[:, t % 4, c * P:(c + 1) * P])
                ins.then_inc(x_turned, 1)

            def gates(g, k):
                if k == 0:
                    pe.wait_ge(x_copied, G * (g + 1))
                    pe.wait_ge(ctx_copied, G * (g + 1))
                    if g == 0:
                        pe.wait_ge(gkctx_ready, 1)
                    if g >= 2:
                        pe.wait_ge(gates_copied, g - 1)
                at, c = slice(g * GT, (g + 1) * GT), k % DC
                kernel, acts = (gk_raw, xnT) if k < DC else (gk_ctx, ctxT)
                ins = mm(bank[4 + g % 2][0:2 * NH, :], kernel[:, c, :], acts[:, c, at], start=(k == 0), stop=(k == 2 * DC - 1))
                if k == 2 * DC - 1:
                    ins.then_inc(gates_done, 1)

            def turn_gates(g):
                pe.wait_ge(gates_copied, g + 1)
                for t in range(G):
                    at = (g * G + t) * 2 * NH
                    turn(bank[7][:, at:at + 2 * NH], gates_sb[:, g % 2, t * P:(t + 1) * P], 2 * NH).then_inc(gates_tok_done, 1)

            for t in range(NB):
                turn_ctx(t)
                turn_x(t)
                if t >= G:
                    gates(t // G - 1, t % G)
                if t % G == 2 and t > 2 * G:
                    turn_gates(t // G - 2)
            pe.wait_ge(rows_in, 96)
            turn(bank[6][:, 0:NROWS], rows[:, :], NROWS).then_inc(cols_turned, 1)
            for k in range(2 * DC):
                gates(NG - 1, k)

            turn_gates(NG - 2)
            turn_gates(NG - 1)
            pe.wait_ge(gates_tok_copied, 1)
            for k in range(2):
                turn(bank[5][:, k * P:(k + 1) * P],
                     gates_tok[:, k * NH:(k + 1) * NH, :].rearrange("p h b -> p (h b)")).then_inc(gates_turned, 1)
            pe.wait_ge(gsum_ready, 1)
            turn(bank[4][:, 0:P], gsc[:, 6, :]).then_inc(glim_turned, 1)
            pe.wait_ge(lim_ready, 1)
            turn(bank[5][:, 0:P], gsc[:, 0, :]).then_inc(glim_turned, 1)

            def max_rows(u):
                b = u // 2
                pe.wait_ge(negmax_ready, 2)
                if u < 2:
                    pe.wait_ge(x_copied, NB)
                else:
                    pe.wait_ge(exp_done, HU * (u - 1))
                mm(bank[u % 2][:, :], ident_bf[:, :], causal_bf[:, :, :].rearrange("p h i -> p (h i)"),
                   start=True, stop=False)
                for k, part in enumerate((neg_hi, neg_lo)):
                    ins = mm(bank[u % 2][:, :], seq_sel[:, b:b + 1].to_broadcast([P, P]),
                             part[:, HU * (u % 2):HU * (u % 2 + 1), :].rearrange("p h i -> p (h i)"),
                             start=False, stop=(k == 1))
                ins.then_inc(maxb_done, 1)

            def keys_queries(u):
                b = u // 2
                pe.wait_ge(qblk_ready[u % 2], u // 2 + 1)
                if u < 2:
                    pe.wait_ge(ctx_copied, NB)
                else:
                    pe.wait_ge(c_ready, u - 1)
                mm(bank[2 + u % 2][:, :], ctxT[:, u % 2, b * P:(b + 1) * P],
                   qblk[:, u % 4, :, :].rearrange("p h i -> p (h i)"),
                   start=True, stop=True).then_inc(qk_done, 1)

            def values(u):
                b = u // 2
                pe.wait_ge(c_ready, u + 1)
                pe.wait_ge(vaug_ready, b + 1)
                if b >= 2:
                    pe.wait_ge(heads_copied, b - 1)
                else:
                    pe.wait_ge(glim_copied, 1)
                for h in range(HU):
                    hh = HU * (u % 2) + h
                    ins = mm(bank[4 + b % 2][:, hh * HA:(hh + 1) * HA], cmat[:, u % 2, h, :],
                             v_aug[:, b % 2, hh, :], start=True, stop=True)
                ins.then_inc(cv_done, 1)

            def turn_xn2(b):
                pe.wait_ge(xn2_ready, b + 1)
                if b == 0:
                    pe.wait_ge(cols_ready, 1)
                else:
                    pe.wait_ge(xn2T_copied, b)
                for c in range(DC):
                    ins = turn(bank[6][:, c * P:(c + 1) * P], xn2[:, b % 8, c * P:(c + 1) * P])
                ins.then_inc(xn2_turned, 1)

            def logits(b):
                pe.wait_ge(xn2T_copied, b + 1)
                pe.wait_ge(router_in, 32)
                if b >= 2 and b % 2 == 0:
                    pe.wait_ge(logits_read, b // 2)
                if b >= 3 and b % 2 == 1:
                    pe.wait_ge(rank_read, b // 2)
                at = b % 2 * E
                for c in range(DC):
                    ins = mm(bank[7][:, at:at + E], xn2T[:, b % 2, c, :], router_w[:, c, :],
                             start=(c == 0), stop=(c == DC - 1))
                ins.then_inc(logits_done, 1)

            def ranks(j):
                pe.wait_ge(mask_ready, j + 1)
                dst = bank[7][:, 64:64 + 2 * E]
                mm(dst, tri_bf[:, :], mask_bf[:, j % 2, :, :].rearrange("p b e -> p (b e)"), start=True, stop=False)
                mm(dst, ones_bf[:, :], seen_bf[:, 2 * j:2 * j + 2, :].rearrange("p b e -> p (b e)"),
                   start=False, stop=True).then_inc(rank_done, 1)

            def turn_lora(l):
                if l == 0:
                    pe.wait_ge(ffnw_in, 48)
                if l < 2:
                    pe.wait_ge(c_ready, 2 * NB)
                else:
                    pe.wait_ge(lb_copied, l - 1)
                for c in range(DC):
                    ins = turn(bank[2 + l % 2][0:R, c * P:(c + 1) * P], lb_sb[:, l, c, :])
                ins.then_inc(lb_turned, 1)

            def weight(l):
                pe.wait_ge(wdeq_ready, l + 1)
                pe.wait_ge(lb_copied, l + 1)
                if l < 2:
                    pe.wait_ge(exp_done, 2 * NB * HU)
                else:
                    pe.wait_ge(wT_lo_ready, l - 1)
                for c in range(DC):
                    at = c * D
                    mm(bank[l % 2][:, at:at + D], la_sb[:, l, c * P:(c + 1) * P], lbT[:, l % 2, :],
                       start=True, stop=True)
                    for o in range(DC):
                        ins = mm(bank[l % 2][:, at + o * P:at + (o + 1) * P], wdeq[:, l, o, c * P:(c + 1) * P],
                                 ident[:, :], start=False, stop=(o == DC - 1), skip_group_check=True)
                ins.then_inc(wT_done, 1)

            max_rows(0)
            for i in range(LAST):
                if 1 <= i <= NB:
                    values(2 * i - 2)
                if i < NB:
                    max_rows(2 * i + 1)
                if 5 <= i < NB + 5:
                    logits(i - 5)
                if i % 2 == 1 and 7 <= i < NB + 7:
                    ranks((i - 7) // 2)
                if i < NB:
                    keys_queries(2 * i)
                if 1 <= i <= NB:
                    values(2 * i - 1)
                if i + 1 < NB:
                    max_rows(2 * i + 2)
                if 4 <= i < NB + 4:
                    turn_xn2(i - 4)
                if i < NB:
                    keys_queries(2 * i + 1)
                if i == NB:
                    turn_lora(0)
                    turn_lora(1)
                    weight(0)
                if NB < i <= NB + 2:
                    turn_lora(i - NB + 1)
                    weight(i - NB)
                if i == NB + 4:
                    turn_lora(4)
                    weight(3)
            for l in range(4, NL):
                if l + 1 < NL:
                    turn_lora(l + 1)
                weight(l)

            def turn_slots(e, j, first=False):
                pe.wait_ge(xin_in[j], 16 * e - 16 * j + 32)
                for c in range(DC):
                    if first:
                        pe.wait_ge(heads_copied, NB)
                    else:
                        pe.wait_ge(xT_lo_ready, DC * e - DC + (c + 1))
                    for m in range(MT):
                        n = P if m < MT - 1 else MTAIL
                        ins = turn(bank[4 + c][:, m * P:m * P + n], xin[0:n, j, m, c * P:(c + 1) * P], n)
                    ins.then_inc(xin_turned, 1)

            def hidden(e, j, first=False):
                pe.wait_ge(w1_lo_ready, DC * e + DC)
                pe.wait_ge(xT_lo_ready, DC * e + DC)
                for f in range(FC):
                    if first and f < 4:
                        pe.wait_ge(wT_lo_ready, NL)
                        pe.wait_ge(lb_copied, NL)
                    else:
                        pe.wait_ge(relu_ready, FC * e + f - 3)
                    dst, fs = bank[f % 4][:, 0:CAP], slice(f * P, (f + 1) * P)
                    for c in range(DC):
                        mm(dst, w1_hi[:, c, fs], xT_hi[:, c, :], start=(c == 0), stop=False)
                        mm(dst, w1_hi[:, c, fs], xT_lo[:, c, :], start=False, stop=False)
                        ins = mm(dst, w1_lo[:, c, fs], xT_hi[:, c, :], start=False, stop=(c == DC - 1))
                    ins.then_inc(h_done, 1)

            def results(e, j, first=False):
                for m in range(MT):
                    n = P if m < MT - 1 else MTAIL
                    if first and m < 2:
                        pe.wait_ge(rank_read, NB // 2)
                    else:
                        pe.wait_ge(y_ready, MT * e + m - 1)
                    dst, ms = bank[6 + (MT * j + m) % 2][0:n, 0:D], slice(m * P, m * P + n)
                    for f in range(FC):
                        if m == 0:
                            pe.wait_ge(h_lo_ready, FC * e + (f + 1))
                            pe.wait_ge(w2_lo_ready, 2 * e + (f // H2 + 1))
                        mm(dst, h_hi[:, f, ms], w2_hi[:, f, :], start=(f == 0), stop=False)
                        mm(dst, h_hi[:, f, ms], w2_lo[:, f, :], start=False, stop=False)
                        ins = mm(dst, h_lo[:, f, ms], w2_hi[:, f, :], start=False, stop=(f == FC - 1))
                    ins.then_inc(y_done, 1)

            turn_slots(0, 0, True)
            hidden(0, 0, True)
            turn_slots(1, 1)
            results(0, 0, True)
            hidden(1, 1)
            turn_slots(2, 0)
            results(1, 1)
            with pe.Fori(1, E // 2 - 1) as k:
                for j in range(2):
                    hidden(2 * k + j, j)
                    turn_slots(2 * k + (j + 1), 1 - j)
                    results(2 * k + j, j)
            for e in range(E - 2, E):
                hidden(e, e % 2)
                if e + 1 < E:
                    turn_slots(e + 1, (e + 1) % 2)
                results(e, e % 2)

            def three(dst, parts, start, stop):
                x, x_low, w, w_low = parts
                mm(dst, x, w, start=start, stop=False)
                mm(dst, x, w_low, start=False, stop=False)
                return mm(dst, x_low, w, start=False, stop=stop)

            def first(blk, n, g):
                pe.wait_ge(hg_lo_ready, DC * n + DC)
                for t in range(G):
                    pe.wait_ge(yb_ready, G * n + (t + 1))
                    ts = slice(t * P, (t + 1) * P)
                    for c in range(DC):
                        w, w_low = (m[:, bass.ds(2 * blk, 1), c, :].rearrange("p a n -> p (a n)") for m in (wT_hi, wT_lo))
                        ins = three(bank[FIRST_BANK[t]][:, 0:D], (hg_hi[:, g % 2, c, ts], hg_lo[:, g % 2, c, ts], w, w_low),
                                    c == 0, c == DC - 1)
                    ins.then_inc(yf_done, 1)

            def score(b):
                pe.wait_ge(q_copied, DC * (b + 1))
                if b < 2:
                    pe.wait_ge(relu_ready, E * FC)
                else:
                    pe.wait_ge(attn_ready, b - 1)
                for c in range(DC):
                    ins = mm(bank[b % 2][:, 0:P], qT[:, b % 2, c, :],
                             vT[:, c, b * P:(b + 1) * P], start=(c == 0), stop=(c == DC - 1))
                ins.then_inc(score_done, 1)

            def attn_values(n, c):
                g, o = n // DC, n % DC
                if n == 0 and c == 0:
                    pe.wait_ge(attnw_in, 32)
                    pe.wait_ge(y_ready, E * MT)
                elif c == 0:
                    pe.wait_ge(vT_copied, n)
                ins = mm(bank[7][:, :], wv_sb[:, c, o * P:(o + 1) * P], ctxT[:, c, g * GT:(g + 1) * GT],
                         start=(c == 0), stop=(c == DC - 1))
                if c == DC - 1:
                    ins.then_inc(vT_done, 1)

            for n in range(DC):
                for c in range(DC):
                    attn_values(n, c)
            for i in range(NB + TO_NORM):
                if TO_SCORE <= i < NB + TO_SCORE:
                    score(i - TO_SCORE)
                if TO_ATTEND <= i < NB + TO_ATTEND:
                    b = i - TO_ATTEND
                    pe.wait_ge(attnT_copied, b + 1)
                    pe.wait_ge(vtok_copied, b + 1)
                    if b >= 1:
                        pe.wait_ge(x3_ready, b)
                    mm(bank[3][:, 0:D], attnT[:, b % 2, :], v_tok[:, b, :], start=True, stop=True).then_inc(ctxv_done, 1)
                if 2 <= i < NB + 2:
                    b = i - 2
                    pe.wait_ge(xn3T_copied, b + 1)
                    if b == 0:
                        pe.wait_ge(y_ready, E * MT)
                    else:
                        pe.wait_ge(vtok_copied, b)
                    pe.wait_ge(vT_copied, DC * (b // G + 1))
                    for c in range(DC):
                        turn(bank[6][:, D + c * P:D + (c + 1) * P], vT[:, c, b * P:(b + 1) * P])
                    for o in range(DC):
                        for c in range(DC):
                            ins = mm(bank[6][:, o * P:(o + 1) * P], wq_sb[:, c, o * P:(o + 1) * P],
                                     xn3T[:, b % 2, c, :], start=(c == 0), stop=(c == DC - 1))
                    ins.then_inc(q_done, 1)
                if 1 <= i <= NB:
                    b = i - 1
                    pe.wait_ge(xn3_ready, b + 1)
                    if b == 0:
                        pe.wait_ge(xT_lo_ready, E * DC)
                    else:
                        pe.wait_ge(xn3T_copied, b)
                    for c in range(DC):
                        ins = turn(bank[4][:, c * P:(c + 1) * P], xn3[:, b % 2, c * P:(c + 1) * P])
                    ins.then_inc(xn3_turned, 1)
                if TO_SCORE <= i < NB + TO_SCORE:
                    b = i - TO_SCORE
                    pe.wait_ge(attn_ready, b + 1)
                    if b >= 1:
                        pe.wait_ge(attnT_copied, b)
                    turn(bank[2][:, 0:P], attn[:, b % 2, :]).then_inc(attn_turned, 1)
                if 1 <= i <= NB - G:
                    attn_values(DC + (i - 1) // 2, (i - 1) % 2)
                if TO_NORM <= i:
                    b = i - TO_NORM
                    pe.wait_ge(xn4_ready, b + 1)
                    if b >= 1:
                        pe.wait_ge(h_ready, b)
                    for c in range(DC):
                        ins = turn(bank[5][:, c * P:(c + 1) * P], xn4[:, b % 2, c * P:(c + 1) * P])
                    ins.then_inc(xn4_turned, 1)
                if i == NB + TO_NORM - 2:
                    pe.wait_ge(attn_ready, NB)
                    pe.wait_ge(q_copied, NB * DC)
                    pe.wait_ge(vtok_copied, NB)
                    pe.wait_ge(vT_copied, NG * DC)
                    first(0, 0, 0)
            pe.wait_ge(attnT_copied, NB)
            pe.wait_ge(x3_ready, NB)

            def turn_zn(n, g):
                pe.wait_ge(zn_ready, (G - 1) * (n + 1))
                pe.wait_ge(zn_last_ready, n + 1)
                if not isinstance(n, int) or n:
                    pe.wait_ge(a_ready, DC * n)
                for c in range(DC):
                    for t in range(G):
                        ins = turn(bank[2 + c][:, t * P:(t + 1) * P], zn[:, (g % 2) * G + t, c * P:(c + 1) * P])
                    ins.then_inc(zn_turned, 1)

            def product(blk, n, g):
                pe.wait_ge(w2cur_ready, 2 * blk + 2)
                pe.wait_ge(h_ready, NB + DC * n)
                for c in range(DC):
                    pe.wait_ge(a_hi_ready, DC * n + (c + 1))
                    for o in range(DC):
                        for k, w in enumerate((w2c_lo, w2c_hi)):
                            mm(bank[4 + o][:, :], w[:, c, o * P:(o + 1) * P], a_hi[:, g % 2, c, :],
                               start=(c == 0 and k == 0), stop=False)
                    pe.wait_ge(a_lo_ready, DC * n + (c + 1))
                    for o in range(DC):
                        ins = mm(bank[4 + o][:, :], w2c_hi[:, c, o * P:(o + 1) * P], a_lo[:, g % 2, c, :],
                                 start=False, stop=(c == DC - 1))
                        if c == DC - 1:
                            ins.then_inc(y2_done, 1)

            def turn_h(g):
                for t in range(g * G, (g + 1) * G):
                    pe.wait_ge(h_ready, NB + DC * NG * (NBLK - 1) + DC * (g + 1))
                    if t < G:
                        pe.wait_ge(yb_ready, G * NG * NBLK + 4)
                    else:
                        pe.wait_ge(fin_ready, t - G + 1)
                    for c in range(DC):
                        ins = turn(bank[FIRST_BANK[t % G]][:, c * P:(c + 1) * P], hT[:, c, t * P:(t + 1) * P])
                    ins.then_inc(fin_turned, 1)

            def block_steps(blk, last):
                for g in range(NG):
                    n = NG * blk + g
                    if not last or g + 2 < NG:
                        first(blk + (g + 2) // NG, n + 2, (g + 2) % NG)
                    if last and 1 <= g < NG - 1:
                        turn_zn(n + 1, (g + 1) % NG)
                    product(blk, n, g)
                    if not last or g == 0:
                        turn_zn(n + 1, (g + 1) % NG)
                    if last and g >= 1:
                        turn_h(g - 1)
                if last:
                    turn_h(NG - 1)

            first(0, 1, 1)
            turn_zn(0, 0)
            with pe.Fori(0, NBLK - 1) as blk:
                block_steps(blk, False)
            block_steps(NBLK - 1, True)


_INS = ["x", "ctx_1024", "L0_xattn_igate_kernel", "L0_xattn_igate_bias", "L0_xattn_fgate_kernel",
        "L0_xattn_fgate_bias", "L0_ffn_gate_w", "L0_ffn_gate_b", "L0_ffn_w1", "L0_ffn_b1", "L0_ffn_w2",
        "L0_ffn_b2", "L1_xattn_Wq", "L1_xattn_bq", "L1_xattn_Wv", "L1_xattn_bv", "L1_ffn_qweights",
        "L1_ffn_scales", "L1_ffn_biases", "L1_ffn_lora_a", "L1_ffn_lora_b", "L1_ffn_ln_gamma",
        "L1_ffn_ln_beta"]


def kernel(**inputs):
    import numpy as np
    import concourse.bacc as bacc
    from concourse.bass_utils import run_bass_kernel_spmd

    nc = bacc.Bacc("TRN2", target_bir_lowering=False, num_devices=1)
    arrays, args = {}, []
    for name in _INS:
        a = np.ascontiguousarray(inputs[name])
        arrays[f"in_{name}"] = a
        args.append(nc.dram_tensor(f"in_{name}", a.shape, mybir.dt.from_np(a.dtype), kind="ExternalInput").ap())
    out = nc.dram_tensor("out_x", tuple(inputs["x"].shape), F32, kind="ExternalOutput").ap()
    mega_kernel(nc, *args, out)
    r = run_bass_kernel_spmd(nc, [arrays], core_ids=[0])
    return r.results[0]["out_x"]
```
